# Optimizing a Trainium2 kernel written in Bass

```python
import numpy as np
import jax
import jax.numpy as jnp

def _softmax(x, axis=-1):
    return jax.nn.softmax(x, axis=axis)

def _gelu(x):
    return jax.nn.gelu(x, approximate=True)

def _silu(x):
    return jax.nn.silu(x)

def _sigmoid(x):
    return jax.nn.sigmoid(x)

def _layernorm(x, axis=-1, eps=1e-05):
    m = jnp.mean(x, axis=axis, keepdims=True)
    v = jnp.var(x, axis=axis, keepdims=True)
    return (x - m) / jnp.sqrt(v + eps)

def _scatter_add(tgt, idx, src, axis=0):
    return tgt.at[idx].add(src)

def _segment_sum(src, seg, n):
    return jax.ops.segment_sum(src, seg, n)
kernel_name = 'mk_sandwich_d1_jaxref_r8_130b8c'

def setup_inputs(seed: int=0):
    np.random.seed(seed)
    _w = jnp.asarray

    def _L0_attn_setup():
        import jax, jax.numpy as jnp
        import numpy as np
        import math
        B, T, C, NH = (4, 256, 128, 16)
        HS = C // NH

        def rope_cache(dim, max_pos):
            half = dim // 2
            inv_freq = 1.0 / 10000.0 ** (jnp.arange(half, dtype=jnp.float32) * 2.0 / dim)
            ang = jnp.arange(max_pos, dtype=jnp.float32)[:, None] * inv_freq[None, :]
            return (jnp.cos(ang), jnp.sin(ang))

        def apply_rope(x, cos, sin):
            x0 = x[..., 0::2]
            x1 = x[..., 1::2]
            c = cos[None, None, :, :]
            s = sin[None, None, :, :]
            r0 = x0 * c - x1 * s
            r1 = x0 * s + x1 * c
            return jnp.stack([r0, r1], axis=-1).reshape(x.shape)
        key = jax.random.key(seed)
        ks = jax.random.split(key, 5)
        sc = 1.0 / math.sqrt(C)
        return {'x': jax.random.normal(ks[0], (B, T, C), jnp.float32), 'Wq': jax.random.normal(ks[1], (C, C), jnp.float32) * sc, 'bq': jnp.zeros((C,), jnp.float32), 'Wk': jax.random.normal(ks[2], (C, C), jnp.float32) * sc, 'bk': jnp.zeros((C,), jnp.float32), 'Wv': jax.random.normal(ks[3], (C, C), jnp.float32) * sc, 'bv': jnp.zeros((C,), jnp.float32), 'Wp': jax.random.normal(ks[4], (C, C), jnp.float32) * sc, 'bp': jnp.zeros((C,), jnp.float32)}
    _L0_attn_in = _L0_attn_setup()

    def _L0_ffn_setup():
        import jax, jax.numpy as jnp
        import numpy as np
        DIM = 128
        INTER = 176
        N_EXPERTS = 16
        TOPK = 2
        N_SHARED = 2
        SHARED_INTER = N_SHARED * INTER
        ROUTE_SCALE = 1.0
        key = jax.random.key(seed)
        ks = jax.random.split(key, 16)
        s = 0.02
        return {'x': jax.random.normal(ks[0], (2, 256, DIM), dtype=jnp.float32), 'gate_w': jax.random.normal(ks[1], (DIM, N_EXPERTS), dtype=jnp.float32) * s, 'gate_b': jnp.zeros((N_EXPERTS,), dtype=jnp.float32), 'w1': jax.random.normal(ks[2], (N_EXPERTS, DIM, INTER), dtype=jnp.float32) * s, 'b1': jnp.zeros((N_EXPERTS, INTER), dtype=jnp.float32), 'w3': jax.random.normal(ks[3], (N_EXPERTS, DIM, INTER), dtype=jnp.float32) * s, 'b3': jnp.zeros((N_EXPERTS, INTER), dtype=jnp.float32), 'w2': jax.random.normal(ks[4], (N_EXPERTS, INTER, DIM), dtype=jnp.float32) * s, 'b2': jnp.zeros((N_EXPERTS, DIM), dtype=jnp.float32), 'sw1': jax.random.normal(ks[5], (DIM, SHARED_INTER), dtype=jnp.float32) * s, 'sb1': jax.random.normal(ks[6], (SHARED_INTER,), dtype=jnp.float32) * s, 'sw3': jax.random.normal(ks[7], (DIM, SHARED_INTER), dtype=jnp.float32) * s, 'sb3': jax.random.normal(ks[8], (SHARED_INTER,), dtype=jnp.float32) * s, 'sw2': jax.random.normal(ks[9], (SHARED_INTER, DIM), dtype=jnp.float32) * s, 'sb2': jax.random.normal(ks[10], (DIM,), dtype=jnp.float32) * s}
    _L0_ffn_in = _L0_ffn_setup()
    _d = {'L0_attn_x': _L0_attn_in['x'], 'L0_attn_Wq': _L0_attn_in['Wq'], 'L0_attn_bq': _L0_attn_in['bq'], 'L0_attn_Wk': _L0_attn_in['Wk'], 'L0_attn_bk': _L0_attn_in['bk'], 'L0_attn_Wv': _L0_attn_in['Wv'], 'L0_attn_bv': _L0_attn_in['bv'], 'L0_attn_Wp': _L0_attn_in['Wp'], 'L0_attn_bp': _L0_attn_in['bp'], 'L0_ffn_gate_w': _L0_ffn_in['gate_w'], 'L0_ffn_gate_b': _L0_ffn_in['gate_b'], 'L0_ffn_w1': _L0_ffn_in['w1'], 'L0_ffn_b1': _L0_ffn_in['b1'], 'L0_ffn_w3': _L0_ffn_in['w3'], 'L0_ffn_b3': _L0_ffn_in['b3'], 'L0_ffn_w2': _L0_ffn_in['w2'], 'L0_ffn_b2': _L0_ffn_in['b2'], 'L0_ffn_sw1': _L0_ffn_in['sw1'], 'L0_ffn_sb1': _L0_ffn_in['sb1'], 'L0_ffn_sw3': _L0_ffn_in['sw3'], 'L0_ffn_sb3': _L0_ffn_in['sb3'], 'L0_ffn_sw2': _L0_ffn_in['sw2'], 'L0_ffn_sb2': _L0_ffn_in['sb2']}
    _x0 = _d['L0_attn_x']
    _d['L0_attn_x'] = jax.random.normal(jax.random.fold_in(jax.random.key(seed), 1), (16, 512, 128), dtype=_x0.dtype)
    del _x0
    return _d

def reference(L0_attn_x, L0_attn_Wq, L0_attn_bq, L0_attn_Wk, L0_attn_bk, L0_attn_Wv, L0_attn_bv, L0_attn_Wp, L0_attn_bp, L0_ffn_gate_w, L0_ffn_gate_b, L0_ffn_w1, L0_ffn_b1, L0_ffn_w3, L0_ffn_b3, L0_ffn_w2, L0_ffn_b2, L0_ffn_sw1, L0_ffn_sb1, L0_ffn_sw3, L0_ffn_sb3, L0_ffn_sw2, L0_ffn_sb2):

    def _L0_attn_ref(x, Wq, bq, Wk, bk, Wv, bv, Wp, bp):
        import jax, jax.numpy as jnp
        import numpy as np
        import math
        B, T, C, NH = (4, 256, 128, 16)
        HS = C // NH

        def rope_cache(dim, max_pos):
            half = dim // 2
            inv_freq = 1.0 / 10000.0 ** (jnp.arange(half, dtype=jnp.float32) * 2.0 / dim)
            ang = jnp.arange(max_pos, dtype=jnp.float32)[:, None] * inv_freq[None, :]
            return (jnp.cos(ang), jnp.sin(ang))

        def apply_rope(x, cos, sin):
            x0 = x[..., 0::2]
            x1 = x[..., 1::2]
            c = cos[None, None, :, :]
            s = sin[None, None, :, :]
            r0 = x0 * c - x1 * s
            r1 = x0 * s + x1 * c
            return jnp.stack([r0, r1], axis=-1).reshape(x.shape)
        Bx, Tx, Cx = x.shape

        def split_heads(y):
            return y.reshape(Bx, Tx, NH, HS).transpose(0, 2, 1, 3)
        q = split_heads(x @ Wq + bq)
        k = split_heads(x @ Wk + bk)
        v = split_heads(x @ Wv + bv)
        cos, sin = rope_cache(HS, Tx)
        q = apply_rope(q, cos, sin)
        k = apply_rope(k, cos, sin)
        att = jnp.einsum('bhqd,bhkd->bhqk', q, k) * (1.0 / math.sqrt(HS))
        causal = jnp.tril(jnp.ones((Tx, Tx), bool))
        att = jnp.where(causal[None, None, :, :], att, jnp.float32(-10000000000.0))
        att = jax.nn.softmax(att, axis=-1)
        y = jnp.einsum('bhqk,bhkd->bhqd', att, v)
        y = y.transpose(0, 2, 1, 3).reshape(Bx, Tx, Cx)
        return y @ Wp + bp

    def _L0_ffn_ref(x, gate_w, gate_b, w1, b1, w3, b3, w2, b2, sw1, sb1, sw3, sb3, sw2, sb2):
        import jax, jax.numpy as jnp
        import numpy as np
        DIM = 128
        INTER = 176
        N_EXPERTS = 16
        TOPK = 2
        N_SHARED = 2
        SHARED_INTER = N_SHARED * INTER
        ROUTE_SCALE = 1.0
        shape = x.shape
        xf = x.reshape(-1, DIM)
        logits = xf @ gate_w + gate_b
        scores = jax.nn.softmax(logits.astype(jnp.float32), axis=-1)
        top_vals, top_idx = jax.lax.top_k(scores, TOPK)
        weights = (top_vals * ROUTE_SCALE).astype(x.dtype)
        cw = (jax.nn.one_hot(top_idx, N_EXPERTS, dtype=x.dtype) * weights[..., None]).sum(axis=1)
        h = jnp.einsum('td,edh->teh', xf, w1) + b1
        g = jnp.einsum('td,edh->teh', xf, w3) + b3
        a = jax.nn.silu(h) * g
        y = jnp.einsum('teh,ehd,te->td', a, w2, cw) + cw @ b2
        z = jax.nn.silu(xf @ sw1 + sb1) * (xf @ sw3 + sb3) @ sw2 + sb2
        return (y + z).reshape(shape)
    x = L0_attn_x
    x = x + _layernorm(_L0_attn_ref(_layernorm(x, axis=-1), L0_attn_Wq, L0_attn_bq, L0_attn_Wk, L0_attn_bk, L0_attn_Wv, L0_attn_bv, L0_attn_Wp, L0_attn_bp), axis=-1)
    x = x + _layernorm(_L0_ffn_ref(_layernorm(x, axis=-1), L0_ffn_gate_w, L0_ffn_gate_b, L0_ffn_w1, L0_ffn_b1, L0_ffn_w3, L0_ffn_b3, L0_ffn_w2, L0_ffn_b2, L0_ffn_sw1, L0_ffn_sb1, L0_ffn_sw3, L0_ffn_sb3, L0_ffn_sw2, L0_ffn_sb2), axis=-1)
    return x

_drawn_inputs = setup_inputs


def setup_inputs(seed=0):
    import zlib

    import numpy as np

    out = dict(_drawn_inputs(seed))
    spreads = {'L0_attn_bq': (0.0, 0.1),
     'L0_attn_bk': (0.0, 0.1),
     'L0_attn_bv': (0.0, 0.1),
     'L0_attn_bp': (0.0, 0.1),
     'L0_ffn_gate_b': (0.0, 0.1),
     'L0_ffn_b1': (0.0, 0.8),
     'L0_ffn_b3': (0.0, 0.8),
     'L0_ffn_b2': (0.0, 0.1)}
    factors = {'L0_ffn_w1': 2.796, 'L0_ffn_w3': 2.785, 'L0_ffn_sb1': 3.108, 'L0_ffn_sb3': 3.002}
    for name, (base, spread) in spreads.items():
        noise = np.random.default_rng([zlib.crc32(name.encode()), seed]).standard_normal(out[name].shape)
        drawn = base * np.exp(spread * noise) if base else spread * noise
        out[name] = jnp.asarray(drawn.astype(out[name].dtype))
    for name, factor in factors.items():
        out[name] = (out[name] * factor).astype(out[name].dtype)
    return out
```

```python
from contextlib import ExitStack

import numpy as np
import concourse.bass as bass
from concourse import mybir

F32 = mybir.dt.float32
BF16 = mybir.dt.bfloat16
U32 = mybir.dt.uint32
ALU = mybir.AluOpType
ACT = mybir.ActivationFunctionType
AX = mybir.AxisListType

P = 128
NT = 4
NH, HS = 16, 8
HG = 4
NG = NH // HG
NPART = 3
ROWS = NPART * NPART * HS
SROWS = ROWS + NPART
NEG = -1e30
EPS = 1e-5


def free_ap(ap, dims, offset=0):
    return bass.AP(ap.tensor, ap.offset + offset, [list(ap.ap[0])] + [list(d) for d in dims])


class Steps:

    def __init__(self, sem, per):
        self.sem, self.per, self.k, self.base = sem, per, 0, 0

    def round(self, n):
        self.base, self.k = n * self.per, 0

    def did(self, instruction):
        self.k += 1
        instruction.then_inc(self.sem, 1)

    def value(self):
        return self.base + self.k

    def closed(self):
        assert self.k == self.per, (self.k, self.per)


def wait(eng, sem, value):
    if isinstance(value, int) and value <= 0:
        return
    eng.wait_ge(sem, value)


P1_UNITS = [(3, (0, 1)), (3, (2, 3)), (2, (0, 1)), (2, (2, 3)), (1, (0, 1, 2, 3)), (0, (0, 1, 2, 3))]
P2_UNITS = ([(0, (h,)) for h in range(HG)] + [(1, (h,)) for h in range(HG)]
            + [(2, (0, 1)), (2, (2, 3))] + [(3, (0, 1, 2, 3))])
END_UNITS = ["y_transposed", "projected", "x_transposed", "qkv_0", "qkv_1", "qk_transposed"]
P1_N = len(P1_UNITS) * NG
P2_N = len(P2_UNITS)
LN_STEPS = 2 * NT
Z_STEPS = 1 + LN_STEPS + NT - 1


def program(nc, x, Wq, bq, Wk, bk, Wv, bv, Wp, bp, gate_w, gate_b, w1, b1, w3, b3, w2, b2,
            sw1, sb1, sw3, sb3, sw2, sb2, cos, sin, out):
    B, T, C = x.shape
    E, _, INTER = w1.shape
    HALF = INTER // 2
    NE = E + sw1.shape[1] // INTER
    NTILES = B * NT
    assert T == NT * P and C == P and B % 2 == 0
    SCALE = 1.0 / float(np.sqrt(HS))
    ctx = ExitStack()
    with ctx:
        def sb(name, shape, dt=F32):
            return ctx.enter_context(nc.sbuf_tensor(name, shape, dt))

        def sem(name):
            return ctx.enter_context(nc.semaphore(name))

        x1 = nc.dram_tensor("x1_scratch", [B, T, C], F32, kind="Internal").ap()

        wide = [ctx.enter_context(nc.psum_tensor(f"wide{n}", [P, 2, 512], F32)) for n in range(2)]
        score = [ctx.enter_context(nc.psum_tensor(f"score{n}", [P, 512], F32)) for n in range(2)]
        heads_ps = ctx.enter_context(nc.psum_tensor("heads_ps", [P, 512], F32))
        misc = ctx.enter_context(nc.psum_tensor("misc", [P, 512], F32))

        ident = sb("ident", [P, P])
        identb = sb("identb", [P, P], BF16)
        maskneg = sb("maskneg", [P, P], BF16)
        cos_sb = sb("cos_sb", [P, NT, HS])
        sin_sb = sb("sin_sb", [P, NT, HS])
        wqkv = sb("wqkv", [P, 3 * P])
        wp = sb("wp", [P, P])
        bqkv_bc = sb("bqkv_bc", [P, 3 * P])
        bp_bc = sb("bp_bc", [P, P])
        xt = sb("xt", [P, NT, P])
        xr = sb("xr", [P, NT, P])
        st = sb("st", [P, NT, 6])
        mv = sb("mv", [P, NT, 2])
        rstd = sb("rstd", [P, NT])
        vareps = sb("vareps", [P, NT])
        mhalf = sb("mhalf", [P, NT])
        st2 = sb("st2", [P, NT, 6])
        mv2 = sb("mv2", [P, NT, 2])
        rstd2 = sb("rstd2", [P, NT])
        xn = sb("xn", [P, NT, P])
        xnT = sb("xnT", [P, NT * P])
        qk = sb("qk", [P, NT, 2 * P])
        ra = sb("ra", [P, NT, 2 * P])
        rb = sb("rb", [P, NT, 2 * P])
        rot = sb("rot", [P, NT, 2, P])
        rest = sb("rest", [P, 2, T])
        parts = sb("parts", [P, 2, NPART, T], BF16)
        qk4 = sb("qk4", [P, 4, NH, T], BF16)
        q4 = [qk4[0:96, n, :, :] for n in range(2)]
        k4 = [qk4[0:96, 2 + n, :, :] for n in range(2)]
        vext = [sb(f"vext{n}", [P, NT, NH, 32]) for n in range(2)]
        mx = sb("mx", [P, NH, NT])
        mrest = sb("mrest", [64, P])
        mparts = sb("mparts", [64, NPART, P], BF16)
        prob = [sb(f"prob{k}", [P, HG, T - k * P]) for k in range(NT)]
        oT = sb("oT", [P, T])
        rinv = sb("rinv", [P, NT, HG])
        y = sb("y", [P, NT, P])
        yT = sb("yT", [P, T])
        z = sb("z", [P, NT, P])

        weights_in = sem("weights_in")
        waits_passed = sem("waits_passed")
        ident0 = sem("ident0")
        ident_ready = sem("ident_ready")
        filled = sem("filled")
        x_in = sem("x_in")
        xn_step = sem("xn_step")
        xn_ready = sem("xn_ready")
        x_vareps = sem("x_vareps")
        x_rstd = sem("x_rstd")
        z_vareps = sem("z_vareps")
        z_rstd = sem("z_rstd")
        f_var = sem("f_var")
        f_vareps = sem("f_vareps")
        f_rstd = sem("f_rstd")
        x_transposed = sem("x_transposed")
        xnT_ready = sem("xnT_ready")
        qkv_done = sem("qkv_done")
        v_ready = sem("v_ready")
        qk_biased = sem("qk_biased")
        rope_cos = sem("rope_cos")
        rope_sin = sem("rope_sin")
        rotated = sem("rotated")
        qk_transposed = sem("qk_transposed")
        part1_ready = sem("part1_ready")
        rest_ready = sem("rest_ready")
        part2_ready = sem("part2_ready")
        part3_ready = sem("part3_ready")
        shuffled = sem("shuffled")
        p1_scores = sem("p1_scores")
        p1_max = sem("p1_max")
        max_transposed = sem("max_transposed")
        m_step = sem("m_step")
        m_ready = sem("m_ready")
        m_in = sem("m_in")
        p2_scores = sem("p2_scores")
        exp_done = sem("exp_done")
        masked = sem("masked")
        pv_done = sem("pv_done")
        heads_copied = sem("heads_copied")
        heads_transposed = sem("heads_transposed")
        rinv_ready = sem("rinv_ready")
        y_ready = sem("y_ready")
        y_transposed = sem("y_transposed")
        yT_ready = sem("yT_ready")
        projected = sem("projected")
        xr_in = sem("xr_in")
        z_step = sem("z_step")
        z_ready = sem("z_ready")
        x1_ready = sem("x1_ready")
        x1_out = sem("x1_out")

        N_SHUFFLE = 2 * NPART * NPART * 16
        N_W = 10 * 16
        x_v = x.rearrange("b (t p) c -> b p t c", p=P)
        x1_v = x1.rearrange("b (t p) c -> b p t c", p=P)
        out_v = out.rearrange("b (t p) c -> b p t c", p=P)
        row = lambda a: a.rearrange("(o n) -> o n", o=1)

        def iterations(eng, body):
            body(-2, True, False, False)
            body(-1, True, True, False)
            body(0, True, True, True)
            body(1, True, True, True)
            with eng.Fori(1, B // 2 - 1) as pair:
                body(2 * pair, True, True, True, 0)
                body(2 * pair + 1, True, True, True, 1)
            body(B - 2, False, True, True)
            body(B - 1, False, False, True)

        def apart(eng):
            eng.sem_inc(waits_passed, 1)

        def par(i, parity):
            return i % 2 if parity is None else parity

        block = ctx.enter_context(nc.Block())

        w13_sb = sb("w13_sb", [P, NE, 2 * INTER])
        w2_sb = sb("w2_sb", [HALF, NE, 2, P])
        b13_bc = free_ap(qk4[:].rearrange("p a h t -> p (a h t)").bitcast(F32), [[2 * INTER, NE], [1, 2 * INTER]])
        gw_sb = sb("gw_sb", [P, E])
        gb_bc = sb("gb_bc", [P, E])
        b2_sb = sb("b2_sb", [E, P])
        sb2_bc = sb("sb2_bc", [P, P])
        iota_e = sb("iota_e", [P, E])
        f_x = sb("f_x", [P, P])
        f_st = sb("f_st", [P, 6])
        f_mv = sb("f_mv", [P, 2])
        f_rs = sb("f_rs", [P, 1])
        f_xn = sb("f_xn", [P, P])
        f_xT = sb("f_xT", [P, P])
        lg = sb("lg", [P, E])
        nmx = sb("nmx", [P, 1])
        ex = sb("ex", [P, E])
        sume = sb("sume", [P, 1])
        rsum = sb("rsum", [P, 1])
        sc = sb("sc", [P, E])
        top = sb("top", [P, 8])
        topi = sb("topi", [P, 8], U32)
        topf = sb("topf", [P, 8])
        oh1 = sb("oh1", [P, E])
        cw = sb("cw", [P, E])
        cwT = sb("cwT", [E, P])
        cwh = sb("cwh", [P, NE])
        hb = [sb(f"hb{n}", [P, 2 * INTER]) for n in range(2)]
        th = [sb(f"th{n}", [P, INTER]) for n in range(2)]
        hs = [sb(f"hs{n}", [P, INTER]) for n in range(2)]
        aa = [sb(f"aa{n}", [P, INTER]) for n in range(2)]
        aT = [sb(f"aT{n}", [HALF, 2, P]) for n in range(2)]
        fz = sb("fz", [P, P])
        fo = [sb(f"fo{n}", [P, P]) for n in range(2)]
        f_fw = sem("f_fw")
        f_in = sem("f_in")
        f_step = sem("f_step")
        f_xn_ready = sem("f_xn_ready")
        f_tr = sem("f_tr")
        f_xT_ready = sem("f_xT_ready")
        f_logits = sem("f_logits")
        f_nmx = sem("f_nmx")
        f_exp = sem("f_exp")
        f_cw = sem("f_cw")
        f_cwtr = sem("f_cwtr")
        f_cwT = sem("f_cwT")
        f_hg = sem("f_hg")
        f_hb = sem("f_hb")
        f_th = sem("f_th")
        f_hs = sem("f_hs")
        f_a = sem("f_a")
        f_atr = sem("f_atr")
        f_aT = sem("f_aT")
        f_y = sem("f_y")
        f_z = sem("f_z")
        f_o = sem("f_o")
        f_out = sem("f_out")
        N_FW = 16 * 16

        @block.sync
        def _(sp):
            for w, s in ((wqkv[:, 0:P], Wq), (wqkv[:, P:2 * P], Wk), (wqkv[:, 2 * P:], Wv), (wp[:], Wp)):
                sp.dma_start(w, s).then_inc(weights_in, 16)
            for n, v in enumerate((bq, bk, bv)):
                sp.dma_start(bqkv_bc[:, n * P:(n + 1) * P], row(v).to_broadcast([P, P])).then_inc(weights_in, 16)
            sp.dma_start(bp_bc[:], row(bp).to_broadcast([P, P])).then_inc(weights_in, 16)
            sp.dma_start(cos_sb[:], cos).then_inc(weights_in, 16)
            sp.dma_start(sin_sb[:], sin).then_inc(weights_in, 16)

            def body(i, a1, p1, p2, parity=None):
                e = par(i, parity)
                if p2:
                    wait(sp, x1_ready, i)
                    apart(sp)
                    sp.dma_start(xr[:], x_v[i]).then_inc(xr_in, 16)
                if a1:
                    wait(sp, xn_ready, i + 2)
                    apart(sp)
                    sp.dma_start(xt[:], x_v[i + 2]).then_inc(x_in, 16)
                if p1:
                    sp.wait_ge(m_ready, i + 2)
                    for r in range(NPART):
                        sp.dma_start(q4[1 - e][ROWS + r:ROWS + r + 1, :, :], mparts[:, r, :]).then_inc(m_in, 16)
                if a1:
                    wait(sp, p2_scores, (i + 1) * P2_N * NG)
                    apart(sp)
                    if isinstance(i, int) and i < 0:
                        sp.wait_ge(filled, 4)
                    sp.wait_ge(part1_ready, i + 3)
                    apart(sp)
                    sp.wait_ge(part3_ready, i + 3)
                    for a in range(NPART):
                        for b in range(NPART):
                            r = (a * NPART + b) * HS
                            sp.dma_start(q4[e][r:r + HS, :, :], parts[:, 0, a, :]).then_inc(shuffled, 16)
                            sp.dma_start(k4[e][r:r + HS, :, :], parts[:, 1, b, :]).then_inc(shuffled, 16)
                if p2:
                    sp.wait_ge(x1_ready, i + 1)
                    apart(sp)
                    sp.dma_start(x1_v[i], z[:]).then_inc(x1_out, 16)

            iterations(sp, body)

            sp.wait_ge(x1_out, B * 16)
            x1_t = x1.rearrange("b (t p) c -> (b t) p c", p=P)
            out_t = out.rearrange("b (t p) c -> (b t) p c", p=P)

            def tile(t, e):
                wait(sp, f_o, t)
                apart(sp)
                sp.dma_start(f_x[:], x1_t[t]).then_inc(f_in, 16)
                sp.wait_ge(f_o, t + 1)
                apart(sp)
                sp.dma_start(out_t[t], fo[e][:]).then_inc(f_out, 16)

            tile(0, 0)
            tile(1, 1)
            with sp.Fori(1, NTILES // 2) as pair:
                tile(2 * pair, 0)
                tile(2 * pair + 1, 1)
            sp.wait_ge(f_out, NTILES * 16)

        @block.gpsimd
        def _(pool):
            for m, s in ((ident, 0.0), (identb, 0.0), (maskneg, 0.0)):
                nc.gpsimd.memset(m[:], s).then_inc(ident0, 1)
            nc.gpsimd.memset(mhalf[:], -0.5).then_inc(ident0, 1)
            pool.wait_ge(ident0, 4)
            nc.gpsimd.affine_select(out=ident[:], in_=ident[:], compare_op=ALU.not_equal, fill=1.0, base=0,
                                    pattern=[[-1, P]], channel_multiplier=1).then_inc(ident_ready, 1)
            nc.gpsimd.affine_select(out=identb[:], in_=identb[:], compare_op=ALU.not_equal, fill=1.0, base=0,
                                    pattern=[[-1, P]], channel_multiplier=1).then_inc(ident_ready, 1)
            nc.gpsimd.affine_select(out=maskneg[:], in_=maskneg[:], compare_op=ALU.is_ge, fill=NEG, base=0,
                                    pattern=[[-1, P]], channel_multiplier=1).then_inc(ident_ready, 1)
            nc.gpsimd.iota(iota_e[:], pattern=[[1, E]], base=0, channel_multiplier=0,
                           allow_small_or_imprecise_dtypes=True).then_inc(ident_ready, 1)

            def inverse_deviation(out_, var, added, before, done):
                apart(pool)
                nc.gpsimd.tensor_scalar(vareps[:, 0:out_.shape[1]], var, EPS, None, ALU.add).then_inc(added, 1)
                pool.wait_ge(added, before + 1)
                nc.gpsimd.tensor_tensor(out_, vareps[:, 0:out_.shape[1]], mhalf[:, 0:out_.shape[1]],
                                        ALU.pow).then_inc(done, 1)

            def body(i, a1, p1, p2, parity=None):
                if p2:
                    for g in range(NG):
                        for kb in range(NT):
                            n = P2_N * g + (4, 8, 10, 11)[kb]
                            pool.wait_ge(exp_done, i * P2_N * NG + n)
                            apart(pool)
                            nc.gpsimd.affine_select(
                                out=prob[kb][:, :, 0:P], in_=prob[kb][:, :, 0:P], compare_op=ALU.is_ge, fill=0.0,
                                base=0, pattern=[[0, HG], [1, P]], channel_multiplier=-1).then_inc(masked, 1)
                if a1:
                    pool.wait_ge(xn_step, (i + 3) * LN_STEPS)
                    inverse_deviation(rstd[:], mv[:].rearrange("p t s -> p (t s)")[:, 1:2 * NT:2], x_vareps, i + 2, x_rstd)
                if p2:
                    if a1:
                        pool.wait_ge(x_rstd, i + 3)
                    else:
                        wait(pool, z_rstd, i)
                    pool.wait_ge(z_step, i * Z_STEPS + 1 + LN_STEPS)
                    inverse_deviation(rstd2[:], mv2[:].rearrange("p t s -> p (t s)")[:, 1:2 * NT:2], z_vareps, i, z_rstd)
                if a1:
                    for t in range(NT):
                        if t % 2 == 0:
                            pool.wait_ge(qk_biased, 2 * (i + 2) + t // 2 + 1)
                            if t == 0:
                                wait(pool, rotated, i + 2)
                        nc.gpsimd.tensor_tensor(
                            free_ap(rb[:, t, :], [[HS, 2 * NH], [2, HS // 2], [1, 2]]),
                            free_ap(qk[:, t, :], [[HS, 2 * NH], [2, HS // 2], [-1, 2]], 1),
                            free_ap(sin_sb[:, t, :], [[0, 2 * NH], [2, HS // 2], [1, 2]]),
                            ALU.mult).then_inc(rope_sin, 1)
                    pool.wait_ge(rest_ready, i + 3)
                    if not (isinstance(i, int) and i < -1):
                        pool.wait_ge(shuffled, (i + 2) * N_SHUFFLE)
                    apart(pool)
                    nc.gpsimd.tensor_copy(parts[:, :, 1, :], rest[:]).then_inc(part2_ready, 1)
                    pool.wait_ge(part2_ready, i + 3)
                    nc.gpsimd.tensor_tensor(parts[:, :, 2, :], rest[:], parts[:, :, 1, :],
                                            ALU.subtract).then_inc(part3_ready, 1)

            pool.wait_ge(weights_in, N_W)
            iterations(pool, body)

            def tile(t, e):
                for k in range(2):
                    pool.wait_ge(f_var, 2 * t + k + 1)
                    inverse_deviation(f_rs[:], f_mv[:, 1:2], f_vareps, 2 * t + k, f_rstd)

            pool.wait_ge(z_rstd, B)
            tile(0, 0)
            tile(1, 1)
            with pool.Fori(1, NTILES // 2) as pair:
                tile(2 * pair, 0)
                tile(2 * pair + 1, 1)

        @block.scalar
        def _(act):
            act.dma_start(w13_sb[:, 0:E, 0:INTER], w1.rearrange("e d h -> d e h")).then_inc(f_fw, 16)
            act.dma_start(w13_sb[:, 0:E, INTER:], w3.rearrange("e d h -> d e h")).then_inc(f_fw, 16)
            act.dma_start(w13_sb[:, E:, 0:INTER], sw1.rearrange("d (s h) -> d s h", h=INTER)).then_inc(f_fw, 16)
            act.dma_start(w13_sb[:, E:, INTER:], sw3.rearrange("d (s h) -> d s h", h=INTER)).then_inc(f_fw, 16)
            for k in range(2):
                act.dma_start(w2_sb[:, 0:E, k, :], w2[:, k * HALF:(k + 1) * HALF, :].rearrange("e h d -> h e d")).then_inc(f_fw, 16)
            for s in range(NE - E):
                act.dma_start(w2_sb[:, E + s, :, :], sw2[s * INTER:(s + 1) * INTER, :].rearrange("(k h) d -> h k d", k=2)).then_inc(f_fw, 16)
            act.dma_start(gw_sb[:], gate_w).then_inc(f_fw, 16)
            act.dma_start(gb_bc[:], row(gate_b).to_broadcast([P, E])).then_inc(f_fw, 16)
            act.dma_start(b2_sb[:], b2).then_inc(f_fw, 16)
            act.dma_start(sb2_bc[:], row(sb2).to_broadcast([P, P])).then_inc(f_fw, 16)

            def body(i, a1, p1, p2, parity=None):
                if p2:
                    for g in range(NG):
                        for u, (kb, hs_) in enumerate(P2_UNITS):
                            n = g * P2_N + u
                            N = T - kb * P
                            act.wait_ge(p2_scores, i * P2_N * NG + n + 1)
                            wait(act, pv_done, i * NG * NT + (g - 1) * NT + kb + 1)
                            nc.scalar.activation(free_ap(prob[kb][:, hs_[0], :], [[1, N * len(hs_)]]),
                                                 score[n % 2][:, 0:N * len(hs_)],
                                                 ACT.Exp, scale=SCALE).then_inc(exp_done, 1)
                        act.wait_ge(pv_done, (i * NG + g + 1) * NT)
                        wait(act, heads_transposed, i * NG + g)
                        nc.scalar.activation(oT[:], heads_ps[:], ACT.Copy).then_inc(heads_copied, 1)
                    act.wait_ge(y_transposed, i + 1)
                    nc.scalar.activation(yT[:], wide[0][:, 0, :], ACT.Copy).then_inc(yT_ready, 1)
                if a1:
                    act.wait_ge(x_transposed, i + 3)
                    nc.scalar.activation(xnT[:], wide[0][:, 0, :], ACT.Copy).then_inc(xnT_ready, 1)
                    act.wait_ge(qk_transposed, i + 3)
                    if not (isinstance(i, int) and i < -1):
                        act.wait_ge(shuffled, (i + 2) * N_SHUFFLE)
                    nc.scalar.activation(parts[:, :, 0, :], wide[1][:], ACT.Copy).then_inc(part1_ready, 1)

            iterations(act, body)
            act.wait_ge(p2_scores, B * P2_N * NG)
            for a, bb, lo in ((b1, sb1, 0), (b3, sb3, INTER)):
                act.dma_start(b13_bc[:, 0:E, lo:lo + INTER], bass.AP(a.tensor, a.offset, [[0, P], [INTER, E], [1, INTER]])).then_inc(f_fw, 16)
                act.dma_start(b13_bc[:, E:, lo:lo + INTER], bass.AP(bb.tensor, bb.offset, [[0, P], [INTER, NE - E], [1, INTER]])).then_inc(f_fw, 16)

            def tile(t, e):
                act.wait_ge(f_tr, t + 1)
                nc.scalar.activation(f_xT[:], misc[:, 0:P], ACT.Copy).then_inc(f_xT_ready, 1)
                act.wait_ge(f_nmx, t + 1)
                nc.scalar.activation(ex[:], lg[:], ACT.Exp, bias=nmx[:, 0:1], accum_out=sume[:, 0:1]).then_inc(f_exp, 1)
                act.wait_ge(f_cwtr, t + 1)
                nc.scalar.activation(cwT[:], misc[0:E, 256:256 + P], ACT.Copy).then_inc(f_cwT, 1)

                def down(ei):
                    act.wait_ge(f_atr, t * NE + ei + 1)
                    nc.scalar.activation(aT[ei % 2][:], score[ei % 2][0:HALF, 0:2 * P].rearrange("p (a b) -> p a b", a=2), ACT.Copy).then_inc(f_aT, 1)

                for ei in range(NE):
                    act.wait_ge(f_hb, t * NE + ei + 1)
                    nc.scalar.activation(th[ei % 2][:], hb[ei % 2][:, 0:INTER], ACT.Tanh, scale=0.5).then_inc(f_th, 1)
                    if ei >= 1:
                        down(ei - 1)
                down(NE - 1)

            tile(0, 0)
            tile(1, 1)
            with act.Fori(1, NTILES // 2) as pair:
                tile(2 * pair, 0)
                tile(2 * pair + 1, 1)

        @block.vector
        def _(dve):
            for n in range(2):
                nc.vector.memset(k4[n][64:96, :, :], 1.0).then_inc(filled, 1)
                nc.vector.memset(vext[n][:], 0.0).then_inc(filled, 1)
            dve.wait_ge(filled, 4)
            for n in range(2):
                nc.vector.memset(vext[n][:, :, :, HS:HS + 1], 1.0).then_inc(filled, 1)
            dve.wait_ge(filled, 6)
            dve.wait_ge(weights_in, N_W)
            ln1 = Steps(xn_step, LN_STEPS)
            ms = Steps(m_step, 3)
            zs = Steps(z_step, Z_STEPS)

            def maxima(i, g, n, e):
                j, hs_ = P1_UNITS[n]
                u = g * len(P1_UNITS) + n
                dve.wait_ge(p1_scores, (i + 1) * P1_N + u + 1)
                if u == 0:
                    wait(dve, max_transposed, i + 1)
                L = (j + 1) * P
                src = wide[u % 2][:, :, 0:L] if j >= 2 else free_ap(wide[u % 2][:, 0, :], [[L, HG], [1, L]])
                h0 = g * HG + hs_[0]
                nc.vector.tensor_reduce(mx[:, h0:h0 + len(hs_), j:j + 1], src, axis=AX.X,
                                        op=ALU.max).then_inc(p1_max, 1)

            def normalised_heads(i, g):
                dve.wait_ge(heads_transposed, i * NG + g + 1)
                hv = misc[:].rearrange("p (t h d) -> p t h d", t=NT, h=HG)
                if g == 0:
                    wait(dve, y_transposed, i)
                nc.vector.reciprocal(rinv[:].rearrange("p t (h o) -> p t h o", o=1), hv[:, :, :, HS:HS + 1]).then_inc(rinv_ready, 1)
                dve.wait_ge(rinv_ready, i * NG + g + 1)
                nc.vector.tensor_tensor(free_ap(y[:, 0, :], [[P, NT], [HS, HG], [1, HS]], g * HG * HS),
                                        hv[:, :, :, 0:HS],
                                        free_ap(rinv[:, 0, :], [[HG, NT], [1, HG], [0, HS]]),
                                        ALU.mult).then_inc(y_ready, 1)

            def layer_norm(steps, src, st_, mv_, rstd_, dst, rstd_ready, last):
                for t in range(NT):
                    steps.did(nc.vector.bn_stats(st_[:, t, :], src[:, t, :]))
                dve.wait_ge(steps.sem, steps.value())
                apart(dve)
                for t in range(NT):
                    steps.did(nc.vector.bn_aggr(mv_[:, t, :], st_[:, t, :]))
                dve.wait_ge(*rstd_ready)
                for t in range(NT):
                    ins = nc.vector.tensor_scalar(dst[:, t, :], src[:, t, :], mv_[:, t, 0:1], rstd_[:, t:t + 1],
                                                  ALU.subtract, ALU.mult)
                    last(t, ins)

            def body(i, a1, p1, p2, parity=None):
                e = par(i, parity)
                for g in range(NG):
                    if p1:
                        for n in range(3):
                            maxima(i, g, n, e)
                    if p2 and g >= 1:
                        normalised_heads(i, g - 1)
                    if p1:
                        for n in range(3, 6):
                            maxima(i, g, n, e)
                if p2:
                    normalised_heads(i, NG - 1)
                if a1:
                    ln1.round(i + 2)
                    dve.wait_ge(x_in, 16 * (i + 3))
                    wait(dve, x_transposed, i + 2)
                    layer_norm(ln1, xt, st, mv, rstd, xn, (x_rstd, i + 3),
                               lambda t, ins: ins.then_inc(xn_ready, 1) if t == NT - 1 else None)
                    ln1.closed()
                if p1:
                    ms.round(i + 1)
                    dve.wait_ge(max_transposed, i + 2)
                    wait(dve, m_in, 16 * NPART * (i + 1))
                    mt = misc[0:64, 0:P]
                    ms.did(nc.vector.tensor_scalar(mparts[:, 0, :], mt, -1.0, None, ALU.mult))
                    dve.wait_ge(m_step, ms.value())
                    ms.did(nc.vector.scalar_tensor_tensor(out=mrest[:], in0=mt, scalar=-1.0, in1=mparts[:, 0, :],
                                                          op0=ALU.mult, op1=ALU.subtract))
                    dve.wait_ge(m_step, ms.value())
                    ms.did(nc.vector.tensor_copy(mparts[:, 1, :], mrest[:]))
                    dve.wait_ge(m_step, ms.value())
                    nc.vector.tensor_tensor(mparts[:, 2, :], mrest[:], mparts[:, 1, :], ALU.subtract).then_inc(m_ready, 1)
                    ms.closed()
                if p2:
                    zs.round(i)
                    dve.wait_ge(projected, i + 1)
                    wait(dve, x1_out, 16 * i)
                    zs.did(nc.vector.tensor_tensor(z[:], wide[1][:, 0, :].rearrange("p (t c) -> p t c", t=NT),
                                                   free_ap(bp_bc[:], [[0, NT], [1, P]]), ALU.add))
                    dve.wait_ge(z_step, zs.value())
                    layer_norm(zs, z, st2, mv2, rstd2, z, (z_rstd, i + 1),
                               lambda t, ins: zs.did(ins) if t < NT - 1 else ins.then_inc(z_ready, 1))
                    zs.closed()
                    dve.wait_ge(z_ready, i + 1)
                    dve.wait_ge(xr_in, 16 * (i + 1))
                    nc.vector.tensor_tensor(z[:], z[:], xr[:], ALU.add).then_inc(x1_ready, 1)
                if a1:
                    if not (isinstance(i, int) and i < 0):
                        dve.wait_ge(pv_done, (i + 1) * NG * NT)
                    ve = vext[e]
                    for u in range(2):
                        dve.wait_ge(qkv_done, 2 * (i + 2) + u + 1)
                        if u == 0:
                            wait(dve, rope_sin, NT * (i + 2))
                        nc.vector.tensor_tensor(
                            ve[:, 2 * u:2 * u + 2, :, 0:HS],
                            wide[1 - u][:, :, 2 * P:3 * P].rearrange("p t (h d) -> p t h d", h=NH),
                            free_ap(bqkv_bc[:], [[0, 2], [HS, NH], [1, HS]], 2 * P), ALU.add).then_inc(v_ready, 1)
                        nc.vector.tensor_tensor(qk[:, 2 * u:2 * u + 2, :], wide[1 - u][:, :, 0:2 * P],
                                                free_ap(bqkv_bc[:], [[0, 2], [1, 2 * P]]), ALU.add).then_inc(qk_biased, 1)
                    dve.wait_ge(qk_biased, 2 * (i + 3))
                    nc.vector.tensor_tensor(free_ap(ra[:, 0, :], [[2 * P, NT], [HS, 2 * NH], [1, HS]]),
                                            free_ap(qk[:, 0, :], [[2 * P, NT], [HS, 2 * NH], [1, HS]]),
                                            free_ap(cos_sb[:, 0, :], [[HS, NT], [0, 2 * NH], [1, HS]]),
                                            ALU.mult).then_inc(rope_cos, 1)
                    dve.wait_ge(rope_cos, i + 3)
                    dve.wait_ge(rope_sin, NT * (i + 3))
                    wait(dve, qk_transposed, i + 2)
                    heads_first = [[P, 2 * NT], [HS, NH], [1, HS]]
                    nc.vector.tensor_tensor(free_ap(rot[:, 0, 0, :], [[P, 2 * NT], [1, NH], [NH, HS]]),
                                            free_ap(ra[:, 0, :], heads_first), free_ap(rb[:, 0, :], heads_first),
                                            ALU.add).then_inc(rotated, 1)
                    dve.wait_ge(part1_ready, i + 3)
                    wait(dve, part3_ready, i + 2)
                    nc.vector.tensor_tensor(rest[:], wide[1][:], parts[:, :, 0, :], ALU.subtract).then_inc(rest_ready, 1)

            iterations(dve, body)

            dve.wait_ge(f_fw, N_FW)
            dve.wait_ge(ident_ready, 4)
            nc.vector.memset(cwh[:], 0.5).then_inc(filled, 1)
            dve.wait_ge(filled, 7)
            fs = Steps(f_step, 13)

            def tile(t, e):
                fs.round(t)

                def link(ins):
                    fs.did(ins)
                    dve.wait_ge(f_step, fs.value())
                    apart(dve)

                dve.wait_ge(f_in, 16 * (t + 1))
                link(nc.vector.bn_stats(f_st[:], f_x[:]))
                nc.vector.bn_aggr(f_mv[:], f_st[:]).then_inc(f_var, 1)
                dve.wait_ge(f_rstd, 2 * t + 1)
                nc.vector.tensor_scalar(f_xn[:], f_x[:], f_mv[:, 0:1], f_rs[:, 0:1], ALU.subtract, ALU.mult).then_inc(f_xn_ready, 1)
                dve.wait_ge(f_logits, t + 1)
                link(nc.vector.tensor_tensor(lg[:], heads_ps[:, 0:E], gb_bc[:], ALU.add))
                nc.vector.reduce_max(nmx[:], lg[:], AX.X, negate=True).then_inc(f_nmx, 1)
                dve.wait_ge(f_exp, t + 1)
                link(nc.vector.reciprocal(rsum[:], sume[:]))
                link(nc.vector.tensor_scalar(sc[:], ex[:], rsum[:, 0:1], None, ALU.mult))
                link(nc.vector.max(top[:], sc[:]))
                link(nc.vector.max_index(topi[:], top[:], sc[:]))
                link(nc.vector.tensor_copy(topf[:], topi[:]))
                link(nc.vector.tensor_scalar(oh1[:], iota_e[:], topf[:, 0:1], top[:, 0:1], ALU.is_equal, ALU.mult))
                link(nc.vector.tensor_scalar(cw[:], iota_e[:], topf[:, 1:2], top[:, 1:2], ALU.is_equal, ALU.mult))
                link(nc.vector.tensor_tensor(cw[:], cw[:], oh1[:], ALU.add))
                link(nc.vector.tensor_scalar(cwh[:, 0:E], cw[:], 0.5, None, ALU.mult))
                nc.vector.tensor_copy(lg[:], cw[:]).then_inc(f_cw, 1)

                for ei in range(NE):
                    b = ei % 2
                    n = t * NE + ei
                    dve.wait_ge(f_hg, n + 1)
                    wait(dve, f_a, n - 1)
                    nc.vector.tensor_tensor(hb[b][:], wide[b][:, 0, 0:2 * INTER], b13_bc[:, ei, :], ALU.add).then_inc(f_hb, 1)
                    if ei >= 1:
                        gated(t, ei - 1)
                gated(t, NE - 1)
                dve.wait_ge(f_y, t + 1)
                link(nc.vector.tensor_tensor(fz[:], heads_ps[:, 128:256], sb2_bc[:], ALU.add))
                link(nc.vector.bn_stats(f_st[:], fz[:]))
                nc.vector.bn_aggr(f_mv[:], f_st[:]).then_inc(f_var, 1)
                dve.wait_ge(f_rstd, 2 * t + 2)
                nc.vector.tensor_scalar(fz[:], fz[:], f_mv[:, 0:1], f_rs[:, 0:1], ALU.subtract, ALU.mult).then_inc(f_z, 1)
                dve.wait_ge(f_z, t + 1)
                wait(dve, f_out, 16 * (t - 1))
                nc.vector.tensor_tensor(fo[e][:], fz[:], f_x[:], ALU.add).then_inc(f_o, 1)
                fs.closed()

            def gated(t, ei):
                b = ei % 2
                n = t * NE + ei
                dve.wait_ge(f_th, n + 1)
                nc.vector.scalar_tensor_tensor(out=hs[b][:], in0=th[b][:], scalar=1.0, in1=hb[b][:, 0:INTER],
                                               op0=ALU.add, op1=ALU.mult).then_inc(f_hs, 1)
                dve.wait_ge(f_hs, n + 1)
                wait(dve, f_atr, n - 1)
                nc.vector.scalar_tensor_tensor(out=aa[b][:], in0=hs[b][:], scalar=cwh[:, ei:ei + 1], in1=hb[b][:, INTER:],
                                               op0=ALU.mult, op1=ALU.mult).then_inc(f_a, 1)

            tile(0, 0)
            tile(1, 1)
            with dve.Fori(1, NTILES // 2) as pair:
                tile(2 * pair, 0)
                tile(2 * pair + 1, 1)

        @block.tensor
        def _(pe):
            pe.wait_ge(weights_in, N_W)
            pe.wait_ge(ident_ready, 4)
            pe.wait_ge(filled, 6)

            def p1_unit(i, g, n, e):
                j, hs_ = P1_UNITS[n]
                u = g * len(P1_UNITS) + n
                if u >= 2:
                    pe.wait_ge(p1_max, (i + 1) * P1_N + u - 1)
                elif u == 0:
                    pass
                L = (j + 1) * P
                for k, h4 in enumerate(hs_):
                    h = g * HG + h4
                    if j >= 2:
                        o = wide[u % 2][:, k, 0:L]
                    else:
                        at = k * L
                        o = wide[u % 2][:, at // 512, at % 512:at % 512 + L]
                    nc.tensor.matmul(o, q4[1 - e][0:ROWS, h, j * P:(j + 1) * P], k4[1 - e][0:ROWS, h, 0:L],
                                     start=True, stop=False)
                    last = nc.tensor.matmul(o[:, j * P:L], identb[:], maskneg[:], start=False, stop=True)
                last.then_inc(p1_scores, 1)

            def p2_unit(i, g, n, e):
                kb, hs_ = P2_UNITS[n]
                u = g * P2_N + n
                N = T - kb * P
                wait(pe, exp_done, i * P2_N * NG + u - 1)
                for k, h4 in enumerate(hs_):
                    h = g * HG + h4
                    last = nc.tensor.matmul(score[u % 2][:, k * N:(k + 1) * N],
                                            k4[e][0:SROWS, h, kb * P:(kb + 1) * P], q4[e][0:SROWS, h, kb * P:T],
                                            start=True, stop=True)
                last.then_inc(p2_scores, 1)

            def values(i, g, kb, e):
                pe.wait_ge(masked, (i * NG + g) * NT + kb + 1)
                if kb == 0:
                    wait(pe, heads_copied, i * NG + g)
                for h4 in range(HG):
                    last = nc.tensor.matmul(heads_ps[32 * h4:32 * h4 + 32, kb * P:T],
                                            vext[e][:, kb, g * HG + h4, :], prob[kb][:, h4, :],
                                            start=(kb == 0), stop=(kb == NT - 1))
                last.then_inc(pv_done, 1)

            def heads_back(i, g):
                pe.wait_ge(heads_copied, i * NG + g + 1)
                wait(pe, y_ready, i * NG + g)
                if g == 0:
                    wait(pe, m_ready, i + 1)
                for t in range(NT):
                    last = nc.tensor.transpose(misc[:, t * P:(t + 1) * P], oT[:, t * P:(t + 1) * P], ident[:])
                last.then_inc(heads_transposed, 1)

            def body(i, a1, p1, p2, parity=None):
                e = par(i, parity)
                if p2:
                    pe.wait_ge(m_in, 16 * NPART * (i + 1))
                    pe.wait_ge(v_ready, 2 * (i + 1))
                for g in range(NG):
                    if p1 and g == 0:
                        pe.wait_ge(shuffled, (i + 2) * N_SHUFFLE)
                        wait(pe, rest_ready, i + 2)
                    todo = []
                    if p2:
                        s = [("s", n) for n in range(P2_N)]
                        todo = s[0:4] + ["1"] + s[4:6] + ["1"] + s[6:8] + [("v", 0), "b", "1"] + s[8:10] + [("v", 1), "1"] + s[10:11] + [("v", 2), "1", "1", ("v", 3)]
                    else:
                        todo = ["1"] * 6
                    n1 = 0
                    for what in todo:
                        if what == "1":
                            if p1:
                                p1_unit(i, g, n1, e)
                            n1 += 1
                        elif what == "b":
                            if g >= 1:
                                heads_back(i, g - 1)
                        elif what[0] == "s":
                            p2_unit(i, g, what[1], e)
                        else:
                            values(i, g, what[1], e)
                if p2:
                    heads_back(i, NG - 1)
                if p1:
                    pe.wait_ge(p1_max, (i + 2) * P1_N)
                    if p2:
                        pe.wait_ge(y_ready, (i + 1) * NG)
                    apart(pe)
                    nc.tensor.transpose(misc[0:64, 0:P], mx[:].rearrange("p h t -> p (h t)"), ident[:]).then_inc(max_transposed, 1)
                if p2:
                    pe.wait_ge(y_ready, (i + 1) * NG)
                    for t in range(NT):
                        last = nc.tensor.transpose(wide[0][:, 0, t * P:(t + 1) * P], y[:, t, :], ident[:])
                    last.then_inc(y_transposed, 1)
                    pe.wait_ge(yT_ready, i + 1)
                    for t in range(NT):
                        last = nc.tensor.matmul(wide[1][:, 0, t * P:(t + 1) * P], yT[:, t * P:(t + 1) * P], wp[:],
                                                start=True, stop=True)
                    last.then_inc(projected, 1)
                if a1:
                    pe.wait_ge(xn_ready, i + 3)
                    for t in range(NT):
                        last = nc.tensor.transpose(wide[0][:, 0, t * P:(t + 1) * P], xn[:, t, :], ident[:])
                    last.then_inc(x_transposed, 1)
                    pe.wait_ge(xnT_ready, i + 3)
                    if p2:
                        pe.wait_ge(z_step, Z_STEPS * i + 1)
                    for u in range(2):
                        if u == 1:
                            pass
                        for t in range(2):
                            tt = 2 * u + t
                            last = nc.tensor.matmul(wide[1 - u][:, t, 0:3 * P], xnT[:, tt * P:(tt + 1) * P], wqkv[:],
                                                    start=True, stop=True)
                        last.then_inc(qkv_done, 1)
                    pe.wait_ge(rotated, i + 3)
                    for s in range(2):
                        for t in range(NT):
                            last = nc.tensor.transpose(wide[1][:, s, t * P:(t + 1) * P], rot[:, t, s, :], ident[:])
                    last.then_inc(qk_transposed, 1)

            iterations(pe, body)

            pe.wait_ge(f_fw, N_FW)
            pe.wait_ge(x1_ready, B)

            def tile(t, e):
                pe.wait_ge(f_xn_ready, t + 1)
                wait(pe, f_cwT, t)
                nc.tensor.transpose(misc[:, 0:P], f_xn[:], ident[:]).then_inc(f_tr, 1)
                pe.wait_ge(f_xT_ready, t + 1)
                nc.tensor.matmul(heads_ps[:, 0:E], f_xT[:], gw_sb[:], start=True, stop=True).then_inc(f_logits, 1)

                def up(ei):
                    n = t * NE + ei
                    wait(pe, f_hb, n - 1)
                    nc.tensor.matmul(wide[ei % 2][:, 0, 0:2 * INTER], f_xT[:], w13_sb[:, ei, :], start=True, stop=True).then_inc(f_hg, 1)

                def across(ei):
                    n = t * NE + ei
                    pe.wait_ge(f_a, n + 1)
                    wait(pe, f_aT, n - 1)
                    for k in range(2):
                        last = nc.tensor.transpose(score[ei % 2][0:HALF, k * P:(k + 1) * P], aa[ei % 2][:, k * HALF:(k + 1) * HALF], ident[:])
                    last.then_inc(f_atr, 1)

                def down(ei):
                    n = t * NE + ei
                    pe.wait_ge(f_aT, n + 1)
                    for k in range(2):
                        last = nc.tensor.matmul(heads_ps[:, 128:256], aT[ei % 2][:, k, :], w2_sb[:, ei, k, :],
                                                start=(ei == 0 and k == 0), stop=False)

                up(0)
                up(1)
                pe.wait_ge(f_cw, t + 1)
                nc.tensor.transpose(misc[0:E, 256:256 + P], lg[:], ident[:]).then_inc(f_cwtr, 1)
                for ei in range(2, NE + 2):
                    if ei < NE:
                        up(ei)
                    across(ei - 2)
                    if ei >= 3:
                        down(ei - 3)
                down(NE - 1)
                pe.wait_ge(f_cwT, t + 1)
                nc.tensor.matmul(heads_ps[:, 128:256], cwT[:], b2_sb[:], start=False, stop=True).then_inc(f_y, 1)

            tile(0, 0)
            tile(1, 1)
            with pe.Fori(1, NTILES // 2) as pair:
                tile(2 * pair, 0)
                tile(2 * pair + 1, 1)


NAMES = ["attn_x", "attn_Wq", "attn_bq", "attn_Wk", "attn_bk", "attn_Wv", "attn_bv", "attn_Wp", "attn_bp",
         "ffn_gate_w", "ffn_gate_b", "ffn_w1", "ffn_b1", "ffn_w3", "ffn_b3", "ffn_w2", "ffn_b2",
         "ffn_sw1", "ffn_sb1", "ffn_sw3", "ffn_sb3", "ffn_sw2", "ffn_sb2"]


def rope_tables(length, dim):
    inv = (np.float32(1.0) / np.float32(10000.0) ** (np.arange(dim // 2, dtype=np.float32) * np.float32(2.0) / np.float32(dim))).astype(np.float32)
    ang = np.arange(length, dtype=np.float32)[:, None] * inv[None, :]
    c = np.repeat(np.cos(ang), 2, axis=1)
    s = np.repeat(np.sin(ang), 2, axis=1) * np.tile(np.array([-1.0, 1.0], np.float32), dim // 2)
    lay = lambda a: np.ascontiguousarray(a.astype(np.float32).reshape(length // P, P, dim).transpose(1, 0, 2))
    return lay(c), lay(s)


def kernel(**inputs):
    import concourse.bacc as bacc
    from concourse.bass_utils import run_bass_kernel_spmd

    nc = bacc.Bacc("TRN2", target_bir_lowering=False, num_devices=1)
    arrays, args = {}, []
    for name in NAMES:
        arrays[name] = np.ascontiguousarray(inputs["L0_" + name])
    arrays["cos"], arrays["sin"] = rope_tables(arrays["attn_x"].shape[1], HS)
    for name, a in arrays.items():
        args.append(nc.dram_tensor(name, a.shape, mybir.dt.from_np(a.dtype), kind="ExternalInput").ap())
    out = nc.dram_tensor("out", arrays["attn_x"].shape, F32, kind="ExternalOutput").ap()
    program(nc, *args, out)
    r = run_bass_kernel_spmd(nc, [arrays], core_ids=[0])
    return r.results[0]["out"]
```

```python
from contextlib import ExitStack

import numpy as np
import concourse.bass as bass
from concourse import mybir

F32 = mybir.dt.float32
BF16 = mybir.dt.bfloat16
U32 = mybir.dt.uint32
I32 = mybir.dt.int32
ALU = mybir.AluOpType
ACT = mybir.ActivationFunctionType
AX = mybir.AxisListType

P = 128
NT = 4
NH, HS = 16, 8
HG = 4
NG = NH // HG
NPART = 3
ROWS = NPART * NPART * HS
SROWS = ROWS + NPART
TOPK = 2
BG = 4
NEG = -1e30
EPS = 1e-5


def free_ap(ap, dims, offset=0):
    return bass.AP(ap.tensor, ap.offset + offset, [list(ap.ap[0])] + [list(d) for d in dims])


class Steps:

    def __init__(self, sem, per):
        self.sem, self.per, self.k, self.base = sem, per, 0, 0

    def round(self, n):
        self.base, self.k = n * self.per, 0

    def did(self, instruction):
        self.k += 1
        instruction.then_inc(self.sem, 1)

    def value(self):
        return self.base + self.k

    def closed(self):
        assert self.k == self.per, (self.k, self.per)


def wait(eng, sem, value):
    if isinstance(value, int) and value <= 0:
        return
    eng.wait_ge(sem, value)


P1_UNITS = [(3, (0, 1)), (3, (2, 3)), (2, (0, 1)), (2, (2, 3)), (1, (0, 1, 2, 3)), (0, (0, 1, 2, 3))]
P2_UNITS = ([(0, (h,)) for h in range(HG)] + [(1, (h,)) for h in range(HG)]
            + [(2, (0, 1)), (2, (2, 3))] + [(3, (0, 1, 2, 3))])
END_UNITS = ["y_transposed", "projected", "x_transposed", "qkv_0", "qkv_1", "qk_transposed"]
P1_N = len(P1_UNITS) * NG
P2_N = len(P2_UNITS)
LN_STEPS = 2 * NT
C_STEPS = NT * TOPK + LN_STEPS + NT
Z_STEPS = 1 + LN_STEPS + NT - 1


def program(nc, x, Wq, bq, Wk, bk, Wv, bv, Wp, bp, gate_w, gate_b, w1, b1, w3, b3, w2, b2,
            sw1, sb1, sw3, sb3, sw2, sb2, cos, sin, out):
    B, T, C = x.shape
    E, _, INTER = w1.shape
    HALF = INTER // 2
    NCH = sw1.shape[1] // HALF
    WIDE = 2 * INTER + P
    TS = B * NT * TOPK
    NBLK = -(-(TS + E) // BG) * BG
    assert T == NT * P and C == P and B % 2 == 0
    SCALE = 1.0 / float(np.sqrt(HS))
    ctx = ExitStack()
    with ctx:
        def sb(name, shape, dt=F32):
            return ctx.enter_context(nc.sbuf_tensor(name, shape, dt))

        def sem(name):
            return ctx.enter_context(nc.semaphore(name))

        x1 = nc.dram_tensor("x1_scratch", [B, T, C], F32, kind="Internal").ap()
        xn_d = nc.dram_tensor("normalised_scratch", [B, T, C], F32, kind="Internal").ap()
        shared_d = nc.dram_tensor("shared_scratch", [B, T, C], F32, kind="Internal").ap()
        sorted_d = nc.dram_tensor("sorted_scratch", [NBLK * P, C], F32, kind="Internal").ap()
        expert_d = nc.dram_tensor("expert_scratch", [NBLK * P, C], F32, kind="Internal").ap()

        wide = [ctx.enter_context(nc.psum_tensor(f"wide{n}", [P, 2, 512], F32)) for n in range(2)]
        score = [ctx.enter_context(nc.psum_tensor(f"score{n}", [P, 512], F32)) for n in range(2)]
        heads_ps = ctx.enter_context(nc.psum_tensor("heads_ps", [P, 512], F32))
        misc = ctx.enter_context(nc.psum_tensor("misc", [P, 512], F32))

        ident = sb("ident", [P, P])
        identb = sb("identb", [P, P], BF16)
        maskneg = sb("maskneg", [P, P], BF16)
        cos_sb = sb("cos_sb", [P, NT, HS])
        sin_sb = sb("sin_sb", [P, NT, HS])
        wqkv = sb("wqkv", [P, 3 * P])
        wp = sb("wp", [P, P])
        bqkv_bc = sb("bqkv_bc", [P, 3 * P])
        bp_bc = sb("bp_bc", [P, P])
        xt = sb("xt", [P, NT, P])
        xr = sb("xr", [P, NT, P])
        st = sb("st", [P, NT, 6])
        mv = sb("mv", [P, NT, 2])
        rstd = sb("rstd", [P, NT])
        vareps = sb("vareps", [P, NT])
        mhalf = sb("mhalf", [P, NT])
        st2 = sb("st2", [P, NT, 6])
        mv2 = sb("mv2", [P, NT, 2])
        rstd2 = sb("rstd2", [P, NT])
        xn = sb("xn", [P, NT, P])
        xnT = sb("xnT", [P, NT * P])
        qk = sb("qk", [P, NT, 2 * P])
        ra = sb("ra", [P, NT, 2 * P])
        rb = sb("rb", [P, NT, 2 * P])
        rot = sb("rot", [P, NT, 2, P])
        rest = sb("rest", [P, 2, T])
        parts = sb("parts", [P, 2, NPART, T], BF16)
        qk4 = sb("qk4", [P, 4, NH, T], BF16)
        q4 = [qk4[0:96, n, :, :] for n in range(2)]
        k4 = [qk4[0:96, 2 + n, :, :] for n in range(2)]
        vext = [sb(f"vext{n}", [P, NT, NH, 32]) for n in range(2)]
        mx = sb("mx", [P, NH, NT])
        mrest = sb("mrest", [64, P])
        mparts = sb("mparts", [64, NPART, P], BF16)
        prob = [sb(f"prob{k}", [P, HG, T - k * P]) for k in range(NT)]
        oT = sb("oT", [P, T])
        rinv = sb("rinv", [P, NT, HG])
        y = sb("y", [P, NT, P])
        yT = sb("yT", [P, T])
        z = sb("z", [P, NT, P])

        weights_in = sem("weights_in")
        waits_passed = sem("waits_passed")
        ident0 = sem("ident0")
        ident_ready = sem("ident_ready")
        filled = sem("filled")
        x_in = sem("x_in")
        xn_step = sem("xn_step")
        xn_ready = sem("xn_ready")
        x_vareps = sem("x_vareps")
        x_rstd = sem("x_rstd")
        z_vareps = sem("z_vareps")
        z_rstd = sem("z_rstd")
        x_transposed = sem("x_transposed")
        xnT_ready = sem("xnT_ready")
        qkv_done = sem("qkv_done")
        v_ready = sem("v_ready")
        qk_biased = sem("qk_biased")
        rope_cos = sem("rope_cos")
        rope_sin = sem("rope_sin")
        rotated = sem("rotated")
        qk_transposed = sem("qk_transposed")
        part1_ready = sem("part1_ready")
        rest_ready = sem("rest_ready")
        part2_ready = sem("part2_ready")
        part3_ready = sem("part3_ready")
        shuffled = sem("shuffled")
        p1_scores = sem("p1_scores")
        p1_max = sem("p1_max")
        max_transposed = sem("max_transposed")
        m_step = sem("m_step")
        m_ready = sem("m_ready")
        m_in = sem("m_in")
        p2_scores = sem("p2_scores")
        exp_done = sem("exp_done")
        masked = sem("masked")
        pv_done = sem("pv_done")
        heads_copied = sem("heads_copied")
        heads_transposed = sem("heads_transposed")
        rinv_ready = sem("rinv_ready")
        y_ready = sem("y_ready")
        y_transposed = sem("y_transposed")
        yT_ready = sem("yT_ready")
        projected = sem("projected")
        xr_in = sem("xr_in")
        z_step = sem("z_step")
        z_ready = sem("z_ready")
        x1_ready = sem("x1_ready")
        x1_out = sem("x1_out")

        N_SHUFFLE = 2 * NPART * NPART * 16
        N_W = 10 * 16
        x_v = x.rearrange("b (t p) c -> b p t c", p=P)
        x1_v = x1.rearrange("b (t p) c -> b p t c", p=P)
        out_v = out.rearrange("b (t p) c -> b p t c", p=P)
        row = lambda a: a.rearrange("(o n) -> o n", o=1)

        def iterations(eng, body):
            body(-2, True, False, False)
            body(-1, True, True, False)
            body(0, True, True, True)
            body(1, True, True, True)
            with eng.Fori(1, B // 2 - 1) as pair:
                body(2 * pair, True, True, True, 0)
                body(2 * pair + 1, True, True, True, 1)
            body(B - 2, False, True, True)
            body(B - 1, False, False, True)

        def apart(eng):
            eng.sem_inc(waits_passed, 1)

        def par(i, parity):
            return i % 2 if parity is None else parity

        block = ctx.enter_context(nc.Block())

        def view(tensor, dtype, dims, offset=0):
            flat = tensor[:].rearrange("p " + " ".join("abcd"[:len(tensor.shape) - 1]) + " -> p ("
                                       + " ".join("abcd"[:len(tensor.shape) - 1]) + ")") if len(tensor.shape) > 2 else tensor[:]
            if flat.dtype != dtype:
                flat = flat.bitcast(dtype)
            steps = [int(np.prod(dims[n + 1:])) for n in range(len(dims))]
            return free_ap(flat, [[a, b] for a, b in zip(steps, dims)], offset)

        w13_sb = sb("w13_sb", [P, E, 2 * INTER])
        w2_sb = sb("w2_sb", [HALF, E, 2, P])
        sw1_sb = sb("sw1_sb", [P, NCH * HALF])
        sw3_sb = sb("sw3_sb", [P, NCH * HALF])
        sw2_sb = sb("sw2_sb", [HALF, NCH, P])
        sb1_col = sb("sb1_col", [HALF, NCH])
        sb1_half = sb("sb1_half", [HALF, NCH])
        sb3_col = sb("sb3_col", [HALF, NCH])
        sb2_bc = sb("sb2_bc", [P, P])
        gw_sb = sb("gw_sb", [P, E])
        gb_bc = sb("gb_bc", [P, E])
        iota_e = sb("iota_e", [P, E])
        iota_blk = sb("iota_blk", [P, NBLK])
        before = sb("before", [P, P], BF16)
        upto = sb("upto", [E, E], BF16)
        onesb = sb("onesb", [P, P], BF16)
        bias_rows = view(qk4, BF16, [E, WIDE], (B + 2 * NCH) * T * 2)[0:NPART]
        bias_f = view(rest, F32, [WIDE])[0:E]
        bias_rest = view(rest, F32, [WIDE], WIDE)[0:E]
        bias_parts = view(parts, BF16, [NPART, WIDE])[0:E]
        r_x = [view(ra, F32, [NT, P], n * NT * P) for n in range(2)]
        r_xn = [view(qk, F32, [NT, P], n * NT * P) for n in range(2)]
        r_xT = [view(rb, F32, [T], n * T) for n in range(2)]
        xT_all = view(qk4, F32, [B, T])
        lg = sb("lg", [P, NT, E])
        lmax = sb("lmax", [P, NT])
        ex = sb("ex", [P, NT, E])
        esum = sb("esum", [P, NT])
        scores = sb("scores", [P, NT, E])
        top = sb("top", [P, NT, 8])
        topi = sb("topi", [P, NT, 8], U32)
        topf = sb("topf", [P, NT, 8])
        chosen = sb("chosen", [P, TS, E], BF16)
        chosen_w = sb("chosen_w", [P, TS])
        counts = sb("counts", [P, E], BF16)
        earlier = view(vext[0], BF16, [TS, E])
        place_e = view(prob[0], F32, [TS, E])
        place_f = sb("place_f", [P, TS])
        place = sb("place", [P, TS], U32)
        n_f = sb("n_f", [E, 1])
        n_i = sb("n_i", [E, 1], I32)
        nblk_i = sb("nblk_i", [E, 1], I32)
        nblk_b = sb("nblk_b", [E, 1], BF16)
        nblk_f = sb("nblk_f", [E, 1])
        first_of = sb("first_of", [E, E], BF16)
        last_blk = sb("last_blk", [E, 1])
        past = sb("past", [E, NBLK], BF16)
        first_place = sb("first_place", [P, E])
        blk_f = sb("blk_f", [P, NBLK])
        blk_expert = sb("blk_expert", [P, NBLK], I32)
        places = [sb(f"places{n}", [P, NT * TOPK], U32) for n in range(2)]
        d_xn = [view(ra, F32, [NT, P], n * NT * P) for n in range(2)]
        s_aT = [[view(qk4, F32, [T], B * T + (n * NCH + c) * T)[0:HALF] for c in range(NCH)] for n in range(2)]
        s_h = [view(prob[1], F32, [T], n * T)[0:HALF] for n in range(2)]
        s_th = [view(prob[2], F32, [T], n * T)[0:HALF] for n in range(2)]
        s_s = [view(rb, F32, [T], n * T)[0:HALF] for n in range(2)]
        s_z = [view(qk, F32, [NT, P], n * NT * P) for n in range(2)]
        e_x = [view(ra, F32, [BG, P], n * BG * P) for n in range(2)]
        e_xT = [sb(f"e_xT{n}", [P, P]) for n in range(2)]
        e_th = [view(rest, F32, [INTER], n * INTER) for n in range(2)]
        e_s = [view(rest, F32, [INTER], (2 + n) * INTER) for n in range(2)]
        e_a = [view(parts, F32, [INTER], n * INTER) for n in range(2)]
        e_aT = [view(parts, F32, [2, P], 2 * INTER + n * 2 * P)[0:HALF] for n in range(2)]
        e_y = [view(rot, F32, [BG, P], n * BG * P) for n in range(2)]
        c_y = [view(vext[1 - n], F32, [NT * TOPK, P]) for n in range(2)]
        c_w = [sb(f"c_w{n}", [P, NT * TOPK]) for n in range(2)]
        c_x = [view(qk, F32, [NT, P], n * NT * P) for n in range(2)]
        c_z = [view(rb, F32, [NT, P], n * NT * P) for n in range(2)]
        f_rstd = sb("f_rstd", [P, NT])
        f_mv = sb("f_mv", [P, NT, 2])
        f_st = sb("f_st", [P, NT, 6])

        f_fw = sem("f_fw")
        bias_step = sem("bias_step")
        bias_split = sem("bias_split")
        bias_in = sem("bias_in")
        zero_ready = sem("zero_ready")
        zeroed = sem("zeroed")
        r_in = [sem("r_in_even"), sem("r_in_odd")]
        r_step = sem("r_step")
        r_vareps = sem("r_vareps")
        r_rstd = sem("r_rstd")
        r_normalised = sem("r_normalised")
        r_stored = [sem("r_stored_even"), sem("r_stored_odd")]
        r_transposed = sem("r_transposed")
        r_xT_ready = sem("r_xT_ready")
        r_kept = [sem("r_kept_even"), sem("r_kept_odd")]
        r_logits = sem("r_logits")
        r_shifted = sem("r_shifted")
        r_exp = sem("r_exp")
        g_step = sem("g_step")
        r_chosen = sem("r_chosen")
        p_counts = sem("p_counts")
        p_step = sem("p_step")
        p_total = sem("p_total")
        p_blocks = sem("p_blocks")
        p_ends = sem("p_ends")
        p_past = sem("p_past")
        p_experts = sem("p_experts")
        p_earlier = sem("p_earlier")
        p_ranks = sem("p_ranks")
        p_done = sem("p_done")
        places_ready = sem("places_ready")
        d_in = [sem("d_in_even"), sem("d_in_odd")]
        d_out = [sem("d_out_even"), sem("d_out_odd")]
        s_up = sem("s_up")
        s_tanh = sem("s_tanh")
        s_halved = sem("s_halved")
        s_silu = sem("s_silu")
        s_gated = sem("s_gated")
        s_down = sem("s_down")
        s_ready = sem("s_ready")
        s_stored = [sem("s_stored_even"), sem("s_stored_odd")]
        e_in = [sem("e_in_even"), sem("e_in_odd")]
        e_transposed = sem("e_transposed")
        e_xT_ready = sem("e_xT_ready")
        e_up = sem("e_up")
        e_tanh = sem("e_tanh")
        e_silu = sem("e_silu")
        e_gated = sem("e_gated")
        e_across = sem("e_across")
        e_aT_ready = sem("e_aT_ready")
        e_down = sem("e_down")
        e_ready = sem("e_ready")
        e_stored = [sem("e_stored_even"), sem("e_stored_odd")]
        c_gathered = [sem("c_gathered_even"), sem("c_gathered_odd")]
        c_in = [sem("c_in_even"), sem("c_in_odd")]
        c_step = sem("c_step")
        c_vareps = sem("c_vareps")
        c_rstd = sem("c_rstd")
        c_ready = sem("c_ready")
        c_stored = [sem("c_stored_even"), sem("c_stored_odd")]
        N_FW = 16 * 18
        NZ = NBLK // 9
        GROUPS = NBLK // BG
        assert NBLK % 9 == 0 and TS == P and GROUPS % 2 == 0
        sorted_z = sorted_d.rearrange("(z p r) c -> z p (r c)", z=9, p=P)
        sorted_g = sorted_d.rearrange("(g k p) c -> g p k c", p=P, k=BG)
        expert_g = expert_d.rearrange("(g k p) c -> g p k c", p=P, k=BG)
        xn_v = xn_d.rearrange("b (t p) c -> b p t c", p=P)
        shared_v = shared_d.rearrange("b (t p) c -> b p t c", p=P)

        def through(b, e, unit):
            return (unit // 2) * (b - e) + unit

        def until(b, e, unit):
            return (unit // 2) * (b - e)

        def both(eng, sems, rounds, unit):
            for s in sems:
                eng.wait_ge(s, rounds // 2 * unit)

        def batches(eng, body):
            body(0, 0)
            body(1, 1)
            with eng.Fori(1, B // 2) as pair:
                body(2 * pair, 0)
                body(2 * pair + 1, 1)

        def groups(eng, body):
            body(0, 0, False)
            body(1, 1, False)
            with eng.Fori(1, GROUPS // 2 - 1) as pair:
                body(2 * pair, 0, False)
                body(2 * pair + 1, 1, False)
            body(GROUPS - 2, 0, False)
            body(GROUPS - 1, 1, True)

        @block.sync
        def _(sp):
            for w, s in ((wqkv[:, 0:P], Wq), (wqkv[:, P:2 * P], Wk), (wqkv[:, 2 * P:], Wv), (wp[:], Wp)):
                sp.dma_start(w, s).then_inc(weights_in, 16)
            for n, v in enumerate((bq, bk, bv)):
                sp.dma_start(bqkv_bc[:, n * P:(n + 1) * P], row(v).to_broadcast([P, P])).then_inc(weights_in, 16)
            sp.dma_start(bp_bc[:], row(bp).to_broadcast([P, P])).then_inc(weights_in, 16)
            sp.dma_start(cos_sb[:], cos).then_inc(weights_in, 16)
            sp.dma_start(sin_sb[:], sin).then_inc(weights_in, 16)

            def body(i, a1, p1, p2, parity=None):
                e = par(i, parity)
                if p2:
                    wait(sp, x1_ready, i)
                    apart(sp)
                    sp.dma_start(xr[:], x_v[i]).then_inc(xr_in, 16)
                if a1:
                    wait(sp, xn_ready, i + 2)
                    apart(sp)
                    sp.dma_start(xt[:], x_v[i + 2]).then_inc(x_in, 16)
                if p1:
                    sp.wait_ge(m_ready, i + 2)
                    for r in range(NPART):
                        sp.dma_start(q4[1 - e][ROWS + r:ROWS + r + 1, :, :], mparts[:, r, :]).then_inc(m_in, 16)
                if a1:
                    wait(sp, p2_scores, (i + 1) * P2_N * NG)
                    apart(sp)
                    if isinstance(i, int) and i < 0:
                        sp.wait_ge(filled, 4)
                    sp.wait_ge(part1_ready, i + 3)
                    apart(sp)
                    sp.wait_ge(part3_ready, i + 3)
                    for a in range(NPART):
                        for b in range(NPART):
                            r = (a * NPART + b) * HS
                            sp.dma_start(q4[e][r:r + HS, :, :], parts[:, 0, a, :]).then_inc(shuffled, 16)
                            sp.dma_start(k4[e][r:r + HS, :, :], parts[:, 1, b, :]).then_inc(shuffled, 16)
                if p2:
                    sp.wait_ge(x1_ready, i + 1)
                    apart(sp)
                    sp.dma_start(x1_v[i], z[:]).then_inc(x1_out, 16)

            iterations(sp, body)

            sp.wait_ge(x1_out, B * 16)

            def routing(b, e):
                if not (isinstance(b, int) and b < 2):
                    sp.wait_ge(r_normalised, b - 1)
                    apart(sp)
                sp.dma_start(r_x[e], x1_v[b]).then_inc(r_in[e], 16)

            def routed(b, e):
                sp.wait_ge(r_normalised, b + 1)
                apart(sp)
                sp.dma_start(xn_v[b], r_xn[e]).then_inc(r_stored[e], 16)
                sp.wait_ge(r_xT_ready, b + 1)
                apart(sp)
                sp.dma_start(xT_all[:, b, :], r_xT[e]).then_inc(r_kept[e], 16)

            routing(0, 0)
            routing(1, 1)
            routed(0, 0)
            routing(2, 0)
            routed(1, 1)
            with sp.Fori(1, B // 2 - 1) as pair:
                routing(2 * pair + 1, 1)
                routed(2 * pair, 0)
                routing(2 * pair + 2, 0)
                routed(2 * pair + 1, 1)
            routing(B - 1, 1)
            routed(B - 2, 0)
            routed(B - 1, 1)

            both(sp, r_stored, B, 16)
            sp.wait_ge(r_chosen, B)

            def dispatch(b, e):
                if not (isinstance(b, int) and b < 2):
                    sp.wait_ge(d_out[e], until(b, e, 16 * NT * TOPK))
                    apart(sp)
                sp.dma_start(d_xn[e], xn_v[b]).then_inc(d_in[e], 16)

            def shared(b, e):
                sp.wait_ge(s_ready, b + 1)
                apart(sp)
                sp.dma_start(shared_v[b], s_z[e]).then_inc(s_stored[e], 16)

            dispatch(0, 0)
            dispatch(1, 1)
            shared(0, 0)
            dispatch(2, 0)
            shared(1, 1)
            with sp.Fori(1, B // 2 - 1) as pair:
                dispatch(2 * pair + 1, 1)
                shared(2 * pair, 0)
                dispatch(2 * pair + 2, 0)
                shared(2 * pair + 1, 1)
            dispatch(B - 1, 1)
            shared(B - 2, 0)
            shared(B - 1, 1)

            both(sp, d_out, B, 16 * NT * TOPK)

            def block_in(g, e):
                if not (isinstance(g, int) and g < 2):
                    sp.wait_ge(e_transposed, BG * (g - 1))
                    apart(sp)
                sp.dma_start(e_x[e], sorted_g[g]).then_inc(e_in[e], 16)

            def block_out(g, e):
                sp.wait_ge(e_ready, BG * (g + 1))
                apart(sp)
                sp.dma_start(expert_g[g], e_y[e]).then_inc(e_stored[e], 16)

            block_in(0, 0)
            block_in(1, 1)
            block_in(2, 0)
            block_out(0, 0)
            with sp.Fori(0, GROUPS // 2 - 2) as pair:
                block_in(2 * pair + 3, 1)
                block_out(2 * pair + 1, 1)
                block_in(2 * pair + 4, 0)
                block_out(2 * pair + 2, 0)
            block_in(GROUPS - 1, 1)
            block_out(GROUPS - 3, 1)
            block_out(GROUPS - 2, 0)
            block_out(GROUPS - 1, 1)

            both(sp, s_stored, B, 16)

            def combine_in(b, e):
                if not (isinstance(b, int) and b < 2):
                    sp.wait_ge(c_stored[e], until(b, e, 16))
                    apart(sp)
                sp.dma_start(c_x[e], x1_v[b]).then_inc(c_in[e], 16)
                sp.dma_start(c_z[e], shared_v[b]).then_inc(c_in[e], 16)

            def combine_out(b, e):
                sp.wait_ge(c_ready, b + 1)
                apart(sp)
                sp.dma_start(out_v[b], c_z[e]).then_inc(c_stored[e], 16)

            combine_in(0, 0)
            combine_in(1, 1)
            combine_out(0, 0)
            combine_in(2, 0)
            combine_out(1, 1)
            with sp.Fori(1, B // 2 - 1) as pair:
                combine_in(2 * pair + 1, 1)
                combine_out(2 * pair, 0)
                combine_in(2 * pair + 2, 0)
                combine_out(2 * pair + 1, 1)
            combine_in(B - 1, 1)
            combine_out(B - 2, 0)
            combine_out(B - 1, 1)
            both(sp, c_stored, B, 16)
            both(sp, e_stored, GROUPS, 16)

        @block.gpsimd
        def _(pool):
            for m, s in ((ident, 0.0), (identb, 0.0), (maskneg, 0.0), (before, 1.0), (upto, 1.0), (onesb, 1.0)):
                nc.gpsimd.memset(m[:], s).then_inc(ident0, 1)
            nc.gpsimd.memset(mhalf[:], -0.5).then_inc(ident0, 1)
            pool.wait_ge(ident0, 7)
            nc.gpsimd.affine_select(out=ident[:], in_=ident[:], compare_op=ALU.not_equal, fill=1.0, base=0,
                                    pattern=[[-1, P]], channel_multiplier=1).then_inc(ident_ready, 1)
            nc.gpsimd.affine_select(out=identb[:], in_=identb[:], compare_op=ALU.not_equal, fill=1.0, base=0,
                                    pattern=[[-1, P]], channel_multiplier=1).then_inc(ident_ready, 1)
            nc.gpsimd.affine_select(out=maskneg[:], in_=maskneg[:], compare_op=ALU.is_ge, fill=NEG, base=0,
                                    pattern=[[-1, P]], channel_multiplier=1).then_inc(ident_ready, 1)
            nc.gpsimd.iota(iota_e[:], pattern=[[1, E]], base=0, channel_multiplier=0,
                           allow_small_or_imprecise_dtypes=True).then_inc(ident_ready, 1)
            nc.gpsimd.iota(iota_blk[:], pattern=[[1, NBLK]], base=0, channel_multiplier=0,
                           allow_small_or_imprecise_dtypes=True).then_inc(ident_ready, 1)
            nc.gpsimd.affine_select(out=before[:], in_=before[:], compare_op=ALU.is_gt, fill=0.0, base=0,
                                    pattern=[[1, P]], channel_multiplier=-1).then_inc(ident_ready, 1)
            nc.gpsimd.affine_select(out=upto[:], in_=upto[:], compare_op=ALU.is_ge, fill=0.0, base=0,
                                    pattern=[[1, E]], channel_multiplier=-1).then_inc(ident_ready, 1)

            def inverse_deviation(out_, var, added, before, done):
                apart(pool)
                nc.gpsimd.tensor_scalar(vareps[:, 0:out_.shape[1]], var, EPS, None, ALU.add).then_inc(added, 1)
                pool.wait_ge(added, before + 1)
                nc.gpsimd.tensor_tensor(out_, vareps[:, 0:out_.shape[1]], mhalf[:, 0:out_.shape[1]],
                                        ALU.pow).then_inc(done, 1)

            def body(i, a1, p1, p2, parity=None):
                if p2:
                    for g in range(NG):
                        for kb in range(NT):
                            n = P2_N * g + (4, 8, 10, 11)[kb]
                            pool.wait_ge(exp_done, i * P2_N * NG + n)
                            apart(pool)
                            nc.gpsimd.affine_select(
                                out=prob[kb][:, :, 0:P], in_=prob[kb][:, :, 0:P], compare_op=ALU.is_ge, fill=0.0,
                                base=0, pattern=[[0, HG], [1, P]], channel_multiplier=-1).then_inc(masked, 1)
                if a1:
                    pool.wait_ge(xn_step, (i + 3) * LN_STEPS)
                    inverse_deviation(rstd[:], mv[:].rearrange("p t s -> p (t s)")[:, 1:2 * NT:2], x_vareps, i + 2, x_rstd)
                if p2:
                    if a1:
                        pool.wait_ge(x_rstd, i + 3)
                    else:
                        wait(pool, z_rstd, i)
                    pool.wait_ge(z_step, i * Z_STEPS + 1 + LN_STEPS)
                    inverse_deviation(rstd2[:], mv2[:].rearrange("p t s -> p (t s)")[:, 1:2 * NT:2], z_vareps, i, z_rstd)
                if a1:
                    for t in range(NT):
                        if t % 2 == 0:
                            pool.wait_ge(qk_biased, 2 * (i + 2) + t // 2 + 1)
                            if t == 0:
                                wait(pool, rotated, i + 2)
                        nc.gpsimd.tensor_tensor(
                            free_ap(rb[:, t, :], [[HS, 2 * NH], [2, HS // 2], [1, 2]]),
                            free_ap(qk[:, t, :], [[HS, 2 * NH], [2, HS // 2], [-1, 2]], 1),
                            free_ap(sin_sb[:, t, :], [[0, 2 * NH], [2, HS // 2], [1, 2]]),
                            ALU.mult).then_inc(rope_sin, 1)
                    pool.wait_ge(rest_ready, i + 3)
                    if not (isinstance(i, int) and i < -1):
                        pool.wait_ge(shuffled, (i + 2) * N_SHUFFLE)
                    apart(pool)
                    nc.gpsimd.tensor_copy(parts[:, :, 1, :], rest[:]).then_inc(part2_ready, 1)
                    pool.wait_ge(part2_ready, i + 3)
                    nc.gpsimd.tensor_tensor(parts[:, :, 2, :], rest[:], parts[:, :, 1, :],
                                            ALU.subtract).then_inc(part3_ready, 1)

            pool.wait_ge(weights_in, N_W)
            iterations(pool, body)

            pool.wait_ge(z_rstd, B)

            def routing(b, e):
                pool.wait_ge(r_step, (b + 1) * LN_STEPS)
                inverse_deviation(f_rstd[:], f_mv[:].rearrange("p t s -> p (t s)")[:, 1:2 * NT:2], r_vareps, b, r_rstd)

            batches(pool, routing)

            pool.wait_ge(zeroed, 16 * 9)

            def dispatch(b, e):
                pool.wait_ge(places_ready, b + 1)
                pool.wait_ge(d_in[e], through(b, e, 16))
                apart(pool)
                for n in range(NT * TOPK):
                    nc.gpsimd.indirect_dma_start(
                        out=sorted_d[:, :], out_offset=bass.IndirectOffsetOnAxis(ap=places[e][:, n:n + 1], axis=0),
                        in_=d_xn[e][:, n // TOPK, :], in_offset=None).then_inc(d_out[e], 16)

            batches(pool, dispatch)

            both(pool, e_stored, GROUPS, 16)

            def gather(b, e):
                pool.wait_ge(places_ready, B + b + 1)
                apart(pool)
                if not (isinstance(b, int) and b < 2):
                    pool.wait_ge(c_step, (b - 1) * C_STEPS)
                    apart(pool)
                for n in range(NT * TOPK):
                    nc.gpsimd.indirect_dma_start(
                        out=c_y[e][:, n, :], out_offset=None, in_=expert_d[:, :],
                        in_offset=bass.IndirectOffsetOnAxis(ap=places[e][:, n:n + 1], axis=0)).then_inc(c_gathered[e], 16)

            def deviation(b, e):
                pool.wait_ge(c_step, b * C_STEPS + NT * TOPK + LN_STEPS)
                inverse_deviation(f_rstd[:], f_mv[:].rearrange("p t s -> p (t s)")[:, 1:2 * NT:2], c_vareps, b, c_rstd)

            gather(0, 0)
            gather(1, 1)
            deviation(0, 0)
            gather(2, 0)
            deviation(1, 1)
            with pool.Fori(1, B // 2 - 1) as pair:
                gather(2 * pair + 1, 1)
                deviation(2 * pair, 0)
                gather(2 * pair + 2, 0)
                deviation(2 * pair + 1, 1)
            gather(B - 1, 1)
            deviation(B - 2, 0)
            deviation(B - 1, 1)

        @block.scalar
        def _(act):
            for w, s in ((w13_sb[:, :, 0:INTER], w1.rearrange("e d h -> d e h")),
                         (w13_sb[:, :, INTER:], w3.rearrange("e d h -> d e h")),
                         (w2_sb[:, :, 0, :], w2[:, 0:HALF, :].rearrange("e h d -> h e d")),
                         (w2_sb[:, :, 1, :], w2[:, HALF:, :].rearrange("e h d -> h e d")),
                         (sw1_sb[:], sw1), (sw3_sb[:], sw3),
                         (sw2_sb[:], sw2.rearrange("(c h) d -> h c d", c=NCH)),
                         (gw_sb[:], gate_w), (gb_bc[:], row(gate_b).to_broadcast([P, E])),
                         (sb2_bc[:], row(sb2).to_broadcast([P, P]))):
                act.dma_start(w, s).then_inc(f_fw, 16)
            for c in range(NCH):
                for col, v in ((sb1_col, sb1), (sb3_col, sb3)):
                    act.dma_start(col[:, c:c + 1], v[c * HALF:(c + 1) * HALF].rearrange("(h o) -> h o", o=1)).then_inc(f_fw, 16)
            act.wait_ge(zero_ready, 1)
            for n in range(9):
                act.dma_start(sorted_z[n], view(prob[0], F32, [NZ * P])).then_inc(zeroed, 16)

            act.wait_ge(zeroed, 16 * 9)

            def body(i, a1, p1, p2, parity=None):
                if p2:
                    for g in range(NG):
                        for u, (kb, hs_) in enumerate(P2_UNITS):
                            n = g * P2_N + u
                            N = T - kb * P
                            act.wait_ge(p2_scores, i * P2_N * NG + n + 1)
                            wait(act, pv_done, i * NG * NT + (g - 1) * NT + kb + 1)
                            nc.scalar.activation(free_ap(prob[kb][:, hs_[0], :], [[1, N * len(hs_)]]),
                                                 score[n % 2][:, 0:N * len(hs_)],
                                                 ACT.Exp, scale=SCALE).then_inc(exp_done, 1)
                        act.wait_ge(pv_done, (i * NG + g + 1) * NT)
                        wait(act, heads_transposed, i * NG + g)
                        nc.scalar.activation(oT[:], heads_ps[:], ACT.Copy).then_inc(heads_copied, 1)
                    act.wait_ge(y_transposed, i + 1)
                    nc.scalar.activation(yT[:], wide[0][:, 0, :], ACT.Copy).then_inc(yT_ready, 1)
                if a1:
                    act.wait_ge(x_transposed, i + 3)
                    nc.scalar.activation(xnT[:], wide[0][:, 0, :], ACT.Copy).then_inc(xnT_ready, 1)
                    act.wait_ge(qk_transposed, i + 3)
                    if not (isinstance(i, int) and i < -1):
                        act.wait_ge(shuffled, (i + 2) * N_SHUFFLE)
                    nc.scalar.activation(parts[:, :, 0, :], wide[1][:], ACT.Copy).then_inc(part1_ready, 1)

            iterations(act, body)
            act.wait_ge(x1_ready, B)
            act.dma_start(bias_f[:, 0:INTER], b1).then_inc(bias_in, 16)
            act.dma_start(bias_f[:, INTER:2 * INTER], b3).then_inc(bias_in, 16)
            act.dma_start(bias_f[:, 2 * INTER:], b2).then_inc(bias_in, 16)
            act.wait_ge(bias_split, 1)
            for r in range(NPART):
                act.dma_start(bias_rows[r:r + 1, :, :], bias_parts[:, r, :]).then_inc(bias_in, 16)

            def transposed(b, e):
                act.wait_ge(r_transposed, b + 1)
                if not (isinstance(b, int) and b < 2):
                    act.wait_ge(r_kept[e], until(b, e, 16))
                nc.scalar.activation(r_xT[e], wide[e][:, 0, :], ACT.Copy).then_inc(r_xT_ready, 1)

            def exponential(b, e):
                act.wait_ge(r_shifted, b + 1)
                nc.scalar.activation(ex[:], lg[:], ACT.Exp).then_inc(r_exp, 1)

            transposed(0, 0)
            transposed(1, 1)
            exponential(0, 0)
            with act.Fori(1, B // 2) as pair:
                transposed(2 * pair, 0)
                exponential(2 * pair - 1, 1)
                transposed(2 * pair + 1, 1)
                exponential(2 * pair, 0)
            exponential(B - 1, 1)

            act.wait_ge(f_fw, N_FW)
            act.wait_ge(bias_split, 2)

            def shared(b, e):
                for c in range(NCH):
                    n = b * NCH + c
                    act.wait_ge(s_up, n + 1)
                    if not (isinstance(n, int) and n < 2):
                        act.wait_ge(s_silu, n - 1)
                    h = wide[c % 2][0:HALF, 0, :]
                    nc.scalar.activation(s_th[c % 2], h, ACT.Tanh, bias=sb1_half[:, c:c + 1], scale=0.5).then_inc(s_tanh, 1)
                    nc.scalar.activation(s_h[c % 2], h, ACT.Identity, bias=sb1_half[:, c:c + 1], scale=0.5).then_inc(s_halved, 1)

            batches(act, shared)

            def x_back(n, k):
                act.wait_ge(e_transposed, n + 1)
                if not (isinstance(n, int) and n < 2):
                    act.wait_ge(e_up, n - 1)
                nc.scalar.activation(e_xT[k % 2][:], (heads_ps, misc)[k % 2][:, 0:P], ACT.Copy).then_inc(e_xT_ready, 1)

            def a_back(n, k):
                act.wait_ge(e_across, n + 1)
                if not (isinstance(n, int) and n < 2):
                    act.wait_ge(e_down, n - 1)
                nc.scalar.activation(e_aT[k % 2][:], score[k % 2][0:HALF, 0:2 * P].rearrange("p (a b) -> p a b", a=2),
                                     ACT.Copy).then_inc(e_aT_ready, 1)

            def experts(g, e, last):
                for k in range(BG):
                    n = g * BG + k
                    if not (last and k == BG - 1):
                        x_back(n + 1, k + 1)
                    act.wait_ge(e_up, n + 1)
                    if not (isinstance(n, int) and n < 2):
                        act.wait_ge(e_silu, n - 1)
                    nc.scalar.activation(e_th[k % 2][:], wide[k % 2][:, 0, 0:INTER], ACT.Tanh, scale=0.5).then_inc(e_tanh, 1)
                    if not (isinstance(n, int) and n < 1):
                        a_back(n - 1, k + 1)

            x_back(0, 0)
            groups(act, experts)
            a_back(NBLK - 1, 1)

        @block.vector
        def _(dve):
            nc.vector.memset(view(prob[0], F32, [NZ * P]), 0.0).then_inc(zero_ready, 1)
            for n in range(2):
                nc.vector.memset(k4[n][64:96, :, :], 1.0).then_inc(filled, 1)
                nc.vector.memset(vext[n][:], 0.0).then_inc(filled, 1)
            dve.wait_ge(filled, 4)
            for n in range(2):
                nc.vector.memset(vext[n][:, :, :, HS:HS + 1], 1.0).then_inc(filled, 1)
            dve.wait_ge(filled, 6)
            dve.wait_ge(weights_in, N_W)
            ln1 = Steps(xn_step, LN_STEPS)
            ms = Steps(m_step, 3)
            zs = Steps(z_step, Z_STEPS)

            def maxima(i, g, n, e):
                j, hs_ = P1_UNITS[n]
                u = g * len(P1_UNITS) + n
                dve.wait_ge(p1_scores, (i + 1) * P1_N + u + 1)
                if u == 0:
                    wait(dve, max_transposed, i + 1)
                L = (j + 1) * P
                src = wide[u % 2][:, :, 0:L] if j >= 2 else free_ap(wide[u % 2][:, 0, :], [[L, HG], [1, L]])
                h0 = g * HG + hs_[0]
                nc.vector.tensor_reduce(mx[:, h0:h0 + len(hs_), j:j + 1], src, axis=AX.X,
                                        op=ALU.max).then_inc(p1_max, 1)

            def normalised_heads(i, g):
                dve.wait_ge(heads_transposed, i * NG + g + 1)
                hv = misc[:].rearrange("p (t h d) -> p t h d", t=NT, h=HG)
                if g == 0:
                    wait(dve, y_transposed, i)
                nc.vector.reciprocal(rinv[:].rearrange("p t (h o) -> p t h o", o=1), hv[:, :, :, HS:HS + 1]).then_inc(rinv_ready, 1)
                dve.wait_ge(rinv_ready, i * NG + g + 1)
                nc.vector.tensor_tensor(free_ap(y[:, 0, :], [[P, NT], [HS, HG], [1, HS]], g * HG * HS),
                                        hv[:, :, :, 0:HS],
                                        free_ap(rinv[:, 0, :], [[HG, NT], [1, HG], [0, HS]]),
                                        ALU.mult).then_inc(y_ready, 1)

            def layer_norm(steps, src, st_, mv_, rstd_, dst, rstd_ready, last):
                for t in range(NT):
                    steps.did(nc.vector.bn_stats(st_[:, t, :], src[:, t, :]))
                dve.wait_ge(steps.sem, steps.value())
                apart(dve)
                for t in range(NT):
                    steps.did(nc.vector.bn_aggr(mv_[:, t, :], st_[:, t, :]))
                dve.wait_ge(*rstd_ready)
                for t in range(NT):
                    ins = nc.vector.tensor_scalar(dst[:, t, :], src[:, t, :], mv_[:, t, 0:1], rstd_[:, t:t + 1],
                                                  ALU.subtract, ALU.mult)
                    last(t, ins)

            def body(i, a1, p1, p2, parity=None):
                e = par(i, parity)
                for g in range(NG):
                    if p1:
                        for n in range(3):
                            maxima(i, g, n, e)
                    if p2 and g >= 1:
                        normalised_heads(i, g - 1)
                    if p1:
                        for n in range(3, 6):
                            maxima(i, g, n, e)
                if p2:
                    normalised_heads(i, NG - 1)
                if a1:
                    ln1.round(i + 2)
                    dve.wait_ge(x_in, 16 * (i + 3))
                    wait(dve, x_transposed, i + 2)
                    layer_norm(ln1, xt, st, mv, rstd, xn, (x_rstd, i + 3),
                               lambda t, ins: ins.then_inc(xn_ready, 1) if t == NT - 1 else None)
                    ln1.closed()
                if p1:
                    ms.round(i + 1)
                    dve.wait_ge(max_transposed, i + 2)
                    wait(dve, m_in, 16 * NPART * (i + 1))
                    mt = misc[0:64, 0:P]
                    ms.did(nc.vector.tensor_scalar(mparts[:, 0, :], mt, -1.0, None, ALU.mult))
                    dve.wait_ge(m_step, ms.value())
                    ms.did(nc.vector.scalar_tensor_tensor(out=mrest[:], in0=mt, scalar=-1.0, in1=mparts[:, 0, :],
                                                          op0=ALU.mult, op1=ALU.subtract))
                    dve.wait_ge(m_step, ms.value())
                    ms.did(nc.vector.tensor_copy(mparts[:, 1, :], mrest[:]))
                    dve.wait_ge(m_step, ms.value())
                    nc.vector.tensor_tensor(mparts[:, 2, :], mrest[:], mparts[:, 1, :], ALU.subtract).then_inc(m_ready, 1)
                    ms.closed()
                if p2:
                    zs.round(i)
                    dve.wait_ge(projected, i + 1)
                    wait(dve, x1_out, 16 * i)
                    zs.did(nc.vector.tensor_tensor(z[:], wide[1][:, 0, :].rearrange("p (t c) -> p t c", t=NT),
                                                   free_ap(bp_bc[:], [[0, NT], [1, P]]), ALU.add))
                    dve.wait_ge(z_step, zs.value())
                    layer_norm(zs, z, st2, mv2, rstd2, z, (z_rstd, i + 1),
                               lambda t, ins: zs.did(ins) if t < NT - 1 else ins.then_inc(z_ready, 1))
                    zs.closed()
                    dve.wait_ge(z_ready, i + 1)
                    dve.wait_ge(xr_in, 16 * (i + 1))
                    nc.vector.tensor_tensor(z[:], z[:], xr[:], ALU.add).then_inc(x1_ready, 1)
                if a1:
                    if not (isinstance(i, int) and i < 0):
                        dve.wait_ge(pv_done, (i + 1) * NG * NT)
                    ve = vext[e]
                    for u in range(2):
                        dve.wait_ge(qkv_done, 2 * (i + 2) + u + 1)
                        if u == 0:
                            wait(dve, rope_sin, NT * (i + 2))
                        nc.vector.tensor_tensor(
                            ve[:, 2 * u:2 * u + 2, :, 0:HS],
                            wide[1 - u][:, :, 2 * P:3 * P].rearrange("p t (h d) -> p t h d", h=NH),
                            free_ap(bqkv_bc[:], [[0, 2], [HS, NH], [1, HS]], 2 * P), ALU.add).then_inc(v_ready, 1)
                        nc.vector.tensor_tensor(qk[:, 2 * u:2 * u + 2, :], wide[1 - u][:, :, 0:2 * P],
                                                free_ap(bqkv_bc[:], [[0, 2], [1, 2 * P]]), ALU.add).then_inc(qk_biased, 1)
                    dve.wait_ge(qk_biased, 2 * (i + 3))
                    nc.vector.tensor_tensor(free_ap(ra[:, 0, :], [[2 * P, NT], [HS, 2 * NH], [1, HS]]),
                                            free_ap(qk[:, 0, :], [[2 * P, NT], [HS, 2 * NH], [1, HS]]),
                                            free_ap(cos_sb[:, 0, :], [[HS, NT], [0, 2 * NH], [1, HS]]),
                                            ALU.mult).then_inc(rope_cos, 1)
                    dve.wait_ge(rope_cos, i + 3)
                    dve.wait_ge(rope_sin, NT * (i + 3))
                    wait(dve, qk_transposed, i + 2)
                    heads_first = [[P, 2 * NT], [HS, NH], [1, HS]]
                    nc.vector.tensor_tensor(free_ap(rot[:, 0, 0, :], [[P, 2 * NT], [1, NH], [NH, HS]]),
                                            free_ap(ra[:, 0, :], heads_first), free_ap(rb[:, 0, :], heads_first),
                                            ALU.add).then_inc(rotated, 1)
                    dve.wait_ge(part1_ready, i + 3)
                    wait(dve, part3_ready, i + 2)
                    nc.vector.tensor_tensor(rest[:], wide[1][:], parts[:, :, 0, :], ALU.subtract).then_inc(rest_ready, 1)

            iterations(dve, body)

            dve.wait_ge(f_fw, N_FW)
            dve.wait_ge(ident_ready, 7)
            dve.wait_ge(bias_in, 48)
            bs = Steps(bias_step, 3)
            bs.did(nc.vector.tensor_copy(bias_parts[:, 0, :], bias_f))
            dve.wait_ge(bias_step, 1)
            bs.did(nc.vector.tensor_tensor(bias_rest, bias_f, bias_parts[:, 0, :], ALU.subtract))
            dve.wait_ge(bias_step, 2)
            bs.did(nc.vector.tensor_copy(bias_parts[:, 1, :], bias_rest))
            dve.wait_ge(bias_step, 3)
            nc.vector.tensor_tensor(bias_parts[:, 2, :], bias_rest, bias_parts[:, 1, :], ALU.subtract).then_inc(bias_split, 1)
            nc.vector.tensor_scalar(sb1_half[:], sb1_col[:], 0.5, None, ALU.mult).then_inc(bias_split, 1)

            rs = Steps(r_step, LN_STEPS)
            gs = Steps(g_step, 6 + 2 * NT)

            def normalise(b, e):
                rs.round(b)
                dve.wait_ge(r_in[e], through(b, e, 16))
                if not (isinstance(b, int) and b < 2):
                    dve.wait_ge(r_transposed, b - 1)
                    dve.wait_ge(r_stored[e], until(b, e, 16))
                layer_norm(rs, r_x[e], f_st, f_mv, f_rstd, r_xn[e], (r_rstd, b + 1),
                           lambda t, ins: ins.then_inc(r_normalised, 1) if t == NT - 1 else None)
                rs.closed()

            def choose(b, e):
                gs.round(b)

                def link(ins):
                    gs.did(ins)
                    dve.wait_ge(g_step, gs.value())

                over_tiles = lambda ap, step, inner: free_ap(ap, [[step, NT]] + inner)
                dve.wait_ge(r_logits, b + 1)
                link(nc.vector.tensor_tensor(lg[:], misc[:, 0:NT * E].rearrange("p (t e) -> p t e", t=NT),
                                             over_tiles(gb_bc[:], 0, [[1, E]]), ALU.add))
                link(nc.vector.tensor_reduce(lmax[:], lg[:], axis=AX.X, op=ALU.max))
                nc.vector.tensor_tensor(lg[:], lg[:], over_tiles(lmax[:], 1, [[0, E]]), ALU.subtract).then_inc(r_shifted, 1)
                dve.wait_ge(r_exp, b + 1)
                link(nc.vector.tensor_reduce(esum[:], ex[:], axis=AX.X, op=ALU.add))
                link(nc.vector.reciprocal(esum[:], esum[:]))
                link(nc.vector.tensor_tensor(scores[:], ex[:], over_tiles(esum[:], 1, [[0, E]]), ALU.mult))
                apart(dve)
                for t in range(NT):
                    gs.did(nc.vector.max(top[:, t, :], scores[:, t, :]))
                dve.wait_ge(g_step, gs.value())
                apart(dve)
                for t in range(NT):
                    gs.did(nc.vector.max_index(topi[:, t, :], top[:, t, :], scores[:, t, :]))
                dve.wait_ge(g_step, gs.value())
                link(nc.vector.tensor_copy(topf[:], topi[:]))
                nc.vector.tensor_tensor(
                    chosen[:].rearrange("p (b t) e -> p b t e", b=B)[:, b, :, :].rearrange("p (t k) e -> p t k e", k=TOPK),
                    free_ap(iota_e[:], [[0, NT], [0, TOPK], [1, E]]),
                    free_ap(topf[:, 0, :], [[8, NT], [1, TOPK], [0, E]]), ALU.is_equal)
                nc.vector.tensor_copy(chosen_w[:].rearrange("p (b t k) -> p b t k", b=B, k=TOPK)[:, b, :, :],
                                      top[:, :, 0:TOPK]).then_inc(r_chosen, 1)
                gs.closed()

            normalise(0, 0)
            normalise(1, 1)
            choose(0, 0)
            with dve.Fori(1, B // 2) as pair:
                normalise(2 * pair, 0)
                choose(2 * pair - 1, 1)
                normalise(2 * pair + 1, 1)
                choose(2 * pair, 0)
            choose(B - 1, 1)

            dve.wait_ge(p_counts, 1)
            ps = Steps(p_step, 8)

            def pstep(ins):
                ps.did(ins)
                dve.wait_ge(p_step, ps.value())

            pstep(nc.vector.tensor_copy(counts[:], misc[:, 0:E]))
            nc.vector.tensor_tensor(earlier, free_ap(before[:], [[1, TS], [0, E]]), free_ap(counts[:], [[0, TS], [1, E]]),
                                    ALU.mult).then_inc(p_earlier, 1)
            dve.wait_ge(p_total, 1)
            pstep(nc.vector.tensor_scalar(n_f[:], heads_ps[0:E, 0:1], float(P - 1), None, ALU.add))
            pstep(nc.vector.tensor_copy(n_i[:], n_f[:]))
            pstep(nc.vector.tensor_single_scalar(nblk_i[:], n_i[:], 7, ALU.arith_shift_right))
            pstep(nc.vector.tensor_copy(nblk_f[:], nblk_i[:]))
            nc.vector.tensor_copy(nblk_b[:], nblk_f[:])
            nc.vector.tensor_scalar(first_of[:], before[0:E, 0:E], nblk_f[:, 0:1], None, ALU.mult).then_inc(p_blocks, 1)
            dve.wait_ge(p_ends, 1)
            pstep(nc.vector.tensor_copy(last_blk[:], score[0][0:E, 0:1]))
            nc.vector.tensor_scalar(first_place[:], score[1][:, 0:E], float(P), None, ALU.mult)
            nc.vector.tensor_scalar(past[:], iota_blk[0:E, :], last_blk[:, 0:1], None, ALU.is_ge).then_inc(p_past, 1)
            dve.wait_ge(p_experts, 1)
            pstep(nc.vector.tensor_scalar(blk_f[:], misc[:, 0:NBLK], float(E - 1), None, ALU.min))
            nc.vector.tensor_copy(blk_expert[:], blk_f[:]).then_inc(p_done, 1)
            dve.wait_ge(p_ranks, 1)
            half = TS // 2
            dve.wait_ge(p_past, 1)
            for n in range(2):
                last = nc.vector.tensor_tensor(place_e[:, n * half:(n + 1) * half, :],
                                               wide[n][:].rearrange("p a (t e) -> p (a t) e", e=E),
                                               free_ap(first_place[:], [[0, half], [1, E]]), ALU.add)
            last.then_inc(p_done, 1)
            dve.wait_ge(p_done, 2)
            nc.vector.tensor_tensor(place_e, place_e, chosen[:], ALU.mult).then_inc(p_done, 1)
            dve.wait_ge(p_done, 3)
            nc.vector.tensor_reduce(place_f[:], place_e, axis=AX.X, op=ALU.add).then_inc(p_done, 1)
            dve.wait_ge(p_done, 4)
            pstep(nc.vector.tensor_copy(place[:], place_f[:]))
            ps.closed()

            def shared(b, e):
                if not (isinstance(b, int) and b < 2):
                    dve.wait_ge(d_out[e], until(b, e, 16 * NT * TOPK))
                nc.vector.tensor_copy(places[e][:], place[:].rearrange("p (b n) -> p b n", b=B)[:, b, :]).then_inc(places_ready, 1)
                for c in range(NCH):
                    n = b * NCH + c
                    dve.wait_ge(s_halved, n + 1)
                    dve.wait_ge(s_tanh, n + 1)
                    if not (isinstance(n, int) and n < 2):
                        dve.wait_ge(s_gated, n - 1)
                    nc.vector.scalar_tensor_tensor(out=s_s[c % 2], in0=s_th[c % 2], scalar=1.0, in1=s_h[c % 2],
                                                   op0=ALU.add, op1=ALU.mult).then_inc(s_silu, 1)
                    dve.wait_ge(s_silu, n + 1)
                    if c == 0 and not (isinstance(b, int) and b < 2):
                        dve.wait_ge(s_down, b - 1)
                    nc.vector.scalar_tensor_tensor(out=s_aT[e][c], in0=wide[c % 2][0:HALF, 1, :], scalar=sb3_col[:, c:c + 1],
                                                   in1=s_s[c % 2], op0=ALU.add, op1=ALU.mult).then_inc(s_gated, 1)
                    if c == 2 and not (isinstance(b, int) and b < 1):
                        shared_out(b - 1, 1 - e)

            def shared_out(b, e):
                dve.wait_ge(s_down, b + 1)
                if not (isinstance(b, int) and b < 2):
                    dve.wait_ge(s_stored[e], until(b, e, 16))
                nc.vector.tensor_tensor(s_z[e], (heads_ps, misc)[e][:].rearrange("p (t c) -> p t c", t=NT),
                                        free_ap(sb2_bc[:], [[0, NT], [1, P]]), ALU.add).then_inc(s_ready, 1)

            batches(dve, shared)
            shared_out(B - 1, 1)

            def expert_out(n, k, g, e):
                dve.wait_ge(e_down, n + 1)
                if k == 0 and not (isinstance(g, int) and g < 2):
                    dve.wait_ge(e_stored[e], until(g, e, 16))
                nc.vector.tensor_copy(e_y[e][:, k, :], wide[k % 2][:, 1, 0:P]).then_inc(e_ready, 1)

            def experts(g, e, last):
                for k in range(BG):
                    n = g * BG + k
                    dve.wait_ge(e_tanh, n + 1)
                    nc.vector.scalar_tensor_tensor(out=e_s[k % 2][:], in0=e_th[k % 2][:], scalar=1.0, in1=wide[k % 2][:, 0, 0:INTER],
                                                   op0=ALU.add, op1=ALU.mult).then_inc(e_silu, 1)
                    dve.wait_ge(e_silu, n + 1)
                    if not (isinstance(n, int) and n < 2):
                        dve.wait_ge(e_across, n - 1)
                    nc.vector.scalar_tensor_tensor(out=e_a[k % 2][:], in0=e_s[k % 2][:], scalar=0.5,
                                                   in1=wide[k % 2][:, 0, INTER:2 * INTER],
                                                   op0=ALU.mult, op1=ALU.mult).then_inc(e_gated, 1)
                    if k >= 2:
                        expert_out(n - 2, k - 2, g, e)
                    elif not (isinstance(g, int) and g < 1):
                        expert_out(n - 2, k + BG - 2, g - 1, 1 - e)

            groups(dve, experts)
            expert_out(NBLK - 2, BG - 2, GROUPS - 1, 1)
            expert_out(NBLK - 1, BG - 1, GROUPS - 1, 1)

            cs = Steps(c_step, C_STEPS)

            def gather_places(b, e):
                if not (isinstance(b, int) and b < 2):
                    dve.wait_ge(c_gathered[e], until(b, e, 16 * NT * TOPK))
                else:
                    both(dve, d_out, B, 16 * NT * TOPK)
                nc.vector.tensor_copy(c_w[e][:], chosen_w[:].rearrange("p (b n) -> p b n", b=B)[:, b, :])
                nc.vector.tensor_copy(places[e][:], place[:].rearrange("p (b n) -> p b n", b=B)[:, b, :]).then_inc(places_ready, 1)

            def combine(b, e):
                cs.round(b)
                dve.wait_ge(c_gathered[e], through(b, e, 16 * NT * TOPK))
                dve.wait_ge(c_in[e], through(b, e, 32))
                dve.wait_ge(places_ready, B + b + 1)
                for k in range(TOPK):
                    for t in range(NT):
                        n = t * TOPK + k
                        cs.did(nc.vector.scalar_tensor_tensor(out=c_z[e][:, t, :], in0=c_y[e][:, n, :], scalar=c_w[e][:, n:n + 1],
                                                              in1=c_z[e][:, t, :], op0=ALU.mult, op1=ALU.add))
                    dve.wait_ge(c_step, cs.value())
                layer_norm(cs, c_z[e], f_st, f_mv, f_rstd, c_z[e], (c_rstd, b + 1), lambda t, ins: cs.did(ins))
                dve.wait_ge(c_step, cs.value())
                cs.closed()
                nc.vector.tensor_tensor(c_z[e], c_z[e], c_x[e], ALU.add).then_inc(c_ready, 1)

            gather_places(0, 0)
            gather_places(1, 1)
            combine(0, 0)
            gather_places(2, 0)
            combine(1, 1)
            with dve.Fori(1, B // 2 - 1) as pair:
                gather_places(2 * pair + 1, 1)
                combine(2 * pair, 0)
                gather_places(2 * pair + 2, 0)
                combine(2 * pair + 1, 1)
            gather_places(B - 1, 1)
            combine(B - 2, 0)
            combine(B - 1, 1)

        @block.tensor
        def _(pe):
            pe.wait_ge(weights_in, N_W)
            pe.wait_ge(ident_ready, 7)
            pe.wait_ge(filled, 6)

            def p1_unit(i, g, n, e):
                j, hs_ = P1_UNITS[n]
                u = g * len(P1_UNITS) + n
                if u >= 2:
                    pe.wait_ge(p1_max, (i + 1) * P1_N + u - 1)
                elif u == 0:
                    pass
                L = (j + 1) * P
                for k, h4 in enumerate(hs_):
                    h = g * HG + h4
                    if j >= 2:
                        o = wide[u % 2][:, k, 0:L]
                    else:
                        at = k * L
                        o = wide[u % 2][:, at // 512, at % 512:at % 512 + L]
                    nc.tensor.matmul(o, q4[1 - e][0:ROWS, h, j * P:(j + 1) * P], k4[1 - e][0:ROWS, h, 0:L],
                                     start=True, stop=False)
                    last = nc.tensor.matmul(o[:, j * P:L], identb[:], maskneg[:], start=False, stop=True)
                last.then_inc(p1_scores, 1)

            def p2_unit(i, g, n, e):
                kb, hs_ = P2_UNITS[n]
                u = g * P2_N + n
                N = T - kb * P
                wait(pe, exp_done, i * P2_N * NG + u - 1)
                for k, h4 in enumerate(hs_):
                    h = g * HG + h4
                    last = nc.tensor.matmul(score[u % 2][:, k * N:(k + 1) * N],
                                            k4[e][0:SROWS, h, kb * P:(kb + 1) * P], q4[e][0:SROWS, h, kb * P:T],
                                            start=True, stop=True)
                last.then_inc(p2_scores, 1)

            def values(i, g, kb, e):
                pe.wait_ge(masked, (i * NG + g) * NT + kb + 1)
                if kb == 0:
                    wait(pe, heads_copied, i * NG + g)
                for h4 in range(HG):
                    last = nc.tensor.matmul(heads_ps[32 * h4:32 * h4 + 32, kb * P:T],
                                            vext[e][:, kb, g * HG + h4, :], prob[kb][:, h4, :],
                                            start=(kb == 0), stop=(kb == NT - 1))
                last.then_inc(pv_done, 1)

            def heads_back(i, g):
                pe.wait_ge(heads_copied, i * NG + g + 1)
                wait(pe, y_ready, i * NG + g)
                if g == 0:
                    wait(pe, m_ready, i + 1)
                for t in range(NT):
                    last = nc.tensor.transpose(misc[:, t * P:(t + 1) * P], oT[:, t * P:(t + 1) * P], ident[:])
                last.then_inc(heads_transposed, 1)

            def body(i, a1, p1, p2, parity=None):
                e = par(i, parity)
                if p2:
                    pe.wait_ge(m_in, 16 * NPART * (i + 1))
                    pe.wait_ge(v_ready, 2 * (i + 1))
                for g in range(NG):
                    if p1 and g == 0:
                        pe.wait_ge(shuffled, (i + 2) * N_SHUFFLE)
                        wait(pe, rest_ready, i + 2)
                    todo = []
                    if p2:
                        s = [("s", n) for n in range(P2_N)]
                        todo = s[0:4] + ["1"] + s[4:6] + ["1"] + s[6:8] + [("v", 0), "b", "1"] + s[8:10] + [("v", 1), "1"] + s[10:11] + [("v", 2), "1", "1", ("v", 3)]
                    else:
                        todo = ["1"] * 6
                    n1 = 0
                    for what in todo:
                        if what == "1":
                            if p1:
                                p1_unit(i, g, n1, e)
                            n1 += 1
                        elif what == "b":
                            if g >= 1:
                                heads_back(i, g - 1)
                        elif what[0] == "s":
                            p2_unit(i, g, what[1], e)
                        else:
                            values(i, g, what[1], e)
                if p2:
                    heads_back(i, NG - 1)
                if p1:
                    pe.wait_ge(p1_max, (i + 2) * P1_N)
                    if p2:
                        pe.wait_ge(y_ready, (i + 1) * NG)
                    apart(pe)
                    nc.tensor.transpose(misc[0:64, 0:P], mx[:].rearrange("p h t -> p (h t)"), ident[:]).then_inc(max_transposed, 1)
                if p2:
                    pe.wait_ge(y_ready, (i + 1) * NG)
                    for t in range(NT):
                        last = nc.tensor.transpose(wide[0][:, 0, t * P:(t + 1) * P], y[:, t, :], ident[:])
                    last.then_inc(y_transposed, 1)
                    pe.wait_ge(yT_ready, i + 1)
                    for t in range(NT):
                        last = nc.tensor.matmul(wide[1][:, 0, t * P:(t + 1) * P], yT[:, t * P:(t + 1) * P], wp[:],
                                                start=True, stop=True)
                    last.then_inc(projected, 1)
                if a1:
                    pe.wait_ge(xn_ready, i + 3)
                    for t in range(NT):
                        last = nc.tensor.transpose(wide[0][:, 0, t * P:(t + 1) * P], xn[:, t, :], ident[:])
                    last.then_inc(x_transposed, 1)
                    pe.wait_ge(xnT_ready, i + 3)
                    if p2:
                        pe.wait_ge(z_step, Z_STEPS * i + 1)
                    for u in range(2):
                        if u == 1:
                            pass
                        for t in range(2):
                            tt = 2 * u + t
                            last = nc.tensor.matmul(wide[1 - u][:, t, 0:3 * P], xnT[:, tt * P:(tt + 1) * P], wqkv[:],
                                                    start=True, stop=True)
                        last.then_inc(qkv_done, 1)
                    pe.wait_ge(rotated, i + 3)
                    for s in range(2):
                        for t in range(NT):
                            last = nc.tensor.transpose(wide[1][:, s, t * P:(t + 1) * P], rot[:, t, s, :], ident[:])
                    last.then_inc(qk_transposed, 1)

            iterations(pe, body)

            pe.wait_ge(f_fw, N_FW)
            pe.wait_ge(x1_ready, B)

            def transposed(b, e):
                pe.wait_ge(r_normalised, b + 1)
                if not (isinstance(b, int) and b < 2):
                    pe.wait_ge(r_xT_ready, b - 1)
                for t in range(NT):
                    last = nc.tensor.transpose(wide[e][:, 0, t * P:(t + 1) * P], r_xn[e][:, t, :], ident[:])
                last.then_inc(r_transposed, 1)

            def logits(b, e):
                pe.wait_ge(r_xT_ready, b + 1)
                if not (isinstance(b, int) and b < 1):
                    pe.wait_ge(r_shifted, b)
                for t in range(NT):
                    last = nc.tensor.matmul(misc[:, t * E:(t + 1) * E], r_xT[e][:, t * P:(t + 1) * P], gw_sb[:],
                                            start=True, stop=True)
                last.then_inc(r_logits, 1)

            transposed(0, 0)
            transposed(1, 1)
            logits(0, 0)
            with pe.Fori(1, B // 2) as pair:
                transposed(2 * pair, 0)
                logits(2 * pair - 1, 1)
                transposed(2 * pair + 1, 1)
                logits(2 * pair, 0)
            logits(B - 1, 1)

            pe.wait_ge(r_chosen, B)
            for k in range(E):
                last = nc.tensor.matmul(misc[:, k:k + 1], chosen[:, :, k], onesb[:, 0:1], start=True, stop=True)
            last.then_inc(p_counts, 1)
            pe.wait_ge(p_step, 1)
            nc.tensor.matmul(heads_ps[0:E, 0:1], counts[:], onesb[:, 0:1], start=True, stop=True).then_inc(p_total, 1)
            pe.wait_ge(p_earlier, 1)
            flat = lambda ap: ap.rearrange("p t e -> p (t e)")
            chosen_flat = flat(chosen[:])
            for n in range(4):
                o = wide[n // 2][:, n % 2, :]
                nc.tensor.matmul(o, before[:], chosen_flat[:, n * 512:(n + 1) * 512], start=True, stop=False)
                last = nc.tensor.matmul(o, onesb[:], flat(earlier)[:, n * 512:(n + 1) * 512], start=False, stop=True)
            last.then_inc(p_ranks, 1)
            pe.wait_ge(p_blocks, 1)
            nc.tensor.matmul(score[0][0:E, 0:1], upto[:], nblk_b[:], start=True, stop=True)
            nc.tensor.matmul(score[1][:, 0:E], onesb[0:E, :], first_of[:], start=True, stop=True).then_inc(p_ends, 1)
            pe.wait_ge(p_past, 1)
            nc.tensor.matmul(misc[:, 0:NBLK], onesb[0:E, :], past[:], start=True, stop=True).then_inc(p_experts, 1)

            both(pe, r_kept, B, 16)
            pe.wait_ge(p_done, 2)

            def shared(b, e):
                for c in range(NCH):
                    n = b * NCH + c
                    if not (isinstance(n, int) and n < 2):
                        pe.wait_ge(s_gated, n - 1)
                    for k, w in enumerate((sw1_sb, sw3_sb)):
                        last = nc.tensor.matmul(wide[c % 2][0:HALF, k, :], w[:, c * HALF:(c + 1) * HALF], xT_all[:, b, :],
                                                start=True, stop=True)
                    last.then_inc(s_up, 1)
                    if c == 1 and not (isinstance(b, int) and b < 1):
                        shared_down(b - 1, 1 - e)

            def shared_down(b, e):
                pe.wait_ge(s_gated, NCH * (b + 1))
                if not (isinstance(b, int) and b < 2):
                    pe.wait_ge(s_ready, b - 1)
                for t in range(NT):
                    for c in range(NCH):
                        last = nc.tensor.matmul((heads_ps, misc)[e][:, t * P:(t + 1) * P], s_aT[e][c][:, t * P:(t + 1) * P],
                                                sw2_sb[:, c, :], start=(c == 0), stop=(c == NCH - 1))
                last.then_inc(s_down, 1)

            batches(pe, shared)
            shared_down(B - 1, 1)

            pe.wait_ge(bias_in, 16 * 6)
            pe.wait_ge(s_ready, B)
            expert_of = lambda n: pe.value_load(blk_expert[0:1, bass.ds(n, 1)], min_val=0, max_val=E - 1)

            def x_across(n, k, g, e):
                if k == 0:
                    pe.wait_ge(e_in[e], through(g, e, 16))
                if not (isinstance(n, int) and n < 2):
                    pe.wait_ge(e_xT_ready, n - 1)
                nc.tensor.transpose((heads_ps, misc)[k % 2][:, 0:P], e_x[e][:, k, :], ident[:]).then_inc(e_transposed, 1)

            def a_across(n, k):
                pe.wait_ge(e_gated, n + 1)
                if not (isinstance(n, int) and n < 2):
                    pe.wait_ge(e_aT_ready, n - 1)
                for half in range(2):
                    last = nc.tensor.transpose(score[k % 2][0:HALF, half * P:(half + 1) * P],
                                               e_a[k % 2][:, half * HALF:(half + 1) * HALF], ident[:])
                last.then_inc(e_across, 1)

            def down(n, k):
                expert = expert_of(n)
                pe.wait_ge(e_aT_ready, n + 1)
                if not (isinstance(n, int) and n < 2):
                    pe.wait_ge(e_ready, n - 1)
                o = wide[k % 2][:, 1, 0:P]
                for half in range(2):
                    nc.tensor.matmul(o, e_aT[k % 2][:, half, :], w2_sb[:, expert, half, :], start=(half == 0), stop=False)
                nc.tensor.matmul(o, onesb[0:NPART, :], bias_rows[:, expert, 2 * INTER:], start=False, stop=True).then_inc(e_down, 1)

            def experts(g, e, last):
                for k in range(BG):
                    n = g * BG + k
                    if k < BG - 1:
                        x_across(n + 1, k + 1, g, e)
                    elif not last:
                        x_across(n + 1, 0, g + 1, 1 - e)
                    expert = expert_of(n)
                    pe.wait_ge(e_xT_ready, n + 1)
                    if not (isinstance(n, int) and n < 2):
                        pe.wait_ge(e_gated, n - 1)
                    o = wide[k % 2][:, 0, 0:2 * INTER]
                    nc.tensor.matmul(o, e_xT[k % 2][:], w13_sb[:, expert, :], start=True, stop=False)
                    nc.tensor.matmul(o, onesb[0:NPART, :], bias_rows[:, expert, 0:2 * INTER], start=False, stop=True).then_inc(e_up, 1)
                    if not (isinstance(n, int) and n < 1):
                        a_across(n - 1, k + 1)
                    if not (isinstance(n, int) and n < 2):
                        down(n - 2, k)

            x_across(0, 0, 0, 0)
            groups(pe, experts)
            down(NBLK - 2, 0)
            a_across(NBLK - 1, 1)
            down(NBLK - 1, 1)


NAMES = ["attn_x", "attn_Wq", "attn_bq", "attn_Wk", "attn_bk", "attn_Wv", "attn_bv", "attn_Wp", "attn_bp",
         "ffn_gate_w", "ffn_gate_b", "ffn_w1", "ffn_b1", "ffn_w3", "ffn_b3", "ffn_w2", "ffn_b2",
         "ffn_sw1", "ffn_sb1", "ffn_sw3", "ffn_sb3", "ffn_sw2", "ffn_sb2"]


def rope_tables(length, dim):
    inv = (np.float32(1.0) / np.float32(10000.0) ** (np.arange(dim // 2, dtype=np.float32) * np.float32(2.0) / np.float32(dim))).astype(np.float32)
    ang = np.arange(length, dtype=np.float32)[:, None] * inv[None, :]
    c = np.repeat(np.cos(ang), 2, axis=1)
    s = np.repeat(np.sin(ang), 2, axis=1) * np.tile(np.array([-1.0, 1.0], np.float32), dim // 2)
    lay = lambda a: np.ascontiguousarray(a.astype(np.float32).reshape(length // P, P, dim).transpose(1, 0, 2))
    return lay(c), lay(s)


def kernel(**inputs):
    import concourse.bacc as bacc
    from concourse.bass_utils import run_bass_kernel_spmd

    nc = bacc.Bacc("TRN2", target_bir_lowering=False, num_devices=1)
    arrays, args = {}, []
    for name in NAMES:
        arrays[name] = np.ascontiguousarray(inputs["L0_" + name])
    arrays["cos"], arrays["sin"] = rope_tables(arrays["attn_x"].shape[1], HS)
    for name, a in arrays.items():
        args.append(nc.dram_tensor(name, a.shape, mybir.dt.from_np(a.dtype), kind="ExternalInput").ap())
    out = nc.dram_tensor("out", arrays["attn_x"].shape, F32, kind="ExternalOutput").ap()
    program(nc, *args, out)
    r = run_bass_kernel_spmd(nc, [arrays], core_ids=[0])
    return r.results[0]["out"]
```

```python
from contextlib import ExitStack

import numpy as np
import concourse.bass as bass
from concourse import mybir

F32 = mybir.dt.float32
BF16 = mybir.dt.bfloat16
U32 = mybir.dt.uint32
I32 = mybir.dt.int32
ALU = mybir.AluOpType
ACT = mybir.ActivationFunctionType
AX = mybir.AxisListType

P = 128
NT = 4
NH, HS = 16, 8
HG = 4
NG = NH // HG
NPART = 3
ROWS = NPART * NPART * HS
SROWS = ROWS + NPART
TOPK = 2
BG = 4
ROUND = 4
NEG = -1e30
EPS = 1e-5


def free_ap(ap, dims, offset=0):
    return bass.AP(ap.tensor, ap.offset + offset, [list(ap.ap[0])] + [list(d) for d in dims])


class Steps:

    def __init__(self, sem, per):
        self.sem, self.per, self.k, self.base = sem, per, 0, 0

    def round(self, n):
        self.base, self.k = n * self.per, 0

    def did(self, instruction):
        self.k += 1
        instruction.then_inc(self.sem, 1)

    def value(self):
        return self.base + self.k

    def closed(self):
        assert self.k == self.per, (self.k, self.per)


def wait(eng, sem, value):
    if isinstance(value, int) and value <= 0:
        return
    eng.wait_ge(sem, value)


P1_UNITS = [(3, (0, 1)), (3, (2, 3)), (2, (0, 1)), (2, (2, 3)), (1, (0, 1, 2, 3)), (0, (0, 1, 2, 3))]
P2_UNITS = ([(0, (h,)) for h in range(HG)] + [(1, (h,)) for h in range(HG)]
            + [(2, (0, 1)), (2, (2, 3))] + [(3, (0, 1, 2, 3))])
P1_N = len(P1_UNITS) * NG
P2_N = len(P2_UNITS)
LN_STEPS = 2 * NT
C_STEPS = NT * TOPK + LN_STEPS + NT
Z_STEPS = LN_STEPS + NT - 1

SLOTS = [
    "s0 last_v s1 X V last_heads s2 s3 late_p Q cos mask0 Y v0 s4 W s5 s6 late_p sin0 s7 sin1 late_p mask1 s8 "
    "s9 mask2 mask3 late_p v1 s10 zstats zrstd M1 v2",
    "s0 s1 sin2 mask0 p s2 s3 p v3 mask1 s4 s5 sin3 p s6 mask2 v0 s7 mask3 Z p s8 p s9 heads stats s10 v1 v2",
    "s0 p p s1 s2 p residual s3 s4 p R mask0 rstats s5 s6 v3 p p s7 s8 heads mask1 v0 s9 p p v1 rrstd s10 M0 "
    "p mask2 rnormal T mask3 v2",
    "s0 s1 v3 p normal s2 s3 rX s4 p rstd mask0 s5 p mask1 third0 s6 third1 choose s7 v0 rL second p mask2 s8 "
    "heads mask3 p s9 p chosen rexp s10 v1 v2",
]
LATE = " ".join(SLOTS).split().count("late_p")
OFFSET = dict(stats=3, rstd=3, normal=3, X=2, Q=2, cos=2, sin=2, R=2, T=2, second=2, third=2, V=1, p=1, late_p=0, M0=1, M1=0,
              s=0, v=0, mask=0, heads=0, last_v=-1, last_heads=-1, Y=-1, W=-1, zstats=-1, zrstd=-1, Z=-1, residual=-1,
              rstats=-1, rrstd=-1, rnormal=-1, rX=-1, rL=-1, choose=-1, rexp=-1, chosen=-1)
WIDE_STEPS = ("V", "X", "Q", "Y", "W", "T", "p", "rX", "rL")
MISC_STEPS = ("heads", "M")


class Step:

    def __init__(self, what, offset, group, n, unit):
        self.what, self.offset, self.group, self.n, self.unit = what, offset, group, n, unit


def schedule():
    steps, passed, units = [], 0, 0
    for slot, text in enumerate(SLOTS):
        for word in text.split():
            what = word.rstrip("0123456789")
            offset = OFFSET[word] if word in OFFSET else OFFSET[what]
            n = int(word[len(what):] or 0)
            group = slot
            if what in ("last_v", "last_heads"):
                n, group, what = NT - 1, NG - 1, what[len("last_"):]
            elif word == "v3" or what == "heads":
                group = slot - 1
            elif what == "late_p":
                what, n, passed = "p", P1_N - LATE + passed, passed + 1
            elif what == "p":
                n, passed = passed - LATE, passed + 1
            unit = None
            if what in WIDE_STEPS:
                unit, units = units, units + 1
            steps.append(Step(what, offset, group, n, unit))
    assert passed == P1_N and units % 2 == 0
    return steps


STEPS = schedule()
WIDE_USES = [s for s in STEPS if s.unit is not None]
GATE_UNIT = next(s.unit for s in STEPS if s.what == "rL") % 2
MISC_USES = [s for s in STEPS if s.what in MISC_STEPS]


def program(nc, x, Wq, bq, Wk, bk, Wv, bv, Wp, bp, gate_w, gate_b, w1, b1, w3, b3, w2, b2,
            sw1, sb1, sw3, sb3, sw2, sb2, cos, sin, out):
    B, T, C = x.shape
    E, _, INTER = w1.shape
    HALF = INTER // 2
    NCH = sw1.shape[1] // HALF
    WIDE = 2 * INTER + P
    TS = B * NT * TOPK
    NBLK = -(-(TS + E) // BG) * BG
    assert T == NT * P and C == P and B % 2 == 0
    EARLY = 5 * B // 8
    assert EARLY % 2 == 0 and B - EARLY <= EARLY - 3
    SCALE = 1.0 / float(np.sqrt(HS))
    ctx = ExitStack()
    with ctx:
        def sb(name, shape, dt=F32):
            return ctx.enter_context(nc.sbuf_tensor(name, shape, dt))

        def sem(name):
            return ctx.enter_context(nc.semaphore(name))

        x1 = nc.dram_tensor("x1_scratch", [B, T, C], F32, kind="Internal").ap()
        xT_d = nc.dram_tensor("transposed_scratch", [P, B, T], F32, kind="Internal").ap()
        xn_d = nc.dram_tensor("normalised_scratch", [B, T, C], F32, kind="Internal").ap()
        shared_d = nc.dram_tensor("shared_scratch", [B, T, C], F32, kind="Internal").ap()
        sorted_d = nc.dram_tensor("sorted_scratch", [NBLK * P, C], F32, kind="Internal").ap()
        expert_d = nc.dram_tensor("expert_scratch", [NBLK * P, C], F32, kind="Internal").ap()

        wide = [ctx.enter_context(nc.psum_tensor(f"wide{n}", [P, 2, 512], F32)) for n in range(2)]
        score = [ctx.enter_context(nc.psum_tensor(f"score{n}", [P, 512], F32)) for n in range(2)]
        heads_ps = ctx.enter_context(nc.psum_tensor("heads_ps", [P, 512], F32))
        misc = ctx.enter_context(nc.psum_tensor("misc", [P, 512], F32))

        ident = sb("ident", [P, P])
        identb = sb("identb", [P, P], BF16)
        maskneg = sb("maskneg", [P, P], BF16)
        cos_sb = sb("cos_sb", [P, NT, HS])
        sin_sb = sb("sin_sb", [P, NT, HS])
        wqkv = sb("wqkv", [P, 3 * P])
        wp = sb("wp", [P, P])
        bqkv_bc = sb("bqkv_bc", [P, 3 * P])
        bp_bc = sb("bp_bc", [P, P])
        zeros = sb("zeros", [P, P])
        xt = sb("xt", [P, NT, P])
        xr = sb("xr", [P, NT, P])
        st = sb("st", [P, NT, 6])
        mv = sb("mv", [P, NT, 2])
        rstd = sb("rstd", [P, NT])
        vareps = sb("vareps", [P, NT])
        vareps2 = sb("vareps2", [P, NT])
        vareps3 = sb("vareps3", [P, NT])
        mhalf = sb("mhalf", [P, NT])
        st2 = sb("st2", [P, NT, 6])
        mv2 = sb("mv2", [P, NT, 2])
        rstd2 = sb("rstd2", [P, NT])
        xn = sb("xn", [P, NT, P])
        xnT = sb("xnT", [P, NT * P])
        qk = sb("qk", [P, NT, 2 * P])
        ra = sb("ra", [P, NT, 2 * P])
        rb = sb("rb", [P, NT, 2 * P])
        rot = sb("rot", [P, NT, 2, P])
        rest = sb("rest", [P, 2, T])
        parts = sb("parts", [P, 2, NPART, T], BF16)
        qk4 = sb("qk4", [P, 4, NH, T], BF16)
        q4 = [qk4[0:96, n, :, :] for n in range(2)]
        k4 = [qk4[0:96, 2 + n, :, :] for n in range(2)]
        vext = [sb(f"vext{n}", [P, NT, NH, 32]) for n in range(2)]
        mx = sb("mx", [P, NH, NT])
        mrest = sb("mrest", [NH // 2 * NT, P])
        mparts = [sb(f"mparts{n}", [NH // 2 * NT, NPART, P], BF16) for n in range(2)]
        prob = [sb(f"prob{k}", [P, HG, T - k * P]) for k in range(NT)]
        oT = sb("oT", [P, T])
        rinv = sb("rinv", [P, NT, HG])
        y = sb("y", [P, NT, P])
        yT = sb("yT", [P, T])
        z = sb("z", [P, NT, P])

        weights_in = sem("weights_in")
        waits_passed = sem("waits_passed")
        ident0 = sem("ident0")
        ident_ready = sem("ident_ready")
        filled = sem("filled")
        rows_filled = sem("rows_filled")
        x_in = sem("x_in")
        xn_step = sem("xn_step")
        xn_ready = sem("xn_ready")
        r_centred = sem("r_centred")
        x_vareps = sem("x_vareps")
        x_rstd = sem("x_rstd")
        z_vareps = sem("z_vareps")
        z_rstd = sem("z_rstd")
        x_transposed = sem("x_transposed")
        xnT_ready = sem("xnT_ready")
        v_made = sem("v_made")
        qk_made = sem("qk_made")
        v_ready = sem("v_ready")
        qk_biased = sem("qk_biased")
        rope_cos = sem("rope_cos")
        rope_sin = sem("rope_sin")
        rotated = sem("rotated")
        qk_transposed = sem("qk_transposed")
        part1_ready = sem("part1_ready")
        rest_ready = sem("rest_ready")
        part2_ready = sem("part2_ready")
        part3_ready = sem("part3_ready")
        shuffled = sem("shuffled")
        p1_scores = sem("p1_scores")
        p1_max = sem("p1_max")
        max_transposed = [sem("max_transposed_low"), sem("max_transposed_high")]
        m_step = [sem("m_step_low"), sem("m_step_high")]
        m_ready = [sem("m_ready_low"), sem("m_ready_high")]
        m_in = [sem("m_in_low"), sem("m_in_high")]
        p2_scores = sem("p2_scores")
        exp_done = sem("exp_done")
        masked = sem("masked")
        pv_done = sem("pv_done")
        heads_copied = sem("heads_copied")
        heads_transposed = sem("heads_transposed")
        rinv_ready = sem("rinv_ready")
        y_ready = sem("y_ready")
        y_transposed = sem("y_transposed")
        yT_ready = sem("yT_ready")
        projected = sem("projected")
        xr_in = sem("xr_in")
        z_biased = sem("z_biased")
        z_step = sem("z_step")
        z_ready = sem("z_ready")
        x1_ready = sem("x1_ready")
        x1_out = sem("x1_out")

        N_SHUFFLE = 2 * NPART * NPART * 16
        N_W = 10 * 16
        x_v = x.rearrange("b (t p) c -> b p t c", p=P)
        x1_v = x1.rearrange("b (t p) c -> b p t c", p=P)
        out_v = out.rearrange("b (t p) c -> b p t c", p=P)
        row = lambda a: a.rearrange("(o n) -> o n", o=1)

        def iterations(eng, body):
            for i in (-3, -2, -1, 0, 1):
                body(i)
            with eng.Fori(1, B // 2 - 2) as pair:
                body(2 * pair, 0)
                body(2 * pair + 1, 1)
            for i in range(B - 4, B + 1):
                body(i)

        def exists(i, offset):
            return not isinstance(i, int) or 0 <= i + offset < B

        def last_use(i, at, uses, every):
            back = 0
            while True:
                at -= every
                if at < 0:
                    at, back = at + len(uses), back + 1
                if isinstance(i, int) and i - back < -3:
                    return None
                if not isinstance(i, int) or 0 <= i - back + uses[at].offset < B:
                    return i + uses[at].offset - back, uses[at]

        def unit_free(eng, i, step):
            read_by = dict(V=v_ready, X=xnT_ready, Q=qk_biased, Y=yT_ready, W=z_biased, T=rest_ready,
                           rX=r_xT_ready, rL=r_biased)
            last = last_use(i, step.unit, WIDE_USES, 2)
            if last is not None and last[1].what == "p":
                eng.wait_ge(p1_max, last[0] * P1_N + last[1].n + 1)
            elif last is not None:
                eng.wait_ge(read_by[last[1].what], last[0] + 1)

        def misc_free(eng, i, step):
            last = last_use(i, MISC_USES.index(step), MISC_USES, 1)
            if last is not None and last[1].what == "heads":
                eng.wait_ge(y_ready, last[0] * NG + last[1].group + 1)
            elif last is not None:
                eng.wait_ge(m_ready[last[1].n], last[0] + 1)

        def apart(eng):
            eng.sem_inc(waits_passed, 1)

        def par(i, parity):
            return i % 2 if parity is None else parity

        block = ctx.enter_context(nc.Block())

        def view(tensor, dtype, dims, offset=0):
            flat = tensor[:].rearrange("p " + " ".join("abcd"[:len(tensor.shape) - 1]) + " -> p ("
                                       + " ".join("abcd"[:len(tensor.shape) - 1]) + ")") if len(tensor.shape) > 2 else tensor[:]
            if flat.dtype != dtype:
                flat = flat.bitcast(dtype)
            steps = [int(np.prod(dims[n + 1:])) for n in range(len(dims))]
            return free_ap(flat, [[a, b] for a, b in zip(steps, dims)], offset)

        w13_sb = sb("w13_sb", [P, E, 2 * INTER])
        w2_sb = sb("w2_sb", [HALF, E, 2, P])
        sw1_sb = sb("sw1_sb", [P, NCH * HALF])
        sw3_sb = sb("sw3_sb", [P, NCH * HALF])
        sw2_sb = sb("sw2_sb", [HALF, NCH, P])
        sb1_col = sb("sb1_col", [HALF, NCH])
        sb1_half = sb("sb1_half", [HALF, NCH])
        sb3_col = sb("sb3_col", [HALF, NCH])
        sb2_bc = sb("sb2_bc", [P, P])
        gw_sb = sb("gw_sb", [P, E])
        gb_bc = sb("gb_bc", [P, E])
        iota_e = sb("iota_e", [P, E])
        iota_blk = sb("iota_blk", [P, NBLK])
        before = sb("before", [P, P], BF16)
        upto = sb("upto", [E, E], BF16)
        onesb = sb("onesb", [P, P], BF16)
        bias_rows = view(qk4, BF16, [E, WIDE], (B + 2 * NCH) * T * 2)[0:NPART]
        bias_f = view(rest, F32, [WIDE])[0:E]
        bias_rest = view(rest, F32, [WIDE], WIDE)[0:E]
        bias_parts = view(parts, BF16, [NPART, WIDE])[0:E]
        xT_all = view(qk4, F32, [B, T])
        lg = sb("lg", [P, NT, E])
        lmax = sb("lmax", [P, NT])
        ex = sb("ex", [P, NT, E])
        esum = sb("esum", [P, NT])
        scores = sb("scores", [P, NT, E])
        top = sb("top", [P, NT, 8])
        topi = sb("topi", [P, NT, 8], U32)
        topf = sb("topf", [P, NT, 8])
        chosen = sb("chosen", [P, TS, E], BF16)
        chosen_w = sb("chosen_w", [P, TS])
        counts = sb("counts", [P, E], BF16)
        earlier = view(vext[0], BF16, [TS, E])
        place_e = view(prob[0], F32, [TS, E])
        place_f = sb("place_f", [P, TS])
        place = sb("place", [P, TS], U32)
        n_f = sb("n_f", [E, 1])
        n_i = sb("n_i", [E, 1], I32)
        nblk_i = sb("nblk_i", [E, 1], I32)
        nblk_b = sb("nblk_b", [E, 1], BF16)
        nblk_f = sb("nblk_f", [E, 1])
        first_of = sb("first_of", [E, E], BF16)
        last_blk = sb("last_blk", [E, 1])
        past = sb("past", [E, NBLK], BF16)
        first_place = sb("first_place", [P, E])
        blk_f = sb("blk_f", [P, NBLK])
        blk_expert = sb("blk_expert", [P, NBLK], I32)
        places = [sb(f"places{n}", [P, NT * TOPK], U32) for n in range(2)]
        d_xn = [view(ra, F32, [NT, P], n * NT * P) for n in range(2)]
        s_aT = [[view(qk4, F32, [T], B * T + (n * NCH + c) * T)[0:HALF] for c in range(NCH)] for n in range(2)]
        s_h = [view(prob[1], F32, [T], n * T)[0:HALF] for n in range(2)]
        s_th = [view(prob[2], F32, [T], n * T)[0:HALF] for n in range(2)]
        s_s = [view(prob[0], F32, [T], n * T)[0:HALF] for n in range(2)]
        s_z = [view(prob[0], F32, [NT, P], (2 + n) * NT * P) for n in range(2)]
        e_x = [view(ra, F32, [BG, P], n * BG * P) for n in range(2)]
        e_xT = [sb(f"e_xT{n}", [P, P]) for n in range(2)]
        e_th = [view(rest, F32, [INTER], n * INTER) for n in range(2)]
        e_s = [view(rest, F32, [INTER], (2 + n) * INTER) for n in range(2)]
        e_a = [view(parts, F32, [INTER], n * INTER) for n in range(2)]
        e_aT = [view(parts, F32, [2, P], 2 * INTER + n * 2 * P)[0:HALF] for n in range(2)]
        e_y = [view(rot, F32, [BG, P], n * BG * P) for n in range(2)]
        c_y = [view(vext[1 - n], F32, [NT * TOPK, P]) for n in range(2)]
        c_w = [sb(f"c_w{n}", [P, NT * TOPK]) for n in range(2)]
        c_x = [view(qk, F32, [NT, P], n * NT * P) for n in range(2)]
        c_z = [view(rb, F32, [NT, P], n * NT * P) for n in range(2)]
        f_rstd = sb("f_rstd", [P, NT])
        f_mv = sb("f_mv", [P, NT, 2])
        f_st = sb("f_st", [P, NT, 6])

        f_fw = sem("f_fw")
        bias_step = sem("bias_step")
        bias_split = sem("bias_split")
        sb1_halved = sem("sb1_halved")
        bias_in = sem("bias_in")
        zero_ready = sem("zero_ready")
        zeroed = sem("zeroed")
        r_step = sem("r_step")
        r_vareps = sem("r_vareps")
        r_rstd = sem("r_rstd")
        r_normalised = sem("r_normalised")
        r_stored = sem("r_stored")
        r_transposed = sem("r_transposed")
        r_xT_ready = sem("r_xT_ready")
        r_kept = sem("r_kept")
        r_back = sem("r_back")
        r_logits = sem("r_logits")
        r_biased = sem("r_biased")
        r_shifted = sem("r_shifted")
        r_exp = sem("r_exp")
        g_step = sem("g_step")
        r_chosen = sem("r_chosen")
        p_counts = sem("p_counts")
        p_step = sem("p_step")
        p_total = sem("p_total")
        p_blocks = sem("p_blocks")
        p_ends = sem("p_ends")
        p_past = sem("p_past")
        p_experts = sem("p_experts")
        p_earlier = sem("p_earlier")
        p_ranks = sem("p_ranks")
        p_done = sem("p_done")
        places_ready = sem("places_ready")
        c_weights = sem("c_weights")
        d_in = [sem("d_in_even"), sem("d_in_odd")]
        d_out = [sem("d_out_even"), sem("d_out_odd")]
        s_up = sem("s_up")
        s_tanh = sem("s_tanh")
        s_halved = sem("s_halved")
        s_silu = sem("s_silu")
        s_gated = sem("s_gated")
        s_down = sem("s_down")
        s_ready = sem("s_ready")
        s_stored = [sem("s_stored_even"), sem("s_stored_odd")]
        e_in = [sem("e_in_even"), sem("e_in_odd")]
        e_transposed = sem("e_transposed")
        e_xT_ready = sem("e_xT_ready")
        e_up = sem("e_up")
        e_tanh = sem("e_tanh")
        e_silu = sem("e_silu")
        e_gated = sem("e_gated")
        e_across = sem("e_across")
        e_aT_ready = sem("e_aT_ready")
        e_down = sem("e_down")
        e_ready = sem("e_ready")
        e_stored = [sem("e_stored_even"), sem("e_stored_odd")]
        c_gathered = [sem("c_gathered_even"), sem("c_gathered_odd")]
        c_in = [sem("c_in_even"), sem("c_in_odd")]
        c_step = sem("c_step")
        c_vareps = sem("c_vareps")
        c_rstd = sem("c_rstd")
        c_ready = sem("c_ready")
        c_stored = [sem("c_stored_even"), sem("c_stored_odd")]
        N_FW = 16 * 18
        NZ = NBLK // 9
        GROUPS = NBLK // BG
        assert NBLK % 9 == 0 and TS == P and GROUPS % 2 == 0
        sorted_z = sorted_d.rearrange("(z p r) c -> z p (r c)", z=9, p=P)
        sorted_g = sorted_d.rearrange("(g k p) c -> g p k c", p=P, k=BG)
        expert_g = expert_d.rearrange("(g k p) c -> g p k c", p=P, k=BG)
        xn_v = xn_d.rearrange("b (t p) c -> b p t c", p=P)
        shared_v = shared_d.rearrange("b (t p) c -> b p t c", p=P)

        def through(b, e, unit):
            return (unit // 2) * (b - e) + unit

        def until(b, e, unit):
            return (unit // 2) * (b - e)

        def both(eng, sems, rounds, unit):
            for s in sems:
                eng.wait_ge(s, rounds // 2 * unit)

        def batches(eng, body):
            body(0, 0)
            body(1, 1)
            with eng.Fori(1, B // 2) as pair:
                body(2 * pair, 0)
                body(2 * pair + 1, 1)

        def shared_early(eng, body):
            body(0, 0, True)
            body(1, 1, False)
            with eng.Fori(1, EARLY // 2) as pair:
                body(2 * pair, 0, False)
                body(2 * pair + 1, 1, False)

        def shared_late(eng, body):
            body(EARLY, 0, True)
            body(EARLY + 1, 1, False)
            with eng.Fori(EARLY // 2 + 1, B // 2) as pair:
                body(2 * pair, 0, False)
                body(2 * pair + 1, 1, False)

        def groups(eng, body):
            body(0, 0, False)
            body(1, 1, False)
            with eng.Fori(1, GROUPS // 2 - 1) as pair:
                body(2 * pair, 0, False)
                body(2 * pair + 1, 1, False)
            body(GROUPS - 2, 0, False)
            body(GROUPS - 1, 1, True)

        @block.sync
        def _(sp):
            for w, s in ((wqkv[:, 0:P], Wq), (wqkv[:, P:2 * P], Wk), (wqkv[:, 2 * P:], Wv), (wp[:], Wp)):
                sp.dma_start(w, s).then_inc(weights_in, 16)
            for n, v in enumerate((bq, bk, bv)):
                sp.dma_start(bqkv_bc[:, n * P:(n + 1) * P], row(v).to_broadcast([P, P])).then_inc(weights_in, 16)
            sp.dma_start(bp_bc[:], row(bp).to_broadcast([P, P])).then_inc(weights_in, 16)
            sp.dma_start(cos_sb[:], cos).then_inc(weights_in, 16)
            sp.dma_start(sin_sb[:], sin).then_inc(weights_in, 16)

            def maxima_in(b, e, half):
                sp.wait_ge(m_ready[half], b + 1)
                for r in range(NPART):
                    sp.dma_start(q4[e][ROWS + r:ROWS + r + 1, half * NH // 2:(half + 1) * NH // 2, :],
                                 mparts[half][:, r, :]).then_inc(m_in[half], 16)

            def body(i, parity=None):
                e = par(i, parity)
                if exists(i, -1):
                    wait(sp, x1_ready, i - 1)
                    apart(sp)
                    sp.dma_start(xr[:], x_v[i - 1]).then_inc(xr_in, 16)
                if exists(i, 3):
                    wait(sp, xn_ready, i + 3)
                    apart(sp)
                    sp.dma_start(xt[:], x_v[i + 3]).then_inc(x_in, 16)
                if exists(i, 0):
                    maxima_in(i, e, 1)
                if exists(i, -1):
                    sp.wait_ge(x1_ready, i)
                    apart(sp)
                    sp.dma_start(x1_v[i - 1], z[:]).then_inc(x1_out, 16)
                if exists(i, 1):
                    maxima_in(i + 1, 1 - e, 0)
                if exists(i, -1):
                    sp.wait_ge(r_normalised, i)
                    apart(sp)
                    sp.dma_start(xn_v[i - 1], z[:]).then_inc(r_stored, 16)
                    sp.wait_ge(r_xT_ready, i)
                    apart(sp)
                    sp.dma_start(xT_d[:, i - 1, :], yT[:]).then_inc(r_kept, 16)
                if exists(i, 2):
                    wait(sp, p2_scores, (i + 1) * P2_N * NG)
                    apart(sp)
                    if isinstance(i, int) and i < 0:
                        sp.wait_ge(rows_filled, 2)
                    sp.wait_ge(part1_ready, i + 3)
                    apart(sp)
                    sp.wait_ge(part3_ready, 2 * (i + 3))
                    for a in range(NPART):
                        for b in range(NPART):
                            r = (a * NPART + b) * HS
                            sp.dma_start(q4[e][r:r + HS, :, :], parts[:, 0, a, :]).then_inc(shuffled, 16)
                            sp.dma_start(k4[e][r:r + HS, :, :], parts[:, 1, b, :]).then_inc(shuffled, 16)

            iterations(sp, body)

            sp.wait_ge(r_kept, 16 * B)
            sp.dma_start(xT_all, xT_d).then_inc(r_back, 16)
            sp.wait_ge(r_stored, 16 * B)
            sp.wait_ge(r_chosen, B)

            def dispatch(b, e):
                if not (isinstance(b, int) and b < 2):
                    sp.wait_ge(d_out[e], until(b, e, 16 * NT * TOPK))
                    apart(sp)
                sp.dma_start(d_xn[e], xn_v[b]).then_inc(d_in[e], 16)

            dispatch(0, 0)
            dispatch(1, 1)
            with sp.Fori(1, B // 2) as pair:
                dispatch(2 * pair, 0)
                dispatch(2 * pair + 1, 1)

            both(sp, d_out, B, 16 * NT * TOPK)

            def block_in(g, e):
                if not (isinstance(g, int) and g < 2):
                    sp.wait_ge(e_transposed, BG * (g - 1))
                    apart(sp)
                sp.dma_start(e_x[e], sorted_g[g]).then_inc(e_in[e], 16)

            def block_out(g, e):
                sp.wait_ge(e_ready, BG * (g + 1))
                apart(sp)
                sp.dma_start(expert_g[g], e_y[e]).then_inc(e_stored[e], 16)

            block_in(0, 0)
            block_in(1, 1)
            block_in(2, 0)
            block_out(0, 0)
            with sp.Fori(0, GROUPS // 2 - 2) as pair:
                block_in(2 * pair + 3, 1)
                block_out(2 * pair + 1, 1)
                block_in(2 * pair + 4, 0)
                block_out(2 * pair + 2, 0)
            block_in(GROUPS - 1, 1)
            block_out(GROUPS - 3, 1)
            block_out(GROUPS - 2, 0)
            block_out(GROUPS - 1, 1)

            def combine_in(b, e):
                if not (isinstance(b, int) and b < 2):
                    sp.wait_ge(c_stored[e], until(b, e, 16))
                    apart(sp)
                sp.dma_start(c_x[e], x1_v[b]).then_inc(c_in[e], 16)
                sp.wait_ge(s_stored[e], through(b, e, 16))
                apart(sp)
                sp.dma_start(c_z[e], shared_v[b]).then_inc(c_in[e], 16)

            def combine_out(b, e):
                sp.wait_ge(c_ready, b + 1)
                apart(sp)
                sp.dma_start(out_v[b], c_z[e]).then_inc(c_stored[e], 16)

            combine_in(0, 0)
            combine_in(1, 1)
            combine_out(0, 0)
            combine_in(2, 0)
            combine_out(1, 1)
            with sp.Fori(1, B // 2 - 1) as pair:
                combine_in(2 * pair + 1, 1)
                combine_out(2 * pair, 0)
                combine_in(2 * pair + 2, 0)
                combine_out(2 * pair + 1, 1)
            combine_in(B - 1, 1)
            combine_out(B - 2, 0)
            combine_out(B - 1, 1)
            sp.wait_ge(x1_out, 16 * B)
            both(sp, c_stored, B, 16)
            both(sp, e_stored, GROUPS, 16)

        @block.gpsimd
        def _(pool):
            for m, s in ((ident, 0.0), (identb, 0.0), (maskneg, 0.0), (before, 1.0), (upto, 1.0), (onesb, 1.0)):
                nc.gpsimd.memset(m[:], s).then_inc(ident0, 1)
            nc.gpsimd.memset(mhalf[:], -0.5).then_inc(ident0, 1)
            pool.wait_ge(ident0, 7)
            nc.gpsimd.affine_select(out=ident[:], in_=ident[:], compare_op=ALU.not_equal, fill=1.0, base=0,
                                    pattern=[[-1, P]], channel_multiplier=1).then_inc(ident_ready, 1)
            nc.gpsimd.affine_select(out=identb[:], in_=identb[:], compare_op=ALU.not_equal, fill=1.0, base=0,
                                    pattern=[[-1, P]], channel_multiplier=1).then_inc(ident_ready, 1)
            nc.gpsimd.affine_select(out=maskneg[:], in_=maskneg[:], compare_op=ALU.is_ge, fill=NEG, base=0,
                                    pattern=[[-1, P]], channel_multiplier=1).then_inc(ident_ready, 1)
            nc.gpsimd.iota(iota_e[:], pattern=[[1, E]], base=0, channel_multiplier=0,
                           allow_small_or_imprecise_dtypes=True).then_inc(ident_ready, 1)
            nc.gpsimd.iota(iota_blk[:], pattern=[[1, NBLK]], base=0, channel_multiplier=0,
                           allow_small_or_imprecise_dtypes=True).then_inc(ident_ready, 1)
            nc.gpsimd.affine_select(out=before[:], in_=before[:], compare_op=ALU.is_gt, fill=0.0, base=0,
                                    pattern=[[1, P]], channel_multiplier=-1).then_inc(ident_ready, 1)
            nc.gpsimd.affine_select(out=upto[:], in_=upto[:], compare_op=ALU.is_ge, fill=0.0, base=0,
                                    pattern=[[1, E]], channel_multiplier=-1).then_inc(ident_ready, 1)

            def inverse_deviation(out_, var, added, before, done, sums=vareps):
                apart(pool)
                nc.gpsimd.tensor_scalar(sums[:, 0:out_.shape[1]], var, EPS, None, ALU.add).then_inc(added, 1)
                pool.wait_ge(added, before + 1)
                nc.gpsimd.tensor_tensor(out_, sums[:, 0:out_.shape[1]], mhalf[:, 0:out_.shape[1]],
                                        ALU.pow).then_inc(done, 1)

            def normalised(src, mv_, rstd_, dst, centred, done, b):
                nc.gpsimd.tensor_tensor(dst[:], src[:], free_ap(mv_[:, 0, :], [[2, NT], [0, P]]), ALU.subtract).then_inc(centred, 1)
                pool.wait_ge(centred, b + 1)
                nc.gpsimd.tensor_tensor(dst[:], dst[:], free_ap(rstd_[:], [[1, NT], [0, P]]), ALU.mult).then_inc(done, 1)

            def body(i, parity=None):
                if isinstance(i, int) and i == -2:
                    pool.wait_ge(x_rstd, 1)
                    for n in range(2):
                        nc.gpsimd.memset(k4[n][64:96, :, :], 1.0).then_inc(rows_filled, 1)
                        pool.wait_ge(rows_filled, n + 1)
                for step in STEPS:
                    if not exists(i, step.offset):
                        continue
                    b, n = i + step.offset, step.n
                    if step.what == "rstd":
                        pool.wait_ge(xn_step, (b + 1) * LN_STEPS)
                        inverse_deviation(rstd[:], mv[:].rearrange("p t s -> p (t s)")[:, 1:2 * NT:2], x_vareps, b, x_rstd)
                    elif step.what == "zrstd":
                        pool.wait_ge(z_step, b * Z_STEPS + LN_STEPS)
                        inverse_deviation(rstd2[:], mv2[:].rearrange("p t s -> p (t s)")[:, 1:2 * NT:2], z_vareps, b, z_rstd,
                                          vareps2)
                    elif step.what == "rnormal":
                        pool.wait_ge(x1_out, 16 * (b + 1))
                        pool.wait_ge(r_rstd, b + 1)
                        normalised(z, f_mv, f_rstd, z, r_centred, r_normalised, b)
                    elif step.what == "rrstd":
                        pool.wait_ge(r_step, (b + 1) * LN_STEPS)
                        inverse_deviation(f_rstd[:], f_mv[:].rearrange("p t s -> p (t s)")[:, 1:2 * NT:2], r_vareps, b, r_rstd,
                                          vareps3)
                    elif step.what == "mask":
                        pool.wait_ge(exp_done, b * P2_N * NG + P2_N * step.group + (4, 8, 10, 11)[n])
                        apart(pool)
                        nc.gpsimd.affine_select(
                            out=prob[n][:, :, 0:P], in_=prob[n][:, :, 0:P], compare_op=ALU.is_ge, fill=0.0,
                            base=0, pattern=[[0, HG], [1, P]], channel_multiplier=-1).then_inc(masked, 1)
                    elif step.what == "sin":
                        if n == 0:
                            pool.wait_ge(qk_biased, b + 1)
                            wait(pool, rotated, b)
                        nc.gpsimd.tensor_tensor(
                            free_ap(rb[:, n, :], [[HS, 2 * NH], [2, HS // 2], [1, 2]]),
                            free_ap(qk[:, n, :], [[HS, 2 * NH], [2, HS // 2], [-1, 2]], 1),
                            free_ap(sin_sb[:, n, :], [[0, 2 * NH], [2, HS // 2], [1, 2]]),
                            ALU.mult).then_inc(rope_sin, 1)
                    elif step.what == "R":
                        pool.wait_ge(rope_cos, b + 1)
                        pool.wait_ge(rope_sin, NT * (b + 1))
                        wait(pool, qk_transposed, b)
                        heads_first = [[P, 2 * NT], [HS, NH], [1, HS]]
                        nc.gpsimd.tensor_tensor(free_ap(rot[:, 0, 0, :], [[P, 2 * NT], [1, NH], [NH, HS]]),
                                                free_ap(ra[:, 0, :], heads_first), free_ap(rb[:, 0, :], heads_first),
                                                ALU.add).then_inc(rotated, 1)
                    elif step.what == "residual":
                        pool.wait_ge(z_ready, b + 1)
                        pool.wait_ge(xr_in, 16 * (b + 1))
                        nc.gpsimd.tensor_tensor(z[:], z[:], xr[:], ALU.add).then_inc(x1_ready, 1)
                    elif step.what == "third":
                        pool.wait_ge(part2_ready, b + 1)
                        nc.gpsimd.tensor_tensor(parts[:, n, 2, :], rest[:, n, :], parts[:, n, 1, :],
                                                ALU.subtract).then_inc(part3_ready, 1)

            pool.wait_ge(ident_ready, 7)
            pool.wait_ge(weights_in, N_W)
            iterations(pool, body)

            pool.wait_ge(z_rstd, B)

            pool.wait_ge(zeroed, 16 * 9)
            pool.wait_ge(p_done, 5)

            def places_of(b, e, done):
                if not (isinstance(b, int) and b < 2):
                    pool.wait_ge((d_out, c_gathered)[done][e], until(b, e, 16 * NT * TOPK))
                elif done:
                    both(pool, d_out, B, 16 * NT * TOPK)
                apart(pool)
                nc.gpsimd.tensor_copy(places[e][:], place[:].rearrange("p (b n) -> p b n", b=B)[:, b, :]).then_inc(places_ready, 1)

            def dispatch(b, e):
                places_of(b, e, 0)
                pool.wait_ge(places_ready, b + 1)
                pool.wait_ge(d_in[e], through(b, e, 16))
                apart(pool)
                for n in range(NT * TOPK):
                    nc.gpsimd.indirect_dma_start(
                        out=sorted_d[:, :], out_offset=bass.IndirectOffsetOnAxis(ap=places[e][:, n:n + 1], axis=0),
                        in_=d_xn[e][:, n // TOPK, :], in_offset=None).then_inc(d_out[e], 16)

            batches(pool, dispatch)

            both(pool, e_stored, GROUPS, 16)

            def gather(b, e):
                places_of(b, e, 1)
                pool.wait_ge(places_ready, B + b + 1)
                apart(pool)
                if not (isinstance(b, int) and b < 2):
                    pool.wait_ge(c_step, (b - 2) * C_STEPS + NT * TOPK)
                    apart(pool)
                for n in range(NT * TOPK):
                    nc.gpsimd.indirect_dma_start(
                        out=c_y[e][:, n, :], out_offset=None, in_=expert_d[:, :],
                        in_offset=bass.IndirectOffsetOnAxis(ap=places[e][:, n:n + 1], axis=0)).then_inc(c_gathered[e], 16)

            def deviation(b, e):
                pool.wait_ge(c_vareps, b + 1)
                nc.gpsimd.tensor_tensor(f_rstd[:], vareps[:], mhalf[:], ALU.pow).then_inc(c_rstd, 1)

            gather(0, 0)
            gather(1, 1)
            deviation(0, 0)
            gather(2, 0)
            deviation(1, 1)
            with pool.Fori(1, B // 2 - 1) as pair:
                gather(2 * pair + 1, 1)
                deviation(2 * pair, 0)
                gather(2 * pair + 2, 0)
                deviation(2 * pair + 1, 1)
            gather(B - 1, 1)
            deviation(B - 2, 0)
            deviation(B - 1, 1)

        @block.scalar
        def _(act):
            act.wait_ge(x_in, 16)
            for w, s in ((w13_sb[:, :, 0:INTER], w1.rearrange("e d h -> d e h")),
                         (w13_sb[:, :, INTER:], w3.rearrange("e d h -> d e h")),
                         (w2_sb[:, :, 0, :], w2[:, 0:HALF, :].rearrange("e h d -> h e d")),
                         (w2_sb[:, :, 1, :], w2[:, HALF:, :].rearrange("e h d -> h e d")),
                         (sw1_sb[:], sw1), (sw3_sb[:], sw3),
                         (sw2_sb[:], sw2.rearrange("(c h) d -> h c d", c=NCH)),
                         (gw_sb[:], gate_w), (gb_bc[:], row(gate_b).to_broadcast([P, E])),
                         (sb2_bc[:], row(sb2).to_broadcast([P, P]))):
                act.dma_start(w, s).then_inc(f_fw, 16)
            for c in range(NCH):
                for col, v in ((sb1_col, sb1), (sb3_col, sb3)):
                    act.dma_start(col[:, c:c + 1], v[c * HALF:(c + 1) * HALF].rearrange("(h o) -> h o", o=1)).then_inc(f_fw, 16)
            act.wait_ge(zero_ready, 1)

            def clear(n):
                act.dma_start(sorted_z[n], free_ap(zeros[:], [[0, NZ], [1, P]])).then_inc(zeroed, 16)

            def body(i, parity=None):
                for step in STEPS:
                    if not exists(i, step.offset):
                        continue
                    b, g, n = i + step.offset, step.group, step.n
                    unit = wide[step.unit % 2] if step.unit is not None else None
                    if step.what == "s":
                        kb, hs_ = P2_UNITS[n]
                        u = g * P2_N + n
                        N = T - kb * P
                        act.wait_ge(p2_scores, b * P2_N * NG + u + 1)
                        wait(act, pv_done, (b * NG + g - 1) * NT + kb + 1)
                        nc.scalar.activation(free_ap(prob[kb][:, hs_[0], :], [[1, N * len(hs_)]]),
                                             score[u % 2][:, 0:N * len(hs_)],
                                             ACT.Exp, scale=SCALE).then_inc(exp_done, 1)
                    elif step.what == "v" and n == NT - 1:
                        act.wait_ge(pv_done, (b * NG + g + 1) * NT)
                        wait(act, heads_transposed, b * NG + g)
                        nc.scalar.activation(oT[:], heads_ps[:], ACT.Copy).then_inc(heads_copied, 1)
                        if isinstance(b, int) and b < 2:
                            clear(b * NG + g)
                            if b * NG + g == 6:
                                clear(7)
                                clear(8)
                    elif step.what == "Y":
                        act.wait_ge(y_transposed, b + 1)
                        wait(act, r_kept, 16 * b)
                        nc.scalar.activation(yT[:], unit[:, 0, :], ACT.Copy).then_inc(yT_ready, 1)
                    elif step.what == "rX":
                        act.wait_ge(r_transposed, b + 1)
                        nc.scalar.activation(yT[:], unit[:, 0, :], ACT.Copy).then_inc(r_xT_ready, 1)
                    elif step.what == "rexp":
                        act.wait_ge(r_shifted, b + 1)
                        nc.scalar.activation(ex[:], lg[:], ACT.Exp).then_inc(r_exp, 1)
                    elif step.what == "X":
                        act.wait_ge(x_transposed, b + 1)
                        wait(act, v_made, b)
                        wait(act, qk_made, b)
                        nc.scalar.activation(xnT[:], unit[:, 0, :], ACT.Copy).then_inc(xnT_ready, 1)
                    elif step.what == "T":
                        act.wait_ge(qk_transposed, b + 1)
                        wait(act, shuffled, b * N_SHUFFLE)
                        nc.scalar.activation(parts[:, :, 0, :], unit[:], ACT.Copy).then_inc(part1_ready, 1)
                    elif step.what == "second":
                        act.wait_ge(rest_ready, b + 1)
                        nc.scalar.activation(parts[:, :, 1, :], rest[:], ACT.Copy).then_inc(part2_ready, 1)

            iterations(act, body)
            act.wait_ge(x1_ready, B)
            act.dma_start(bias_f[:, 0:INTER], b1).then_inc(bias_in, 16)
            act.dma_start(bias_f[:, INTER:2 * INTER], b3).then_inc(bias_in, 16)
            act.dma_start(bias_f[:, 2 * INTER:], b2).then_inc(bias_in, 16)
            def shared_away(b, e):
                act.wait_ge(s_ready, b + 1)
                apart(act)
                act.dma_start(shared_v[b], s_z[e]).then_inc(s_stored[e], 16)

            act.wait_ge(f_fw, N_FW)
            act.wait_ge(sb1_halved, 1)

            def shared(b, e, first):
                for c in range(NCH):
                    n = b * NCH + c
                    act.wait_ge(s_up, n + 1)
                    if not (isinstance(n, int) and n < 2):
                        act.wait_ge(s_silu, n - 1)
                    h = wide[c % 2][0:HALF, 0, :]
                    nc.scalar.activation(s_th[c % 2], h, ACT.Tanh, bias=sb1_half[:, c:c + 1], scale=0.5).then_inc(s_tanh, 1)
                    nc.scalar.activation(s_h[c % 2], h, ACT.Identity, bias=sb1_half[:, c:c + 1], scale=0.5).then_inc(s_halved, 1)
                if not first:
                    shared_away(b - 1, 1 - e)

            shared_early(act, shared)
            shared_away(EARLY - 1, 1)
            act.wait_ge(bias_split, 1)
            for r in range(NPART):
                act.dma_start(bias_rows[r:r + 1, :, :], bias_parts[:, r, :]).then_inc(bias_in, 16)

            def x_back(n, k):
                act.wait_ge(e_transposed, n + 1)
                if not (isinstance(n, int) and n < 2):
                    act.wait_ge(e_up, n - 1)
                nc.scalar.activation(e_xT[k % 2][:], (heads_ps, misc)[k % 2][:, 0:P], ACT.Copy).then_inc(e_xT_ready, 1)

            def a_back(n, k):
                act.wait_ge(e_across, n + 1)
                if not (isinstance(n, int) and n < 2):
                    act.wait_ge(e_down, n - 1)
                nc.scalar.activation(e_aT[k % 2][:], score[k % 2][0:HALF, 0:2 * P].rearrange("p (a b) -> p a b", a=2),
                                     ACT.Copy).then_inc(e_aT_ready, 1)

            def experts(g, e, last):
                for k in range(BG):
                    n = g * BG + k
                    if not (last and k == BG - 1):
                        x_back(n + 1, k + 1)
                    act.wait_ge(e_up, n + 1)
                    if not (isinstance(n, int) and n < 2):
                        act.wait_ge(e_silu, n - 1)
                    nc.scalar.activation(e_th[k % 2][:], wide[k % 2][:, 0, 0:INTER], ACT.Tanh, scale=0.5).then_inc(e_tanh, 1)
                    if not (isinstance(n, int) and n < 1):
                        a_back(n - 1, k + 1)

            x_back(0, 0)
            groups(act, experts)
            a_back(NBLK - 1, 1)

            shared_late(act, shared)
            shared_away(B - 1, 1)

        @block.vector
        def _(dve):
            nc.vector.memset(zeros[:], 0.0).then_inc(zero_ready, 1)
            for n in range(2):
                nc.vector.memset(vext[n][:], 0.0).then_inc(filled, 1)
            dve.wait_ge(filled, 2)
            for n in range(2):
                nc.vector.memset(vext[n][:, :, :, HS:HS + 1], 1.0).then_inc(filled, 1)
            dve.wait_ge(filled, 4)
            dve.wait_ge(weights_in, N_W)
            ln1 = Steps(xn_step, LN_STEPS)
            ms = [Steps(m_step[n], 3) for n in range(2)]
            zs = Steps(z_step, Z_STEPS)

            def normalised_heads(i, g):
                dve.wait_ge(heads_transposed, i * NG + g + 1)
                hv = misc[:].rearrange("p (t h d) -> p t h d", t=NT, h=HG)
                if g == 0:
                    wait(dve, y_transposed, i)
                nc.vector.reciprocal(rinv[:].rearrange("p t (h o) -> p t h o", o=1), hv[:, :, :, HS:HS + 1]).then_inc(rinv_ready, 1)
                dve.wait_ge(rinv_ready, i * NG + g + 1)
                nc.vector.tensor_tensor(free_ap(y[:, 0, :], [[P, NT], [HS, HG], [1, HS]], g * HG * HS),
                                        hv[:, :, :, 0:HS],
                                        free_ap(rinv[:, 0, :], [[HG, NT], [1, HG], [0, HS]]),
                                        ALU.mult).then_inc(y_ready, 1)

            def statistics(steps, src, st_, mv_):
                for t in range(NT):
                    steps.did(nc.vector.bn_stats(st_[:, t, :], src[:, t, :]))
                dve.wait_ge(steps.sem, steps.value())
                apart(dve)
                for t in range(NT):
                    steps.did(nc.vector.bn_aggr(mv_[:, t, :], st_[:, t, :]))

            def normalised(src, mv_, rstd_, dst, rstd_ready, last):
                dve.wait_ge(*rstd_ready)
                for t in range(NT):
                    ins = nc.vector.tensor_scalar(dst[:, t, :], src[:, t, :], mv_[:, t, 0:1], rstd_[:, t:t + 1],
                                                  ALU.subtract, ALU.mult)
                    last(t, ins)

            rs = Steps(r_step, LN_STEPS)
            gs = Steps(g_step, 5 + 2 * NT)

            def link(ins):
                gs.did(ins)
                dve.wait_ge(g_step, gs.value())

            def over_tiles(ap, step, inner):
                return free_ap(ap, [[step, NT]] + inner)

            def shifted_logits(b, unit):
                dve.wait_ge(r_logits, b + 1)
                gs.round(b)
                nc.vector.tensor_tensor(lg[:], unit[:, 0, 0:NT * E].rearrange("p (t e) -> p t e", t=NT),
                                             over_tiles(gb_bc[:], 0, [[1, E]]), ALU.add).then_inc(r_biased, 1)
                dve.wait_ge(r_biased, b + 1)
                link(nc.vector.tensor_reduce(lmax[:], lg[:], axis=AX.X, op=ALU.max))
                nc.vector.tensor_tensor(lg[:], lg[:], over_tiles(lmax[:], 1, [[0, E]]), ALU.subtract).then_inc(r_shifted, 1)

            def choose(b):
                dve.wait_ge(r_exp, b + 1)
                link(nc.vector.tensor_reduce(esum[:], ex[:], axis=AX.X, op=ALU.add))
                link(nc.vector.reciprocal(esum[:], esum[:]))
                link(nc.vector.tensor_tensor(scores[:], ex[:], over_tiles(esum[:], 1, [[0, E]]), ALU.mult))
                apart(dve)
                for t in range(NT):
                    gs.did(nc.vector.max(top[:, t, :], scores[:, t, :]))
                dve.wait_ge(g_step, gs.value())
                apart(dve)
                for t in range(NT):
                    gs.did(nc.vector.max_index(topi[:, t, :], top[:, t, :], scores[:, t, :]))
                dve.wait_ge(g_step, gs.value())
                link(nc.vector.tensor_copy(topf[:], topi[:]))
                nc.vector.tensor_tensor(
                    chosen[:].rearrange("p (b t) e -> p b t e", b=B)[:, b, :, :].rearrange("p (t k) e -> p t k e", k=TOPK),
                    free_ap(iota_e[:], [[0, NT], [0, TOPK], [1, E]]),
                    free_ap(topf[:, 0, :], [[8, NT], [1, TOPK], [0, E]]), ALU.is_equal)
                nc.vector.tensor_copy(chosen_w[:].rearrange("p (b t k) -> p b t k", b=B, k=TOPK)[:, b, :, :],
                                      top[:, :, 0:TOPK]).then_inc(r_chosen, 1)
                gs.closed()

            def body(i, parity=None):
                for step in STEPS:
                    if not exists(i, step.offset):
                        continue
                    b, g, n = i + step.offset, step.group, step.n
                    e = par(i, parity) if step.offset % 2 == 0 else 1 - par(i, parity)
                    unit = wide[step.unit % 2] if step.unit is not None else None
                    if step.what == "rstats":
                        rs.round(b)
                        dve.wait_ge(x1_ready, b + 1)
                        statistics(rs, z, f_st, f_mv)
                        rs.closed()
                    elif step.what == "choose":
                        if isinstance(b, int) and b == 0:
                            dve.wait_ge(f_fw, N_FW)
                            dve.wait_ge(ident_ready, 7)
                            nc.vector.tensor_scalar(sb1_half[:], sb1_col[:], 0.5, None, ALU.mult).then_inc(sb1_halved, 1)
                        shifted_logits(b, wide[GATE_UNIT])
                    elif step.what == "chosen":
                        choose(b)
                    elif step.what == "stats":
                        ln1.round(b)
                        dve.wait_ge(x_in, 16 * (b + 1))
                        statistics(ln1, xt, st, mv)
                        ln1.closed()
                    elif step.what == "normal":
                        wait(dve, x_transposed, b)
                        normalised(xt, mv, rstd, xn, (x_rstd, b + 1),
                                   lambda t, ins: ins.then_inc(xn_ready, 1) if t == NT - 1 else None)
                    elif step.what == "V":
                        dve.wait_ge(v_made, b + 1)
                        wait(dve, pv_done, (b - 1) * NG * NT)
                        nc.vector.tensor_tensor(
                            free_ap(vext[e][:, 0, 0, :], [[NH * 32, NT], [32, NH], [1, HS]]),
                            free_ap(unit[:, 0, :], [[P, NT], [HS, NH], [1, HS]]),
                            free_ap(bqkv_bc[:], [[0, NT], [HS, NH], [1, HS]], 2 * P), ALU.add).then_inc(v_ready, 1)
                    elif step.what == "Q":
                        dve.wait_ge(qk_made, b + 1)
                        wait(dve, rope_sin, NT * b)
                        nc.vector.tensor_tensor(qk[:], unit[:].rearrange("p a (t c) -> p (a t) c", c=2 * P),
                                                free_ap(bqkv_bc[:], [[0, NT], [1, 2 * P]]), ALU.add).then_inc(qk_biased, 1)
                    elif step.what == "cos":
                        dve.wait_ge(qk_biased, b + 1)
                        wait(dve, rotated, b)
                        nc.vector.tensor_tensor(free_ap(ra[:, 0, :], [[2 * P, NT], [HS, 2 * NH], [1, HS]]),
                                                free_ap(qk[:, 0, :], [[2 * P, NT], [HS, 2 * NH], [1, HS]]),
                                                free_ap(cos_sb[:, 0, :], [[HS, NT], [0, 2 * NH], [1, HS]]),
                                                ALU.mult).then_inc(rope_cos, 1)
                    elif step.what == "T":
                        dve.wait_ge(part1_ready, b + 1)
                        wait(dve, part3_ready, 2 * b)
                        nc.vector.tensor_tensor(rest[:], unit[:], parts[:, :, 0, :], ALU.subtract).then_inc(rest_ready, 1)
                    elif step.what == "p":
                        j, hs_ = P1_UNITS[n % len(P1_UNITS)]
                        dve.wait_ge(p1_scores, b * P1_N + n + 1)
                        if n % (P1_N // 2) == 0:
                            wait(dve, max_transposed[n // (P1_N // 2)], b)
                        L = (j + 1) * P
                        src = unit[:, :, 0:L] if j >= 2 else free_ap(unit[:, 0, :], [[L, HG], [1, L]])
                        h0 = n // len(P1_UNITS) * HG + hs_[0]
                        nc.vector.tensor_reduce(mx[:, h0:h0 + len(hs_), j:j + 1], src, axis=AX.X,
                                                op=ALU.max).then_inc(p1_max, 1)
                    elif step.what == "M":
                        ms[n].round(b)
                        dve.wait_ge(max_transposed[n], b + 1)
                        wait(dve, m_in[n], 16 * NPART * b)
                        mt, mp = misc[0:NH // 2 * NT, 0:P], mparts[n]
                        ms[n].did(nc.vector.tensor_scalar(mp[:, 0, :], mt, -1.0, None, ALU.mult))
                        dve.wait_ge(m_step[n], ms[n].value())
                        ms[n].did(nc.vector.scalar_tensor_tensor(out=mrest[:], in0=mt, scalar=-1.0, in1=mp[:, 0, :],
                                                                 op0=ALU.mult, op1=ALU.subtract))
                        dve.wait_ge(m_step[n], ms[n].value())
                        ms[n].did(nc.vector.tensor_copy(mp[:, 1, :], mrest[:]))
                        dve.wait_ge(m_step[n], ms[n].value())
                        nc.vector.tensor_tensor(mp[:, 2, :], mrest[:], mp[:, 1, :], ALU.subtract).then_inc(m_ready[n], 1)
                        ms[n].closed()
                    elif step.what == "heads":
                        normalised_heads(b, g)
                    elif step.what == "W":
                        zs.round(b)
                        dve.wait_ge(projected, b + 1)
                        wait(dve, r_stored, 16 * b)
                        nc.vector.tensor_tensor(z[:], unit[:, 0, :].rearrange("p (t c) -> p t c", t=NT),
                                                free_ap(bp_bc[:], [[0, NT], [1, P]]), ALU.add).then_inc(z_biased, 1)
                    elif step.what == "zstats":
                        dve.wait_ge(z_biased, b + 1)
                        statistics(zs, z, st2, mv2)
                    elif step.what == "Z":
                        normalised(z, mv2, rstd2, z, (z_rstd, b + 1),
                                   lambda t, ins: zs.did(ins) if t < NT - 1 else ins.then_inc(z_ready, 1))
                        zs.closed()

            iterations(dve, body)

            dve.wait_ge(p_counts, 1)
            ps = Steps(p_step, 7)

            def pstep(ins):
                ps.did(ins)
                dve.wait_ge(p_step, ps.value())

            pstep(nc.vector.tensor_copy(counts[:], misc[:, 0:E]))
            nc.vector.tensor_tensor(earlier, free_ap(before[:], [[1, TS], [0, E]]), free_ap(counts[:], [[0, TS], [1, E]]),
                                    ALU.mult).then_inc(p_earlier, 1)
            dve.wait_ge(p_total, 1)
            pstep(nc.vector.tensor_scalar(n_f[:], heads_ps[0:E, 0:1], float(P - 1), None, ALU.add))
            pstep(nc.vector.tensor_copy(n_i[:], n_f[:]))
            pstep(nc.vector.tensor_single_scalar(nblk_i[:], n_i[:], 7, ALU.arith_shift_right))
            pstep(nc.vector.tensor_copy(nblk_f[:], nblk_i[:]))
            nc.vector.tensor_copy(nblk_b[:], nblk_f[:])
            nc.vector.tensor_scalar(first_of[:], before[0:E, 0:E], nblk_f[:, 0:1], None, ALU.mult).then_inc(p_blocks, 1)
            dve.wait_ge(p_ends, 1)
            pstep(nc.vector.tensor_copy(last_blk[:], score[0][0:E, 0:1]))
            nc.vector.tensor_scalar(first_place[:], score[1][:, 0:E], float(P), None, ALU.mult)
            nc.vector.tensor_scalar(past[:], iota_blk[0:E, :], last_blk[:, 0:1], None, ALU.is_ge).then_inc(p_past, 1)
            dve.wait_ge(p_experts, 1)
            pstep(nc.vector.tensor_scalar(blk_f[:], misc[:, 0:NBLK], float(E - 1), None, ALU.min))
            nc.vector.tensor_copy(blk_expert[:], blk_f[:]).then_inc(p_done, 1)
            dve.wait_ge(p_ranks, 1)
            half = TS // 2
            dve.wait_ge(p_past, 1)
            for n in range(2):
                last = nc.vector.tensor_tensor(place_e[:, n * half:(n + 1) * half, :],
                                               wide[n][:].rearrange("p a (t e) -> p (a t) e", e=E),
                                               free_ap(first_place[:], [[0, half], [1, E]]), ALU.add)
            last.then_inc(p_done, 1)
            dve.wait_ge(p_done, 2)
            nc.vector.tensor_tensor(place_e, place_e, chosen[:], ALU.mult).then_inc(p_done, 1)
            dve.wait_ge(p_done, 3)
            nc.vector.tensor_reduce(place_f[:], place_e, axis=AX.X, op=ALU.add).then_inc(p_done, 1)
            dve.wait_ge(p_done, 4)
            nc.vector.tensor_copy(place[:], place_f[:]).then_inc(p_done, 1)
            dve.wait_ge(p_done, 5)
            ps.closed()

            def shared_chunk(b, e, c, first):
                n = b * NCH + c
                dve.wait_ge(s_halved, n + 1)
                dve.wait_ge(s_tanh, n + 1)
                if not (isinstance(n, int) and n < 2):
                    dve.wait_ge(s_gated, n - 1)
                nc.vector.scalar_tensor_tensor(out=s_s[c % 2], in0=s_th[c % 2], scalar=1.0, in1=s_h[c % 2],
                                               op0=ALU.add, op1=ALU.mult).then_inc(s_silu, 1)
                dve.wait_ge(s_silu, n + 1)
                if c == 0 and not (isinstance(b, int) and b < 2):
                    dve.wait_ge(s_down, b - 1)
                nc.vector.scalar_tensor_tensor(out=s_aT[e][c], in0=wide[c % 2][0:HALF, 1, :], scalar=sb3_col[:, c:c + 1],
                                               in1=s_s[c % 2], op0=ALU.add, op1=ALU.mult).then_inc(s_gated, 1)
                if c == 2 and not first:
                    shared_out(b - 1, 1 - e)

            def shared(b, e, first):
                for c in range(NCH):
                    shared_chunk(b, e, c, first)

            def shared_out(b, e):
                dve.wait_ge(s_down, b + 1)
                if not (isinstance(b, int) and b < 2):
                    dve.wait_ge(s_stored[e], until(b, e, 16))
                nc.vector.tensor_tensor(s_z[e], (heads_ps, misc)[e][:].rearrange("p (t c) -> p t c", t=NT),
                                        free_ap(sb2_bc[:], [[0, NT], [1, P]]), ALU.add).then_inc(s_ready, 1)

            shared_early(dve, shared)
            shared_out(EARLY - 1, 1)

            dve.wait_ge(bias_in, 48)
            bs = Steps(bias_step, 3)
            bs.did(nc.vector.tensor_copy(bias_parts[:, 0, :], bias_f))
            dve.wait_ge(bias_step, 1)
            bs.did(nc.vector.tensor_tensor(bias_rest, bias_f, bias_parts[:, 0, :], ALU.subtract))
            dve.wait_ge(bias_step, 2)
            bs.did(nc.vector.tensor_copy(bias_parts[:, 1, :], bias_rest))
            dve.wait_ge(bias_step, 3)
            nc.vector.tensor_tensor(bias_parts[:, 2, :], bias_rest, bias_parts[:, 1, :], ALU.subtract).then_inc(bias_split, 1)

            def expert_out(n, k, g, e):
                dve.wait_ge(e_down, n + 1)
                if k == 0 and not (isinstance(g, int) and g < 2):
                    dve.wait_ge(e_stored[e], until(g, e, 16))
                nc.vector.tensor_copy(e_y[e][:, k, :], wide[k % 2][:, 1, 0:P]).then_inc(e_ready, 1)

            def experts(g, e, last):
                for k in range(BG):
                    n = g * BG + k
                    dve.wait_ge(e_tanh, n + 1)
                    nc.vector.scalar_tensor_tensor(out=e_s[k % 2][:], in0=e_th[k % 2][:], scalar=1.0, in1=wide[k % 2][:, 0, 0:INTER],
                                                   op0=ALU.add, op1=ALU.mult).then_inc(e_silu, 1)
                    dve.wait_ge(e_silu, n + 1)
                    if not (isinstance(n, int) and n < 2):
                        dve.wait_ge(e_across, n - 1)
                    nc.vector.scalar_tensor_tensor(out=e_a[k % 2][:], in0=e_s[k % 2][:], scalar=0.5,
                                                   in1=wide[k % 2][:, 0, INTER:2 * INTER],
                                                   op0=ALU.mult, op1=ALU.mult).then_inc(e_gated, 1)
                    if k >= 2:
                        expert_out(n - 2, k - 2, g, e)
                    elif not (isinstance(g, int) and g < 1):
                        expert_out(n - 2, k + BG - 2, g - 1, 1 - e)

            groups(dve, experts)
            expert_out(NBLK - 2, BG - 2, GROUPS - 1, 1)
            expert_out(NBLK - 1, BG - 1, GROUPS - 1, 1)

            cs = Steps(c_step, C_STEPS)

            def combine(b, e, half_batch):
                cs.round(b)
                if not (isinstance(b, int) and b < 2):
                    dve.wait_ge(c_step, (b - 2) * C_STEPS + NT * TOPK)
                nc.vector.tensor_copy(c_w[e][:], chosen_w[:].rearrange("p (b n) -> p b n", b=B)[:, b, :]).then_inc(c_weights, 1)
                dve.wait_ge(c_gathered[e], through(b, e, 16 * NT * TOPK))
                dve.wait_ge(c_in[e], through(b, e, 32))
                dve.wait_ge(c_weights, b + 1)
                for k in range(TOPK):
                    for t in range(NT):
                        n = t * TOPK + k
                        cs.did(nc.vector.scalar_tensor_tensor(out=c_z[e][:, t, :], in0=c_y[e][:, n, :], scalar=c_w[e][:, n:n + 1],
                                                              in1=c_z[e][:, t, :], op0=ALU.mult, op1=ALU.add))
                    dve.wait_ge(c_step, cs.value())
                statistics(cs, c_z[e], f_st, f_mv)
                dve.wait_ge(c_step, cs.value())
                nc.vector.tensor_scalar(vareps[:], f_mv[:].rearrange("p t s -> p (t s)")[:, 1:2 * NT:2], EPS, None,
                                        ALU.add).then_inc(c_vareps, 1)
                half_batch(0)
                normalised(c_z[e], f_mv, f_rstd, c_z[e], (c_rstd, b + 1), lambda t, ins: cs.did(ins))
                dve.wait_ge(c_step, cs.value())
                cs.closed()
                nc.vector.tensor_tensor(c_z[e], c_z[e], c_x[e], ALU.add).then_inc(c_ready, 1)
                half_batch(1)

            def combined(q, b, e, first):
                combine(q, 0, lambda k: shared_chunk(b, e, k, first))
                combine(q + 1, 1, lambda k: shared_chunk(b, e, 2 + k, first))

            combined(0, EARLY, 0, True)
            combined(2, EARLY + 1, 1, False)
            with dve.Fori(1, (B - EARLY) // 2) as two:
                combined(4 * two, EARLY + 2 * two, 0, False)
                combined(4 * two + 2, EARLY + 2 * two + 1, 1, False)
            shared_out(B - 1, 1)
            for b in range(2 * (B - EARLY), B):
                combine(b, b % 2, lambda k: None)

        @block.tensor
        def _(pe):
            pe.wait_ge(weights_in, N_W)
            pe.wait_ge(ident_ready, 7)
            pe.wait_ge(filled, 4)

            def body(i, parity=None):
                for step in STEPS:
                    if not exists(i, step.offset):
                        continue
                    b, g, n = i + step.offset, step.group, step.n
                    e = par(i, parity) if step.offset % 2 == 0 else 1 - par(i, parity)
                    if step.unit is not None:
                        unit = wide[step.unit % 2]
                        unit_free(pe, i, step)
                    if step.what == "s":
                        kb, hs_ = P2_UNITS[n]
                        u = g * P2_N + n
                        N = T - kb * P
                        if n == 0 and g % (NG // 2) == 0:
                            pe.wait_ge(m_in[g // (NG // 2)], 16 * NPART * (b + 1))
                        wait(pe, exp_done, b * P2_N * NG + u - 1)
                        for k, h4 in enumerate(hs_):
                            h = g * HG + h4
                            last = nc.tensor.matmul(score[u % 2][:, k * N:(k + 1) * N],
                                                    k4[e][0:SROWS, h, kb * P:(kb + 1) * P], q4[e][0:SROWS, h, kb * P:T],
                                                    start=True, stop=True)
                        last.then_inc(p2_scores, 1)
                    elif step.what == "v":
                        pe.wait_ge(masked, (b * NG + g) * NT + n + 1)
                        if n == 0:
                            wait(pe, heads_copied, b * NG + g)
                            pe.wait_ge(v_ready, b + 1)
                        for h4 in range(HG):
                            last = nc.tensor.matmul(heads_ps[32 * h4:32 * h4 + 32, n * P:T],
                                                    vext[e][:, n, g * HG + h4, :], prob[n][:, h4, :],
                                                    start=(n == 0), stop=(n == NT - 1))
                        last.then_inc(pv_done, 1)
                    elif step.what == "heads":
                        pe.wait_ge(heads_copied, b * NG + g + 1)
                        misc_free(pe, i, step)
                        for t in range(NT):
                            last = nc.tensor.transpose(misc[:, t * P:(t + 1) * P], oT[:, t * P:(t + 1) * P], ident[:])
                        last.then_inc(heads_transposed, 1)
                    elif step.what == "M":
                        misc_free(pe, i, step)
                        pe.wait_ge(p1_max, b * P1_N + (n + 1) * P1_N // 2)
                        apart(pe)
                        nc.tensor.transpose(misc[0:NH // 2 * NT, 0:P],
                                            mx[:, n * NH // 2:(n + 1) * NH // 2, :].rearrange("p h t -> p (h t)"),
                                            ident[:]).then_inc(max_transposed[n], 1)
                    elif step.what == "p":
                        if n == 0:
                            pe.wait_ge(shuffled, (b + 1) * N_SHUFFLE)
                        j, hs_ = P1_UNITS[n % len(P1_UNITS)]
                        L = (j + 1) * P
                        for k, h4 in enumerate(hs_):
                            h = n // len(P1_UNITS) * HG + h4
                            at = k * L
                            o = unit[:, k, 0:L] if j >= 2 else unit[:, at // 512, at % 512:at % 512 + L]
                            nc.tensor.matmul(o, q4[e][0:ROWS, h, j * P:(j + 1) * P], k4[e][0:ROWS, h, 0:L],
                                             start=True, stop=False)
                            last = nc.tensor.matmul(o[:, j * P:L], identb[:], maskneg[:], start=False, stop=True)
                        last.then_inc(p1_scores, 1)
                    elif step.what == "rX":
                        pe.wait_ge(r_normalised, b + 1)
                        for t in range(NT):
                            last = nc.tensor.transpose(unit[:, 0, t * P:(t + 1) * P], z[:, t, :], ident[:])
                        last.then_inc(r_transposed, 1)
                    elif step.what == "rL":
                        pe.wait_ge(r_xT_ready, b + 1)
                        if isinstance(b, int) and b == 0:
                            pe.wait_ge(f_fw, N_FW)
                        for t in range(NT):
                            last = nc.tensor.matmul(unit[:, 0, t * E:(t + 1) * E], yT[:, t * P:(t + 1) * P], gw_sb[:],
                                                    start=True, stop=True)
                        last.then_inc(r_logits, 1)
                    elif step.what == "X":
                        pe.wait_ge(xn_ready, b + 1)
                        for t in range(NT):
                            last = nc.tensor.transpose(unit[:, 0, t * P:(t + 1) * P], xn[:, t, :], ident[:])
                        last.then_inc(x_transposed, 1)
                    elif step.what == "V":
                        pe.wait_ge(xnT_ready, b + 1)
                        for t in range(NT):
                            last = nc.tensor.matmul(unit[:, 0, t * P:(t + 1) * P], xnT[:, t * P:(t + 1) * P],
                                                    wqkv[:, 2 * P:], start=True, stop=True)
                        last.then_inc(v_made, 1)
                    elif step.what == "Q":
                        pe.wait_ge(xnT_ready, b + 1)
                        for t in range(NT):
                            last = nc.tensor.matmul(unit[:, t // 2, t % 2 * 2 * P:(t % 2 + 1) * 2 * P],
                                                    xnT[:, t * P:(t + 1) * P], wqkv[:, 0:2 * P], start=True, stop=True)
                        last.then_inc(qk_made, 1)
                    elif step.what == "T":
                        pe.wait_ge(rotated, b + 1)
                        for s in range(2):
                            for t in range(NT):
                                last = nc.tensor.transpose(unit[:, s, t * P:(t + 1) * P], rot[:, t, s, :], ident[:])
                        last.then_inc(qk_transposed, 1)
                    elif step.what == "Y":
                        pe.wait_ge(y_ready, (b + 1) * NG)
                        for t in range(NT):
                            last = nc.tensor.transpose(unit[:, 0, t * P:(t + 1) * P], y[:, t, :], ident[:])
                        last.then_inc(y_transposed, 1)
                    elif step.what == "W":
                        pe.wait_ge(yT_ready, b + 1)
                        for t in range(NT):
                            last = nc.tensor.matmul(unit[:, 0, t * P:(t + 1) * P], yT[:, t * P:(t + 1) * P], wp[:],
                                                    start=True, stop=True)
                        last.then_inc(projected, 1)

            iterations(pe, body)

            pe.wait_ge(r_chosen, B)
            for k in range(E):
                last = nc.tensor.matmul(misc[:, k:k + 1], chosen[:, :, k], onesb[:, 0:1], start=True, stop=True)
            last.then_inc(p_counts, 1)
            pe.wait_ge(p_step, 1)
            nc.tensor.matmul(heads_ps[0:E, 0:1], counts[:], onesb[:, 0:1], start=True, stop=True).then_inc(p_total, 1)
            pe.wait_ge(p_earlier, 1)
            flat = lambda ap: ap.rearrange("p t e -> p (t e)")
            chosen_flat = flat(chosen[:])
            for n in range(4):
                o = wide[n // 2][:, n % 2, :]
                nc.tensor.matmul(o, before[:], chosen_flat[:, n * 512:(n + 1) * 512], start=True, stop=False)
                last = nc.tensor.matmul(o, onesb[:], flat(earlier)[:, n * 512:(n + 1) * 512], start=False, stop=True)
            last.then_inc(p_ranks, 1)
            pe.wait_ge(p_blocks, 1)
            nc.tensor.matmul(score[0][0:E, 0:1], upto[:], nblk_b[:], start=True, stop=True)
            nc.tensor.matmul(score[1][:, 0:E], onesb[0:E, :], first_of[:], start=True, stop=True).then_inc(p_ends, 1)
            pe.wait_ge(p_past, 1)
            nc.tensor.matmul(misc[:, 0:NBLK], onesb[0:E, :], past[:], start=True, stop=True).then_inc(p_experts, 1)

            pe.wait_ge(r_back, 16)
            pe.wait_ge(p_done, 2)

            def shared(b, e, first):
                for c in range(NCH):
                    n = b * NCH + c
                    if not (isinstance(n, int) and n < 2):
                        pe.wait_ge(s_gated, n - 1)
                    for k, w in enumerate((sw1_sb, sw3_sb)):
                        last = nc.tensor.matmul(wide[c % 2][0:HALF, k, :], w[:, c * HALF:(c + 1) * HALF], xT_all[:, b, :],
                                                start=True, stop=True)
                    last.then_inc(s_up, 1)
                    if c == 1 and not first:
                        shared_down(b - 1, 1 - e)

            def shared_down(b, e):
                pe.wait_ge(s_gated, NCH * (b + 1))
                if not (isinstance(b, int) and b < 2):
                    pe.wait_ge(s_ready, b - 1)
                for t in range(NT):
                    for c in range(NCH):
                        last = nc.tensor.matmul((heads_ps, misc)[e][:, t * P:(t + 1) * P], s_aT[e][c][:, t * P:(t + 1) * P],
                                                sw2_sb[:, c, :], start=(c == 0), stop=(c == NCH - 1))
                last.then_inc(s_down, 1)

            shared_early(pe, shared)
            shared_down(EARLY - 1, 1)

            pe.wait_ge(bias_in, 16 * 6)
            pe.wait_ge(s_ready, EARLY)

            def experts_of(g, groups_=1):
                _, values = nc.values_load_multi_w_load_instructions(
                    blk_expert[0:1, bass.ds(g * BG, groups_ * BG)], engines=(mybir.EngineType.PE,), min_val=0, max_val=E - 1,
                    skip_runtime_bounds_check_because="a minimum bounds them where they are made")
                return list(values)

            def x_across(n, k, g, e):
                if k == 0:
                    pe.wait_ge(e_in[e], through(g, e, 16))
                if not (isinstance(n, int) and n < 2):
                    pe.wait_ge(e_xT_ready, n - 1)
                nc.tensor.transpose((heads_ps, misc)[k % 2][:, 0:P], e_x[e][:, k, :], ident[:]).then_inc(e_transposed, 1)

            def a_across(n, k):
                pe.wait_ge(e_gated, n + 1)
                if not (isinstance(n, int) and n < 2):
                    pe.wait_ge(e_aT_ready, n - 1)
                for half in range(2):
                    last = nc.tensor.transpose(score[k % 2][0:HALF, half * P:(half + 1) * P],
                                               e_a[k % 2][:, half * HALF:(half + 1) * HALF], ident[:])
                last.then_inc(e_across, 1)

            def down(n, k, expert):
                pe.wait_ge(e_aT_ready, n + 1)
                if not (isinstance(n, int) and n < 2):
                    pe.wait_ge(e_ready, n - 1)
                o = wide[k % 2][:, 1, 0:P]
                for half in range(2):
                    nc.tensor.matmul(o, e_aT[k % 2][:, half, :], w2_sb[:, expert, half, :], start=(half == 0), stop=False)
                nc.tensor.matmul(o, onesb[0:NPART, :], bias_rows[:, expert, 2 * INTER:], start=False, stop=True).then_inc(e_down, 1)

            def experts(g, e, last, of, preload):
                for k in range(BG):
                    n = g * BG + k
                    if k < BG - 1:
                        x_across(n + 1, k + 1, g, e)
                    elif not last:
                        x_across(n + 1, 0, g + 1, 1 - e)
                    pe.wait_ge(e_xT_ready, n + 1)
                    if not (isinstance(n, int) and n < 2):
                        pe.wait_ge(e_gated, n - 1)
                    o = wide[k % 2][:, 0, 0:2 * INTER]
                    nc.tensor.matmul(o, e_xT[k % 2][:], w13_sb[:, of[BG + k], :], start=True, stop=False)
                    nc.tensor.matmul(o, onesb[0:NPART, :], bias_rows[:, of[BG + k], 0:2 * INTER], start=False, stop=True).then_inc(e_up, 1)
                    if k == BG - 2 and preload:
                        following = experts_of(g + 1)
                    if not (isinstance(n, int) and n < 1):
                        a_across(n - 1, k + 1)
                    if not (isinstance(n, int) and n < 2):
                        down(n - 2, k, of[BG + k - 2])
                return of[BG:] + following if preload else of[BG:]

            def round_of_groups(g, last):
                of = [None] * BG + experts_of(g) if isinstance(g, int) and g == 0 else experts_of(g - 1, 2)
                for k in range(ROUND):
                    of = experts(g + k, k % 2, last and k == ROUND - 1, of, k < ROUND - 1)
                return of

            x_across(0, 0, 0, 0)
            round_of_groups(0, False)
            with pe.Fori(1, GROUPS // ROUND - 1) as r:
                round_of_groups(r * ROUND, False)
            of = round_of_groups(GROUPS - ROUND, True)
            down(NBLK - 2, 0, of[-2])
            a_across(NBLK - 1, 1)
            down(NBLK - 1, 1, of[-1])

            pe.wait_ge(e_ready, NBLK)
            shared_late(pe, shared)
            shared_down(B - 1, 1)


NAMES = ["attn_x", "attn_Wq", "attn_bq", "attn_Wk", "attn_bk", "attn_Wv", "attn_bv", "attn_Wp", "attn_bp",
         "ffn_gate_w", "ffn_gate_b", "ffn_w1", "ffn_b1", "ffn_w3", "ffn_b3", "ffn_w2", "ffn_b2",
         "ffn_sw1", "ffn_sb1", "ffn_sw3", "ffn_sb3", "ffn_sw2", "ffn_sb2"]


def rope_tables(length, dim):
    inv = (np.float32(1.0) / np.float32(10000.0) ** (np.arange(dim // 2, dtype=np.float32) * np.float32(2.0) / np.float32(dim))).astype(np.float32)
    ang = np.arange(length, dtype=np.float32)[:, None] * inv[None, :]
    c = np.repeat(np.cos(ang), 2, axis=1)
    s = np.repeat(np.sin(ang), 2, axis=1) * np.tile(np.array([-1.0, 1.0], np.float32), dim // 2)
    lay = lambda a: np.ascontiguousarray(a.astype(np.float32).reshape(length // P, P, dim).transpose(1, 0, 2))
    return lay(c), lay(s)


def kernel(**inputs):
    import concourse.bacc as bacc
    from concourse.bass_utils import run_bass_kernel_spmd

    nc = bacc.Bacc("TRN2", target_bir_lowering=False, num_devices=1)
    arrays, args = {}, []
    for name in NAMES:
        arrays[name] = np.ascontiguousarray(inputs["L0_" + name])
    arrays["cos"], arrays["sin"] = rope_tables(arrays["attn_x"].shape[1], HS)
    for name, a in arrays.items():
        args.append(nc.dram_tensor(name, a.shape, mybir.dt.from_np(a.dtype), kind="ExternalInput").ap())
    out = nc.dram_tensor("out", arrays["attn_x"].shape, F32, kind="ExternalOutput").ap()
    program(nc, *args, out)
    r = run_bass_kernel_spmd(nc, [arrays], core_ids=[0])
    return r.results[0]["out"]
```
